# Optimizing a Trainium2 kernel written in Bass

```python
import numpy as np
import jax
import jax.numpy as jnp

def _softmax(x, axis=-1):
    return jax.nn.softmax(x, axis=axis)

def _gelu(x):
    return jax.nn.gelu(x, approximate=True)

def _silu(x):
    return jax.nn.silu(x)

def _sigmoid(x):
    return jax.nn.sigmoid(x)

def _layernorm(x, axis=-1, eps=1e-05):
    m = jnp.mean(x, axis=axis, keepdims=True)
    v = jnp.var(x, axis=axis, keepdims=True)
    return (x - m) / jnp.sqrt(v + eps)

def _scatter_add(tgt, idx, src, axis=0):
    return tgt.at[idx].add(src)

def _segment_sum(src, seg, n):
    return jax.ops.segment_sum(src, seg, n)
kernel_name = 'mk_xattn_ffn_d4_seqx_r8_a424bc'

def setup_inputs(seed: int=0):
    np.random.seed(seed)
    _w = jnp.asarray

    def _rec_inputs():
        import jax
        import jax.numpy as jnp
        _rk = jax.random.key(seed)
        x = -0.0002928 + 1 * jax.random.normal(jax.random.fold_in(_rk, 1), (2, 256, 128), jnp.float32)
        _lenS = 256 - jax.random.randint(jax.random.fold_in(_rk, 7), (2,), 0, max(1, 256 // 4) + 1, jnp.int32)
        _lenS2 = 512 - jax.random.randint(jax.random.fold_in(_rk, 8), (2,), 0, max(1, 512 // 4) + 1, jnp.int32)
        _ctx_768P = jax.random.normal(jax.random.fold_in(_rk, 11), (2, 16, 96), jnp.float32)
        _ctx_768c = jax.random.dirichlet(jax.random.fold_in(_rk, 511), 0.3 * jnp.ones((16,), jnp.float32), (2, 512))
        _ctx_768t = jnp.einsum('bsk,bkd->bsd', _ctx_768c, _ctx_768P)
        _ctx_768t = _ctx_768t * jax.lax.rsqrt(jnp.mean(jnp.square(_ctx_768t)) + 1e-12) * 0.953939
        ctx_768 = 2.09791e-05 + 1.00001 * (_ctx_768t + 0.3 * jax.random.normal(jax.random.fold_in(_rk, 611), (2, 512, 96), jnp.float32))
        return (x, ctx_768)
    x, ctx_768 = _rec_inputs()

    def _L0_xattn_setup():
        import jax, jax.numpy as jnp
        import numpy as np
        HEADS = 8
        DIM_HEAD = 128
        ATTN_MATRIX_SCALE = 1.5
        SCALE = DIM_HEAD ** (-0.5)

        def _split_heads(t):
            b, n, _ = t.shape
            t = t.reshape(b, n, HEADS, DIM_HEAD)
            return t.transpose(2, 0, 1, 3).reshape(HEADS, b * n, DIM_HEAD)
        key = jax.random.key(seed)
        ks = jax.random.split(key, 7)
        b, n, m = (2, 256, 256)
        qd, cd, inner = (128, 96, HEADS * DIM_HEAD)
        x = jax.random.normal(ks[0], (b, n, qd), dtype=jnp.float32)
        context = jax.random.normal(ks[1], (b, m, cd), dtype=jnp.float32)
        Wq = jax.random.normal(ks[2], (qd, inner), dtype=jnp.float32) * qd ** (-0.5)
        Wk = jax.random.normal(ks[3], (cd, inner), dtype=jnp.float32) * cd ** (-0.5)
        Wv = jax.random.normal(ks[4], (cd, inner), dtype=jnp.float32) * cd ** (-0.5)
        Wout = jax.random.normal(ks[5], (inner, qd), dtype=jnp.float32) * inner ** (-0.5)
        bout = jnp.zeros((qd,), dtype=jnp.float32)
        return {'x': x, 'context': context, 'Wq': Wq, 'Wk': Wk, 'Wv': Wv, 'Wout': Wout, 'bout': bout}
    _L0_xattn_all = _L0_xattn_setup()
    _L0_xattn_in = {k: v for k, v in _L0_xattn_all.items() if k in ('Wq', 'Wk', 'Wv', 'Wout', 'bout')}
    del _L0_xattn_all

    def _L0_ffn_setup():
        import jax, jax.numpy as jnp
        import numpy as np
        IN_DIM = 128
        OUT_DIM = 128
        NUM_EXPERTS = 8
        TOP_K = 2
        key = jax.random.key(seed)
        ks = jax.random.split(key, 5)
        s = 1.0 / np.sqrt(IN_DIM)
        x = jax.random.normal(ks[0], (4, 256, IN_DIM), dtype=jnp.float32)
        Wg = jax.random.uniform(ks[1], (IN_DIM, NUM_EXPERTS), jnp.float32, -s, s)
        bg = jnp.zeros((NUM_EXPERTS,), jnp.float32)
        We = jax.random.uniform(ks[2], (NUM_EXPERTS, OUT_DIM, IN_DIM), jnp.float32, -s, s)
        be = jax.random.uniform(ks[3], (NUM_EXPERTS, OUT_DIM), jnp.float32, -s, s)
        return {'x': x, 'Wg': Wg, 'bg': bg, 'We': We, 'be': be}
    _L0_ffn_all = _L0_ffn_setup()
    _L0_ffn_in = {k: v for k, v in _L0_ffn_all.items() if k in ('Wg', 'bg', 'We', 'be')}
    del _L0_ffn_all

    def _L1_xattn_setup():
        import jax, jax.numpy as jnp
        import numpy as np
        IMG_DIM, TXT_DIM, HID = (128, 96, 128)
        B, LQ, LK = (8, 256, 256)
        key = jax.random.key(seed)
        ks = jax.random.split(key, 8)
        s_img = 1.0 / np.sqrt(IMG_DIM)
        s_txt = 1.0 / np.sqrt(TXT_DIM)
        return {'image_features': jax.random.normal(ks[0], (B, LQ, IMG_DIM), jnp.float32), 'text_features': jax.random.normal(ks[1], (B, LK, TXT_DIM), jnp.float32), 'Wq': jax.random.uniform(ks[2], (IMG_DIM, HID), jnp.float32, -s_img, s_img), 'bq': jax.random.uniform(ks[3], (HID,), jnp.float32, -s_img, s_img), 'Wk': jax.random.uniform(ks[4], (TXT_DIM, HID), jnp.float32, -s_txt, s_txt), 'bk': jax.random.uniform(ks[5], (HID,), jnp.float32, -s_txt, s_txt), 'Wv': jax.random.uniform(ks[6], (TXT_DIM, HID), jnp.float32, -s_txt, s_txt), 'bv': jax.random.uniform(ks[7], (HID,), jnp.float32, -s_txt, s_txt)}
    _L1_xattn_all = _L1_xattn_setup()
    _L1_xattn_in = {k: v for k, v in _L1_xattn_all.items() if k in ('Wq', 'bq', 'Wk', 'bk', 'Wv', 'bv')}
    del _L1_xattn_all

    def _L1_ffn_setup():
        import jax, jax.numpy as jnp
        import numpy as np
        TOP_K = 2
        EPS = 1e-09
        key = jax.random.key(seed)
        ks = jax.random.split(key, 6)
        B, T, D, H, E = (4, 256, 128, 256, 8)
        x = jax.random.normal(ks[0], (B, T, D), dtype=jnp.float32)
        Wg = jax.random.normal(ks[1], (E, D), dtype=jnp.float32) * 0.02
        W1 = jax.random.normal(ks[2], (E, 2 * H, D), dtype=jnp.float32) * 0.02
        b1 = jax.random.normal(ks[3], (E, 2 * H), dtype=jnp.float32) * 0.02
        Wo = jax.random.normal(ks[4], (D, H), dtype=jnp.float32) * 0.02
        bo = jax.random.normal(ks[5], (D,), dtype=jnp.float32) * 0.02
        return {'x': x, 'Wg': Wg, 'W1': W1, 'b1': b1, 'Wo': Wo, 'bo': bo}
    _L1_ffn_all = _L1_ffn_setup()
    _L1_ffn_in = {k: v for k, v in _L1_ffn_all.items() if k in ('Wg', 'W1', 'b1', 'Wo', 'bo')}
    del _L1_ffn_all

    def _L2_xattn_setup():
        import jax, jax.numpy as jnp
        import numpy as np
        import math
        E = 128
        EV = 128
        FFN = 512
        DINO = 96
        B, S, P = (64, 64, 32)

        def bitnet_linear(x, W, b):
            w_scale = jnp.maximum(jnp.mean(jnp.abs(W)), 1e-05)
            qW = jnp.sign(W) * (jnp.abs(W) > 0.5 * w_scale).astype(W.dtype)
            i_scale = jnp.maximum(jnp.max(jnp.abs(x)), 1e-08) / 127.0
            qx = jnp.clip(jnp.round(x / i_scale), -128.0, 127.0)
            out = jnp.einsum('...i,oi->...o', qx, qW) * (w_scale * i_scale)
            return out + b
        key = jax.random.key(seed)
        ks = iter(jax.random.split(key, 32))

        def lin_w(fin, fout):
            return jax.random.normal(next(ks), (fout, fin), jnp.float32) * math.sqrt(2.0 / fin)
        return {'text_embeddings': jax.random.normal(next(ks), (B, S, E), jnp.float32), 'dinov2_features': jax.random.normal(next(ks), (B, P, DINO), jnp.float32), 'W_d2v': lin_w(DINO, EV), 'b_d2v': jnp.zeros((EV,), jnp.float32), 'W_img': lin_w(EV, E), 'b_img': jnp.zeros((E,), jnp.float32), 'W_txt': lin_w(E, E), 'b_txt': jnp.zeros((E,), jnp.float32), 'W_att0': lin_w(E, E // 2), 'b_att0': jnp.zeros((E // 2,), jnp.float32), 'W_att1': lin_w(E, E // 2), 'b_att1': jnp.zeros((E // 2,), jnp.float32), 'W_f1': lin_w(2 * E, FFN), 'b_f1': jnp.zeros((FFN,), jnp.float32), 'W_f2': lin_w(FFN, E), 'b_f2': jnp.zeros((E,), jnp.float32)}
    _L2_xattn_all = _L2_xattn_setup()
    _L2_xattn_in = {k: v for k, v in _L2_xattn_all.items() if k in ('W_d2v', 'b_d2v', 'W_img', 'b_img', 'W_txt', 'b_txt', 'W_att0', 'b_att0', 'W_att1', 'b_att1', 'W_f1', 'b_f1', 'W_f2', 'b_f2')}
    del _L2_xattn_all

    def _L2_ffn_setup():
        import jax, jax.numpy as jnp
        import numpy as np
        B, T, C, H, E, MIN_E = (4, 256, 128, 128, 16, 2)
        IS_CAUSAL = False

        def _forward(hidden_states, sim_matrix, gates, q_proj, k_proj, v_proj, o_proj):
            b, t, c = hidden_states.shape
            n = b * t
            x = hidden_states.reshape(n, c)
            xn = x / jnp.maximum(jnp.linalg.norm(x, axis=-1, keepdims=True), 1e-12)
            sn = sim_matrix / jnp.maximum(jnp.linalg.norm(sim_matrix, axis=0, keepdims=True), 1e-12)
            logits = xn @ sn - jax.nn.sigmoid(gates)
            gated = jax.nn.relu(logits)
            hard = (gated > 0).astype(gated.dtype)
            mask = gated + jax.lax.stop_gradient(hard - gated)
            inactive = jnp.sum(hard, axis=1) == 0
            _, fb_idx = jax.lax.top_k(logits, MIN_E)
            fb = jnp.zeros((n, logits.shape[1]), gated.dtype).at[jnp.arange(n)[:, None], fb_idx].set(1.0)
            put = jax.lax.stop_gradient(inactive[:, None].astype(gated.dtype) * fb)
            mask = mask * (1.0 - put) + put
            masked = jnp.where(mask > 0, gated, -jnp.inf)
            w = jax.nn.softmax(masked, axis=-1)

            def moe_proj(p):
                y = jnp.einsum('nc,ech->neh', x, p)
                return jnp.einsum('ne,neh->nh', w, y)
            q = moe_proj(q_proj).reshape(b, t, -1)
            k = moe_proj(k_proj).reshape(b, t, -1)
            v = moe_proj(v_proj).reshape(b, t, -1)
            h = q.shape[-1]
            scores = jnp.einsum('bth,bsh->bts', q, k) / jnp.sqrt(jnp.asarray(h, q.dtype))
            if IS_CAUSAL and t > 1:
                causal = jnp.tril(jnp.ones((t, t), bool))
                scores = jnp.where(causal[None], scores, -jnp.inf)
            attn = jax.nn.softmax(scores, axis=-1)
            o = jnp.einsum('bts,bsh->bth', attn, v).reshape(n, h)
            z = jnp.einsum('ne,nh->enh', w, o)
            out = jnp.einsum('enh,ehc->nc', z, o_proj)
            return out.reshape(b, t, c)
        key = jax.random.key(seed)
        ks = jax.random.split(key, 6)
        lim_qkv = float(np.sqrt(6.0 / (C + H)))
        inp = {'hidden_states': jax.random.normal(ks[0], (B, T, C), jnp.float32), 'sim_matrix': jax.random.normal(ks[1], (C, E), jnp.float32), 'gates': jnp.zeros((E,), jnp.float32), 'q_proj': jax.random.uniform(ks[2], (E, C, H), jnp.float32, -lim_qkv, lim_qkv), 'k_proj': jax.random.uniform(ks[3], (E, C, H), jnp.float32, -lim_qkv, lim_qkv), 'v_proj': jax.random.uniform(ks[4], (E, C, H), jnp.float32, -lim_qkv, lim_qkv), 'o_proj': jax.random.uniform(ks[5], (E, H, C), jnp.float32, -lim_qkv, lim_qkv)}
        return inp
    _L2_ffn_all = _L2_ffn_setup()
    _L2_ffn_in = {k: v for k, v in _L2_ffn_all.items() if k in ('sim_matrix', 'gates', 'q_proj', 'k_proj', 'v_proj', 'o_proj')}
    del _L2_ffn_all

    def _L3_xattn_setup():
        import jax, jax.numpy as jnp
        import numpy as np
        N_HEADS = 16
        key = jax.random.key(seed)
        ks = jax.random.split(key, 8)
        b, l, m = (8, 128, 128)
        d_embed, d_cross = (128, 96)
        s_q = 1.0 / np.sqrt(d_embed)
        s_kv = 1.0 / np.sqrt(d_cross)
        return {'x': jax.random.normal(ks[0], (b, l, d_embed), jnp.float32), 'y': jax.random.normal(ks[1], (b, m, d_cross), jnp.float32), 'Wq': jax.random.normal(ks[2], (d_embed, d_embed), jnp.float32) * s_q, 'bq': jax.random.normal(ks[3], (d_embed,), jnp.float32) * 0.01, 'Wkv': jax.random.normal(ks[4], (2 * d_embed, d_cross), jnp.float32) * s_kv, 'bkv': jax.random.normal(ks[5], (2 * d_embed,), jnp.float32) * 0.01, 'Wo': jax.random.normal(ks[6], (d_embed, d_embed), jnp.float32) * s_q, 'bo': jax.random.normal(ks[7], (d_embed,), jnp.float32) * 0.01}
    _L3_xattn_all = _L3_xattn_setup()
    _L3_xattn_in = {k: v for k, v in _L3_xattn_all.items() if k in ('Wq', 'bq', 'Wkv', 'bkv', 'Wo', 'bo')}
    del _L3_xattn_all

    def _L3_ffn_setup():
        import math
        import jax, jax.numpy as jnp
        import numpy as np
        TOP_K = 2
        CAP_FACTOR = 1.25
        CLAMP = 10000.0
        key = jax.random.key(seed)
        k1, k2, k3, k4, k5 = jax.random.split(key, 5)
        B, S, D, F, E = (4, 256, 128, 512, 8)
        std = 0.02
        return {'x': jax.random.normal(k1, (B, S, D), dtype=jnp.float32), 'Wr': jax.random.normal(k2, (D, E), dtype=jnp.float32) * std, 'W1': jax.random.normal(k3, (E, D, F), dtype=jnp.float32) * std, 'W3': jax.random.normal(k4, (E, D, F), dtype=jnp.float32) * std, 'W2': jax.random.normal(k5, (E, F, D), dtype=jnp.float32) * std}
    _L3_ffn_all = _L3_ffn_setup()
    _L3_ffn_in = {k: v for k, v in _L3_ffn_all.items() if k in ('Wr', 'W1', 'W3', 'W2')}
    del _L3_ffn_all
    return {'x': x, 'ctx_768': ctx_768, 'L0_xattn_Wq': _L0_xattn_in['Wq'], 'L0_xattn_Wk': _L0_xattn_in['Wk'], 'L0_xattn_Wv': _L0_xattn_in['Wv'], 'L0_xattn_Wout': _L0_xattn_in['Wout'], 'L0_xattn_bout': _L0_xattn_in['bout'], 'L0_ffn_Wg': _L0_ffn_in['Wg'], 'L0_ffn_bg': _L0_ffn_in['bg'], 'L0_ffn_We': _L0_ffn_in['We'], 'L0_ffn_be': _L0_ffn_in['be'], 'L1_xattn_Wq': _L1_xattn_in['Wq'], 'L1_xattn_bq': _L1_xattn_in['bq'], 'L1_xattn_Wk': _L1_xattn_in['Wk'], 'L1_xattn_bk': _L1_xattn_in['bk'], 'L1_xattn_Wv': _L1_xattn_in['Wv'], 'L1_xattn_bv': _L1_xattn_in['bv'], 'L1_ffn_Wg': _L1_ffn_in['Wg'], 'L1_ffn_W1': _L1_ffn_in['W1'], 'L1_ffn_b1': _L1_ffn_in['b1'], 'L1_ffn_Wo': _L1_ffn_in['Wo'], 'L1_ffn_bo': _L1_ffn_in['bo'], 'L2_xattn_W_d2v': _L2_xattn_in['W_d2v'], 'L2_xattn_b_d2v': _L2_xattn_in['b_d2v'], 'L2_xattn_W_img': _L2_xattn_in['W_img'], 'L2_xattn_b_img': _L2_xattn_in['b_img'], 'L2_xattn_W_txt': _L2_xattn_in['W_txt'], 'L2_xattn_b_txt': _L2_xattn_in['b_txt'], 'L2_xattn_W_att0': _L2_xattn_in['W_att0'], 'L2_xattn_b_att0': _L2_xattn_in['b_att0'], 'L2_xattn_W_att1': _L2_xattn_in['W_att1'], 'L2_xattn_b_att1': _L2_xattn_in['b_att1'], 'L2_xattn_W_f1': _L2_xattn_in['W_f1'], 'L2_xattn_b_f1': _L2_xattn_in['b_f1'], 'L2_xattn_W_f2': _L2_xattn_in['W_f2'], 'L2_xattn_b_f2': _L2_xattn_in['b_f2'], 'L2_ffn_sim_matrix': _L2_ffn_in['sim_matrix'], 'L2_ffn_gates': _L2_ffn_in['gates'], 'L2_ffn_q_proj': _L2_ffn_in['q_proj'], 'L2_ffn_k_proj': _L2_ffn_in['k_proj'], 'L2_ffn_v_proj': _L2_ffn_in['v_proj'], 'L2_ffn_o_proj': _L2_ffn_in['o_proj'], 'L3_xattn_Wq': _L3_xattn_in['Wq'], 'L3_xattn_bq': _L3_xattn_in['bq'], 'L3_xattn_Wkv': _L3_xattn_in['Wkv'], 'L3_xattn_bkv': _L3_xattn_in['bkv'], 'L3_xattn_Wo': _L3_xattn_in['Wo'], 'L3_xattn_bo': _L3_xattn_in['bo'], 'L3_ffn_Wr': _L3_ffn_in['Wr'], 'L3_ffn_W1': _L3_ffn_in['W1'], 'L3_ffn_W3': _L3_ffn_in['W3'], 'L3_ffn_W2': _L3_ffn_in['W2']}

def reference(x, ctx_768, L0_xattn_Wq, L0_xattn_Wk, L0_xattn_Wv, L0_xattn_Wout, L0_xattn_bout, L0_ffn_Wg, L0_ffn_bg, L0_ffn_We, L0_ffn_be, L1_xattn_Wq, L1_xattn_bq, L1_xattn_Wk, L1_xattn_bk, L1_xattn_Wv, L1_xattn_bv, L1_ffn_Wg, L1_ffn_W1, L1_ffn_b1, L1_ffn_Wo, L1_ffn_bo, L2_xattn_W_d2v, L2_xattn_b_d2v, L2_xattn_W_img, L2_xattn_b_img, L2_xattn_W_txt, L2_xattn_b_txt, L2_xattn_W_att0, L2_xattn_b_att0, L2_xattn_W_att1, L2_xattn_b_att1, L2_xattn_W_f1, L2_xattn_b_f1, L2_xattn_W_f2, L2_xattn_b_f2, L2_ffn_sim_matrix, L2_ffn_gates, L2_ffn_q_proj, L2_ffn_k_proj, L2_ffn_v_proj, L2_ffn_o_proj, L3_xattn_Wq, L3_xattn_bq, L3_xattn_Wkv, L3_xattn_bkv, L3_xattn_Wo, L3_xattn_bo, L3_ffn_Wr, L3_ffn_W1, L3_ffn_W3, L3_ffn_W2):
    import jax
    import jax.numpy as jnp

    def _L0_xattn_ref(x, context, Wq, Wk, Wv, Wout, bout):
        import jax, jax.numpy as jnp
        import numpy as np
        HEADS = 8
        DIM_HEAD = 128
        ATTN_MATRIX_SCALE = 1.5
        SCALE = DIM_HEAD ** (-0.5)

        def _split_heads(t):
            b, n, _ = t.shape
            t = t.reshape(b, n, HEADS, DIM_HEAD)
            return t.transpose(2, 0, 1, 3).reshape(HEADS, b * n, DIM_HEAD)
        b, n, _ = x.shape
        qh = _split_heads(jnp.einsum('bnq,qi->bni', x, Wq))
        kh = _split_heads(jnp.einsum('bmc,ci->bmi', context, Wk))
        vh = _split_heads(jnp.einsum('bmc,ci->bmi', context, Wv))
        sim = jnp.einsum('hid,hjd->hij', qh, kh) * SCALE
        mean = jnp.mean(sim, axis=-1, keepdims=True)
        sim = (sim - mean) * ATTN_MATRIX_SCALE + mean
        attn = jax.nn.softmax(sim, axis=-1)
        out = jnp.einsum('hij,hjd->hid', attn, vh)
        out = out.reshape(HEADS, b, n, DIM_HEAD).transpose(1, 2, 0, 3)
        out = out.reshape(b, n, HEADS * DIM_HEAD)
        return jnp.einsum('bni,iq->bnq', out, Wout) + bout

    def _L0_ffn_ref(x, Wg, bg, We, be):
        import jax, jax.numpy as jnp
        import numpy as np
        IN_DIM = 128
        OUT_DIM = 128
        NUM_EXPERTS = 8
        TOP_K = 2
        gate = jax.nn.softmax(x @ Wg + bg, axis=-1)
        topk_vals, topk_idx = jax.lax.top_k(gate, TOP_K)
        onehot = jax.nn.one_hot(topk_idx, NUM_EXPERTS, dtype=gate.dtype)
        gate_sparse = jnp.einsum('bsk,bske->bse', topk_vals, onehot)
        gate_sparse = gate_sparse / jnp.sum(gate_sparse, axis=-1, keepdims=True)
        y = jnp.einsum('bsi,eoi->bseo', x, We) + be[None, None, :, :].transpose(0, 1, 2, 3)
        out = jnp.einsum('bseo,bse->bso', y, gate_sparse)
        return out

    def _L1_xattn_ref(image_features, text_features, Wq, bq, Wk, bk, Wv, bv):
        import jax, jax.numpy as jnp
        import numpy as np
        IMG_DIM, TXT_DIM, HID = (128, 96, 128)
        B, LQ, LK = (8, 256, 256)
        query = jnp.einsum('bqi,ih->bqh', image_features, Wq) + bq
        key = jnp.einsum('bkt,th->bkh', text_features, Wk) + bk
        value = jnp.einsum('bkt,th->bkh', text_features, Wv) + bv
        scale = 1.0 / jnp.sqrt(jnp.asarray(HID, query.dtype))
        scores = jnp.einsum('bqh,bkh->bqk', query, key) * scale
        weights = jax.nn.softmax(scores, axis=-1)
        attended = jnp.einsum('bqk,bkh->bqh', weights, value)
        return attended

    def _L1_ffn_ref(x, Wg, W1, b1, Wo, bo):
        import jax, jax.numpy as jnp
        import numpy as np
        TOP_K = 2
        EPS = 1e-09
        E = Wg.shape[0]
        gate_logits = jnp.einsum('btd,ed->bte', x, Wg)
        gate_scores = jax.nn.softmax(gate_logits, axis=-1)
        topk_val, topk_idx = jax.lax.top_k(gate_scores, TOP_K)
        topk_val = topk_val / (topk_val.sum(axis=-1, keepdims=True) + EPS)
        comb = (jax.nn.one_hot(topk_idx, E, dtype=x.dtype) * topk_val[..., None]).sum(axis=-2)
        out = jnp.zeros_like(x)
        for e in range(E):
            h = jnp.einsum('btd,hd->bth', x, W1[e]) + b1[e]
            a, b = jnp.split(h, 2, axis=-1)
            g = a * jax.nn.sigmoid(b)
            eo = jnp.einsum('bth,dh->btd', g, Wo) + bo
            out = out + eo * comb[..., e:e + 1]
        return out

    def _L2_xattn_ref(text_embeddings, dinov2_features, W_d2v, b_d2v, W_img, b_img, W_txt, b_txt, W_att0, b_att0, W_att1, b_att1, W_f1, b_f1, W_f2, b_f2):
        import jax, jax.numpy as jnp
        import numpy as np
        import math
        E = 128
        EV = 128
        FFN = 512
        DINO = 96
        B, S, P = (64, 64, 32)

        def bitnet_linear(x, W, b):
            w_scale = jnp.maximum(jnp.mean(jnp.abs(W)), 1e-05)
            qW = jnp.sign(W) * (jnp.abs(W) > 0.5 * w_scale).astype(W.dtype)
            i_scale = jnp.maximum(jnp.max(jnp.abs(x)), 1e-08) / 127.0
            qx = jnp.clip(jnp.round(x / i_scale), -128.0, 127.0)
            out = jnp.einsum('...i,oi->...o', qx, qW) * (w_scale * i_scale)
            return out + b
        b, s, e = text_embeddings.shape
        vis = bitnet_linear(dinov2_features, W_d2v, b_d2v)
        image_embeds = bitnet_linear(vis, W_img, b_img)
        fused = bitnet_linear(text_embeddings, W_txt, b_txt)
        inv_sqrt_e = 1.0 / math.sqrt(e)
        for Wa, ba in ((W_att0, b_att0), (W_att1, b_att1)):
            kv = bitnet_linear(image_embeds, Wa, ba)
            k = jnp.concatenate([kv, kv], axis=-1)
            scores = jnp.einsum('bse,bpe->bsp', fused, k) * inv_sqrt_e
            attn = jax.nn.softmax(scores, axis=-1)
            fused = fused + 0.1 * jnp.einsum('bsp,bpe->bse', attn, k)
        avg_img = jnp.mean(image_embeds, axis=1, keepdims=True)
        concatenated = jnp.concatenate([fused, jnp.broadcast_to(avg_img, (b, s, e))], axis=-1)
        h = jax.nn.relu(bitnet_linear(concatenated, W_f1, b_f1))
        return bitnet_linear(h, W_f2, b_f2)

    def _L2_ffn_ref(hidden_states, sim_matrix, gates, q_proj, k_proj, v_proj, o_proj):
        import jax, jax.numpy as jnp
        import numpy as np
        B, T, C, H, E, MIN_E = (4, 256, 128, 128, 16, 2)
        IS_CAUSAL = False

        def _forward(hidden_states, sim_matrix, gates, q_proj, k_proj, v_proj, o_proj):
            b, t, c = hidden_states.shape
            n = b * t
            x = hidden_states.reshape(n, c)
            xn = x / jnp.maximum(jnp.linalg.norm(x, axis=-1, keepdims=True), 1e-12)
            sn = sim_matrix / jnp.maximum(jnp.linalg.norm(sim_matrix, axis=0, keepdims=True), 1e-12)
            logits = xn @ sn - jax.nn.sigmoid(gates)
            gated = jax.nn.relu(logits)
            hard = (gated > 0).astype(gated.dtype)
            mask = gated + jax.lax.stop_gradient(hard - gated)
            inactive = jnp.sum(hard, axis=1) == 0
            _, fb_idx = jax.lax.top_k(logits, MIN_E)
            fb = jnp.zeros((n, logits.shape[1]), gated.dtype).at[jnp.arange(n)[:, None], fb_idx].set(1.0)
            put = jax.lax.stop_gradient(inactive[:, None].astype(gated.dtype) * fb)
            mask = mask * (1.0 - put) + put
            masked = jnp.where(mask > 0, gated, -jnp.inf)
            w = jax.nn.softmax(masked, axis=-1)

            def moe_proj(p):
                y = jnp.einsum('nc,ech->neh', x, p)
                return jnp.einsum('ne,neh->nh', w, y)
            q = moe_proj(q_proj).reshape(b, t, -1)
            k = moe_proj(k_proj).reshape(b, t, -1)
            v = moe_proj(v_proj).reshape(b, t, -1)
            h = q.shape[-1]
            scores = jnp.einsum('bth,bsh->bts', q, k) / jnp.sqrt(jnp.asarray(h, q.dtype))
            if IS_CAUSAL and t > 1:
                causal = jnp.tril(jnp.ones((t, t), bool))
                scores = jnp.where(causal[None], scores, -jnp.inf)
            attn = jax.nn.softmax(scores, axis=-1)
            o = jnp.einsum('bts,bsh->bth', attn, v).reshape(n, h)
            z = jnp.einsum('ne,nh->enh', w, o)
            out = jnp.einsum('enh,ehc->nc', z, o_proj)
            return out.reshape(b, t, c)
        return _forward(hidden_states, sim_matrix, gates, q_proj, k_proj, v_proj, o_proj)

    def _L3_xattn_ref(x, y, Wq, bq, Wkv, bkv, Wo, bo):
        import jax, jax.numpy as jnp
        import numpy as np
        N_HEADS = 16
        b, l, d = x.shape
        m = y.shape[1]
        h = N_HEADS
        dh = d // h
        q = (jnp.einsum('bld,ed->ble', x, Wq) + bq).reshape(b, l, h, dh)
        kv = (jnp.einsum('bmc,ec->bme', y, Wkv) + bkv).reshape(b, m, h, 2 * dh)
        k, v = (kv[..., :dh], kv[..., dh:])
        scale = 1.0 / jnp.sqrt(jnp.asarray(dh, x.dtype))
        att = jax.nn.softmax(jnp.einsum('blhd,bmhd->blmh', q, k) * scale, axis=2)
        out = jnp.einsum('blmh,bmhd->blhd', att, v).reshape(b, l, d)
        return jnp.einsum('bld,ed->ble', out, Wo) + bo

    def _L3_ffn_ref(x, Wr, W1, W3, W2):
        import math
        import jax, jax.numpy as jnp
        import numpy as np
        TOP_K = 2
        CAP_FACTOR = 1.25
        CLAMP = 10000.0
        B, S, D = x.shape
        E = Wr.shape[1]
        K = TOP_K
        T = B * S
        cap = max(1, math.ceil(T * K * CAP_FACTOR / E))
        xf = x.reshape(T, D)
        logits = jnp.clip(xf @ Wr, -CLAMP, CLAMP)
        top_v, top_i = jax.lax.top_k(logits, K)
        m = jnp.max(top_v, axis=-1, keepdims=True)
        expv = jnp.exp(top_v - m)
        top_p = expv / (jnp.sum(expv, axis=-1, keepdims=True) + 1e-12)
        Sp = T * K
        experts = top_i.reshape(Sp)
        weights = top_p.reshape(Sp)
        tokens = jnp.repeat(jnp.arange(T), K)
        oh = experts[:, None] == jnp.arange(E)[None, :]
        pos = jnp.sum(jnp.cumsum(oh.astype(jnp.int32), axis=0) * oh, axis=-1) - 1
        kept = pos < cap
        pos_safe = jnp.where(kept, pos, cap)
        xe = jnp.zeros((E, cap + 1, D), x.dtype).at[experts, pos_safe].set(xf[tokens])[:, :cap]
        h = jax.nn.silu(jnp.einsum('ecd,edf->ecf', xe, W1)) * jnp.einsum('ecd,edf->ecf', xe, W3)
        ye = jnp.einsum('ecf,efd->ecd', h, W2)
        yp = ye[experts, jnp.minimum(pos_safe, cap - 1)]
        wk = weights * kept.astype(weights.dtype)
        out = jnp.zeros((T, D), x.dtype).at[tokens].add(wk[:, None] * yp)
        return out.reshape(B, S, D)
    x = x + _L0_xattn_ref(_layernorm(x, axis=-1), ctx_768, L0_xattn_Wq, L0_xattn_Wk, L0_xattn_Wv, L0_xattn_Wout, L0_xattn_bout)
    x = x + _L0_ffn_ref(_layernorm(x, axis=-1), L0_ffn_Wg, L0_ffn_bg, L0_ffn_We, L0_ffn_be)
    x = x + _L1_xattn_ref(_layernorm(x, axis=-1), ctx_768, L1_xattn_Wq, L1_xattn_bq, L1_xattn_Wk, L1_xattn_bk, L1_xattn_Wv, L1_xattn_bv)
    x = x + _L1_ffn_ref(_layernorm(x, axis=-1), L1_ffn_Wg, L1_ffn_W1, L1_ffn_b1, L1_ffn_Wo, L1_ffn_bo)
    x = x + _L2_xattn_ref(_layernorm(x, axis=-1), ctx_768, L2_xattn_W_d2v, L2_xattn_b_d2v, L2_xattn_W_img, L2_xattn_b_img, L2_xattn_W_txt, L2_xattn_b_txt, L2_xattn_W_att0, L2_xattn_b_att0, L2_xattn_W_att1, L2_xattn_b_att1, L2_xattn_W_f1, L2_xattn_b_f1, L2_xattn_W_f2, L2_xattn_b_f2)
    x = x + _L2_ffn_ref(_layernorm(x, axis=-1), L2_ffn_sim_matrix, L2_ffn_gates, L2_ffn_q_proj, L2_ffn_k_proj, L2_ffn_v_proj, L2_ffn_o_proj)
    x = x + _L3_xattn_ref(_layernorm(x, axis=-1), ctx_768, L3_xattn_Wq, L3_xattn_bq, L3_xattn_Wkv, L3_xattn_bkv, L3_xattn_Wo, L3_xattn_bo)
    x = x + _L3_ffn_ref(_layernorm(x, axis=-1), L3_ffn_Wr, L3_ffn_W1, L3_ffn_W3, L3_ffn_W2)
    return x

_drawn_inputs = setup_inputs


def setup_inputs(seed=0):
    import zlib

    import numpy as np

    out = dict(_drawn_inputs(seed))
    spreads = {'L0_xattn_bout': (0.0, 0.1),
     'L0_ffn_bg': (0.0, 0.1),
     'L2_xattn_b_d2v': (0.0, 0.1),
     'L2_xattn_b_img': (0.0, 0.1),
     'L2_xattn_b_txt': (0.0, 0.1),
     'L2_xattn_b_att0': (0.0, 0.793),
     'L2_xattn_b_att1': (0.0, 0.768),
     'L2_xattn_b_f1': (0.0, 0.1),
     'L2_xattn_b_f2': (0.0, 0.1),
     'L2_ffn_gates': (0.0, 0.1)}
    factors = {'L1_xattn_bq': 5.832,
     'L1_xattn_bk': 8.0,
     'L1_ffn_b1': 6.809,
     'L2_ffn_q_proj': 3.472,
     'L2_ffn_k_proj': 3.449,
     'L3_xattn_bq': 8.0,
     'L3_xattn_bkv': 7.291,
     'L3_xattn_bo': 7.74,
     'L3_ffn_Wr': 8.0,
     'L3_ffn_W1': 8.0,
     'L3_ffn_W3': 8.0,
     'L3_ffn_W2': 8.0}
    for name, (base, spread) in spreads.items():
        noise = np.random.default_rng([zlib.crc32(name.encode()), seed]).standard_normal(out[name].shape)
        drawn = base * np.exp(spread * noise) if base else spread * noise
        out[name] = jnp.asarray(drawn.astype(out[name].dtype))
    for name, factor in factors.items():
        out[name] = (out[name] * factor).astype(out[name].dtype)
    return out
```

```python
from contextlib import ExitStack

import concourse.bass as bass
from concourse import mybir

F32 = mybir.dt.float32
BF16 = mybir.dt.bfloat16
ALU = mybir.AluOpType
ACT = mybir.ActivationFunctionType
X = mybir.AxisListType.X
RADD = bass.bass_isa.ReduceOp.add
RMAX = bass.bass_isa.ReduceOp.max

P = 128
B = 2
D = 128
C = 96
N = 512
T = N // P
M = 1024
MT = M // P
KB = M // B
BIG = 3.0e38
ROUND = 12582912.0


class Chain:

    def __init__(self, engine, semaphore):
        self.engine, self.semaphore = engine, semaphore
        self.base, self.step, self.turn, self.per = 0, 0, None, 0

    def __call__(self, ins):
        ins.then_inc(self.semaphore, 1)
        self.step += 1
        if self.turn is None:
            self.engine.wait_ge(self.semaphore, self.base + self.step)
        else:
            self.engine.wait_ge(self.semaphore, self.turn * self.per + (self.base + self.step))
        return ins

    def enter(self, turn, per):
        self.base, self.step, self.turn, self.per = self.base + self.step, 0, turn, per

    def leave(self, turns):
        assert self.step == self.per, (self.step, self.per)
        self.base, self.step, self.turn = self.base + turns * self.per, 0, None


def wide(ap, n):
    return ap.unsqueeze(2).broadcast_to([ap.shape[0], ap.shape[1], n])


def build(nc, i, out):
    with ExitStack() as ctx:
        def sb(name, shape, dt=F32):
            return ctx.enter_context(nc.sbuf_tensor(name, shape, dt))

        def sem(name):
            return ctx.enter_context(nc.semaphore(name))

        PS = ctx.enter_context(nc.psum_tensor("PS", [P, 8, 512], F32))

        def bank(b):
            return PS[:, b, :]

        def quarters(b):
            return PS[:, b, :].rearrange("p (t d) -> p t d", t=4)

        x = sb("x", [P, T, D])
        xn = sb("xn", [P, T, D])
        xT = sb("xT", [P, N])
        ident = sb("ident", [P, P])
        identb = sb("identb", [P, P], BF16)
        ctx_rows = sb("ctx_rows", [P, MT, C])
        ctxT = sb("ctxT", [C, M])
        stats = sb("stats", [P, T, 6])
        moments = sb("moments", [P, T, 2])
        rstd = sb("rstd", [P, T])
        minus_half = sb("minus_half", [P, 16])

        room = sb("room", [P, 12288])

        weight_room = sb("weight_room", [P, 8192])

        def place_in(whole, at, shape):
            size = 1
            for n in shape[1:]:
                size *= n
            ap = whole[0:shape[0], at:at + size]
            if len(shape) == 3:
                ap = ap.rearrange("p (a b) -> p a b", a=shape[1])
            return ap

        def place(at, shape):
            return place_in(room, at, shape)

        def place_weights(at, shape):
            return place_in(weight_room, at, shape)

        x_loaded = sem("x_loaded")
        ctx_loaded = sem("ctx_loaded")
        ident_zero = sem("ident_zero")
        ident_done = sem("ident_done")
        dve_chain = sem("dve_chain")
        act_chain = sem("act_chain")
        pool_chain = sem("pool_chain")
        x_updated = sem("x_updated")
        ln_moments = sem("ln_moments")
        ln_rstd = sem("ln_rstd")
        ln_rows = sem("ln_rows")
        ln_turned = sem("ln_turned")
        ln_xT = sem("ln_xT")
        stored = sem("stored")

        def const_pool(pool):
            nc.gpsimd.memset(ident[:], 0.0).then_inc(ident_zero, 1)
            nc.gpsimd.memset(minus_half[:], -0.5).then_inc(ident_done, 1)
            pool.wait_ge(ident_zero, 1)
            nc.gpsimd.affine_select(out=ident[:], in_=ident[:], compare_op=ALU.not_equal, fill=1.0, base=0,
                                    pattern=[[-1, P]], channel_multiplier=1).then_inc(ident_done, 1)
            pool.wait_ge(ident_done, 2)
            nc.gpsimd.tensor_copy(identb[:], ident[:]).then_inc(ident_done, 1)

        LN_BANK = 7

        def ln_dve(dve, link, n):
            if n == 0:
                dve.wait_ge(x_loaded, 16)
            else:
                dve.wait_ge(x_updated, T * n)
            for t in range(T):
                ins = nc.vector.bn_stats(stats[:, t, :], x[:, t, :])
            link(ins)
            for t in range(T):
                ins = nc.vector.bn_aggr(moments[:, t, :], stats[:, t, :])
            ins.then_inc(ln_moments, 1)
            dve.wait_ge(ln_rstd, n + 1)
            for t in range(T):
                nc.vector.tensor_scalar(xn[:, t, :], x[:, t, :], moments[:, t, 0:1], rstd[:, t:t + 1],
                                        ALU.subtract, ALU.mult).then_inc(ln_rows, 1)

        def ln_pool(pool, link, n):
            pool.wait_ge(ln_moments, n + 1)
            link(nc.gpsimd.tensor_scalar(rstd[:], moments[:, :, 1], 1e-5, None, ALU.add))
            nc.gpsimd.tensor_tensor(rstd[:], rstd[:], minus_half[:, 0:T], ALU.pow).then_inc(ln_rstd, 1)

        def ln_pe(pe, n):
            for t in range(T):
                pe.wait_ge(ln_rows, T * n + t + 1)
                ins = nc.tensor.transpose(bank(LN_BANK)[:, t * P:(t + 1) * P], xn[:, t, :], ident[:])
            ins.then_inc(ln_turned, 1)

        def ln_act(act, n):
            act.wait_ge(ln_turned, n + 1)
            nc.scalar.activation(xT[:], bank(LN_BANK), ACT.Copy).then_inc(ln_xT, 1)

        H0 = 8
        S0 = 1.5 * float(D) ** -0.5
        wq = place_weights(0, [P, H0 * D])
        wk = place_weights(1024, [C, H0 * D])
        wv = place_weights(2048, [C, H0 * D])
        wout = place_weights(3072, [P, H0, D])
        wqT = place(6144, [P, H0, D])
        wkT = place(7168, [P, H0, C])
        wvT = place(7936, [P, H0, C])
        A_all = place_weights(4096, [P, H0, C])
        M_all = place_weights(4864, [C, H0, D])
        A_head = sb("A_head", [P, C])
        T_head = place(8704, [C, N])
        probs = place(0, [P, 2, M])
        probsT = place(2048, [P, MT, N])
        mixT = place(9216, [C, N])
        row_max = sb("row_max", [P, T])
        neg_max = sb("neg_max", [P, T])
        row_sum = sb("row_sum", [P, T])
        row_inv = sb("row_inv", [P, T])
        bout = sb("bout", [P, D])
        l0_loaded = sem("l0_loaded")
        fold_turned = sem("fold_turned")
        fold_dve = sem("fold_dve")
        fold_act = sem("fold_act")
        l0_A = sem("l0_A")
        l0_query = sem("l0_query")
        l0_T = sem("l0_T")
        l0_scores = sem("l0_scores")
        l0_negmax = sem("l0_negmax")
        l0_probs = sem("l0_probs")
        l0_turned = sem("l0_turned")
        l0_free_a = sem("l0_free_a")
        l0_free_b = sem("l0_free_b")
        l0_mixed = sem("l0_mixed")
        l0_mixT = sem("l0_mixT")
        l0_headout = sem("l0_headout")
        l0_added = sem("l0_added")

        def fold_pe(pe):
            pe.wait_ge(ident_done, 2)
            pe.wait_ge(ctx_loaded, 16)
            for half in range(2):
                for q in range(4):
                    ins = nc.tensor.transpose(bank(half)[0:C, q * P:(q + 1) * P], ctx_rows[:, 4 * half + q, :], ident[:])
                ins.then_inc(fold_turned, 1)
            pe.wait_ge(l0_loaded, 16 * 5)
            for n, w in ((2, wq), (4, wk), (6, wv)):
                rows = P if n == 2 else C
                for half in range(2):
                    for q in range(4):
                        h = 4 * half + q
                        ins = nc.tensor.transpose(bank(n + half)[:, q * P:q * P + rows], w[:, h * D:(h + 1) * D],
                                                  ident[0:rows, 0:rows])
                    ins.then_inc(fold_turned, 1)
            pe.wait_ge(fold_dve, 4)
            pe.wait_ge(fold_act, 4)
            for half in range(2):
                for q in range(4):
                    h = 4 * half + q
                    ins = nc.tensor.matmul(bank(half)[:, q * P:q * P + C], wqT[:, h, :], wkT[:, h, :],
                                           start=True, stop=True)
                ins.then_inc(fold_turned, 1)
            for half in range(2):
                for q in range(4):
                    h = 4 * half + q
                    ins = nc.tensor.matmul(bank(2 + half)[0:C, q * P:(q + 1) * P], wvT[:, h, :], wout[:, h, :],
                                           start=True, stop=True)
                ins.then_inc(fold_turned, 1)

        def fold_copy(eng, copy, half, done):
            lo = 4 * half
            eng.wait_ge(fold_turned, 1 + half)
            copy(ctxT[:, half * 512:(half + 1) * 512], bank(half)[0:C, :]).then_inc(done, 1)
            eng.wait_ge(fold_turned, 3 + half)
            copy(wqT[:, lo:lo + 4, :], quarters(2 + half)).then_inc(done, 1)
            eng.wait_ge(fold_turned, 5 + half)
            copy(wkT[:, lo:lo + 4, :], quarters(4 + half)[:, :, 0:C]).then_inc(done, 1)
            eng.wait_ge(fold_turned, 7 + half)
            copy(wvT[:, lo:lo + 4, :], quarters(6 + half)[:, :, 0:C]).then_inc(done, 1)
            eng.wait_ge(fold_turned, 9 + half)
            copy(A_all[:, lo:lo + 4, :], quarters(half)[:, :, 0:C]).then_inc(done, 1)
            eng.wait_ge(fold_turned, 11 + half)
            copy(M_all[:, lo:lo + 4, :], quarters(2 + half)[0:C]).then_inc(done, 1)

        def act_copy(dst, src):
            return nc.scalar.activation(dst, src, ACT.Copy)

        def l0_scores_pe(pe, t):
            for half in range(2):
                ins = nc.tensor.matmul(bank(2 * (t % 2) + half), T_head[:, t * P:(t + 1) * P],
                                       ctxT[:, half * 512:(half + 1) * 512], start=True, stop=True)
            ins.then_inc(l0_scores, 1)

        def l0_query_pe(pe, h):
            pe.wait_ge(l0_A, h + 1)
            nc.tensor.matmul(bank(7)[0:C, :], A_head[:], xT[:], start=True, stop=True).then_inc(l0_query, 1)

        def l0_turn_pe(pe, h, t):
            pe.wait_ge(l0_probs, T * h + (t + 1))
            for half, free in ((0, l0_free_a), (1, l0_free_b)):
                pe.wait_ge(free, T * h + (t + 1))
                for q in range(4):
                    k = 4 * half + q
                    ins = nc.tensor.transpose(bank(4 + half)[:, q * P:(q + 1) * P],
                                              probs[:, t % 2, k * P:(k + 1) * P], ident[:])
                ins.then_inc(l0_turned, 1)

        def l0_head_pe(pe, h, last):
            l0_scores_pe(pe, 1)
            l0_turn_pe(pe, h, 0)
            l0_scores_pe(pe, 2)
            l0_turn_pe(pe, h, 1)
            l0_scores_pe(pe, 3)
            if not last:
                l0_query_pe(pe, h + 1)
            l0_turn_pe(pe, h, 2)
            l0_turn_pe(pe, h, 3)
            pe.wait_ge(l0_added, h + 1)
            for half, free in ((0, l0_free_a), (1, l0_free_b)):
                pe.wait_ge(free, T * h + (T + 1))
                for q in range(4):
                    k = 4 * half + q
                    ins = nc.tensor.matmul(bank(6)[0:C, :], ctx_rows[:, k, :], probsT[:, k, :],
                                           start=(k == 0), stop=(k == MT - 1))
            ins.then_inc(l0_mixed, 1)
            if not last:
                pe.wait_ge(l0_T, h + 2)
                l0_scores_pe(pe, 0)
            pe.wait_ge(l0_mixT, h + 1)
            for t in range(T):
                ins = nc.tensor.matmul(bank(6)[:, t * P:(t + 1) * P], mixT[:, t * P:(t + 1) * P],
                                       M_all[:, h, :] if last else M_all[:, bass.ds(h, 1), :], start=True, stop=True)
            ins.then_inc(l0_headout, 1)

        def l0_pe(pe):
            pe.wait_ge(ln_xT, 1)
            pe.wait_ge(fold_dve, 6)
            pe.wait_ge(fold_act, 6)
            l0_query_pe(pe, 0)
            pe.wait_ge(l0_T, 1)
            l0_scores_pe(pe, 0)
            with pe.Fori(0, H0 - 1) as h:
                l0_head_pe(pe, h, False)
            l0_head_pe(pe, H0 - 1, True)

        def l0_max_dve(dve, link, h, t):
            dve.wait_ge(l0_scores, T * h + (t + 1))
            link(nc.vector.tensor_reduce(row_max[:, t:t + 1], PS[:, 2 * (t % 2):2 * (t % 2) + 2, :],
                                         mybir.AxisListType.XY, ALU.max))
            nc.vector.tensor_scalar(neg_max[:, t:t + 1], row_max[:, t:t + 1], -S0, None, ALU.mult).then_inc(l0_negmax, 1)

        def l0_turned_dve(dve, h, t):
            dve.wait_ge(l0_turned, 2 * T * h + (2 * t + 1))
            nc.vector.tensor_copy(probsT[:, 0:4, t * P:(t + 1) * P], quarters(4)).then_inc(l0_free_a, 1)

        def l0_head_dve(dve, link, h, last):
            for t in range(T):
                if t < T - 1:
                    l0_max_dve(dve, link, h, t + 1)
                l0_turned_dve(dve, h, t)
            dve.wait_ge(l0_probs, T * h + T)
            link(nc.vector.reciprocal(row_inv[:], row_sum[:]))
            if not last:
                l0_max_dve(dve, link, h + 1, 0)
            dve.wait_ge(l0_headout, h + 1)
            dve.wait_ge(l0_added, h + 1)
            for t in range(T):
                ins = nc.vector.scalar_tensor_tensor(out=x[:, t, :], in0=quarters(6)[:, t, :], scalar=row_inv[:, t:t + 1],
                                                     in1=x[:, t, :], op0=ALU.mult, op1=ALU.add)
                if last:
                    ins.then_inc(x_updated, 1)
            if not last:
                ins.then_inc(l0_added, 1)

        def l0_dve(dve, link):
            dve.wait_ge(l0_loaded, 16 * 5)
            dve.wait_ge(ln_rows, T)
            dve.sem_inc(l0_free_a, 1)
            nc.vector.tensor_tensor(x[:], x[:], bout[:].unsqueeze(1).broadcast_to([P, T, D]), ALU.add).then_inc(l0_added, 1)
            l0_max_dve(dve, link, 0, 0)
            with dve.Fori(0, H0 - 1) as h:
                link.enter(h, 5)
                l0_head_dve(dve, link, h, False)
            link.leave(H0 - 1)
            l0_head_dve(dve, link, H0 - 1, True)

        def l0_exp_act(act, h, t):
            act.wait_ge(l0_negmax, T * h + (t + 1))
            nc.scalar.activation(probs[:, t % 2, :].rearrange("p (b k) -> p b k", b=2), PS[:, 2 * (t % 2):2 * (t % 2) + 2, :],
                                 ACT.Exp, bias=neg_max[:, t:t + 1], scale=S0,
                                 accum_out=row_sum[:, t:t + 1]).then_inc(l0_probs, 1)

        def l0_head_act(act, h, last):
            for t in range(T):
                if t < T - 1:
                    l0_exp_act(act, h, t + 1)
                elif not last:
                    act.wait_ge(l0_query, h + 2)
                    act_copy(T_head[:], bank(7)[0:C, :]).then_inc(l0_T, 1)
                act.wait_ge(l0_turned, 2 * T * h + (2 * t + 2))
                act_copy(probsT[:, 4:8, t * P:(t + 1) * P], quarters(5)).then_inc(l0_free_b, 1)
            act.wait_ge(l0_mixed, h + 1)
            act_copy(mixT[:], bank(6)[0:C, :]).then_inc(l0_mixT, 1)
            if not last:
                l0_exp_act(act, h + 1, 0)

        def l0_act(act):
            act.sem_inc(l0_free_b, 1)
            act.wait_ge(l0_query, 1)
            act_copy(T_head[:], bank(7)[0:C, :]).then_inc(l0_T, 1)
            l0_exp_act(act, 0, 0)
            with act.Fori(0, H0 - 1) as h:
                l0_head_act(act, h, False)
            l0_head_act(act, H0 - 1, True)

        def l0_pool(pool):
            pool.wait_ge(fold_dve, 5)
            pool.wait_ge(fold_act, 5)
            nc.gpsimd.tensor_copy(A_head[:], A_all[:, 0, :]).then_inc(l0_A, 1)
            with pool.Fori(1, H0) as h:
                pool.wait_ge(l0_query, h)
                nc.gpsimd.tensor_copy(A_head[:], A_all[:, bass.ds(h, 1), :].rearrange("p a c -> p (a c)")).then_inc(l0_A, 1)

        rev = sb("rev", [P, T, 16])
        logits = sb("logits", [P, T, 16])
        shifted = sb("shifted", [P, T, 16])
        gate = sb("gate", [P, T, 16])
        left = sb("left", [P, T, 16])
        equal = sb("equal", [P, T, 16])
        first = sb("first", [P, T, 16])
        second = sb("second", [P, T, 16])
        chosen = sb("chosen", [P, T, 16])
        comb = sb("comb", [P, T, 16])
        most = sb("most", [P, T])
        peak = sb("peak", [P, T])
        total = sb("total", [P, T])
        total2 = sb("total2", [P, T])
        rev_done = sem("rev_done")
        gate_shifted = sem("gate_shifted")
        gate_exp = sem("gate_exp")

        def rev_pool():
            for e in range(16):
                ins = nc.gpsimd.memset(rev[:, :, e], 16.0 - e)
            ins.then_inc(rev_done, 1)

        def top2_dve(link, values, E):
            v = values
            for pick in (first, second):
                link(nc.vector.tensor_reduce(most[:], v[:, :, 0:E], X, ALU.max))
                link(nc.vector.tensor_tensor(equal[:, :, 0:E], v[:, :, 0:E], wide(most[:], E), ALU.is_equal))
                link(nc.vector.tensor_tensor(equal[:, :, 0:E], equal[:, :, 0:E], rev[:, :, 0:E], ALU.mult))
                link(nc.vector.tensor_reduce(most[:], equal[:, :, 0:E], X, ALU.max))
                link(nc.vector.tensor_tensor(pick[:, :, 0:E], equal[:, :, 0:E], wide(most[:], E), ALU.is_equal))
                if pick is first:
                    link(nc.vector.scalar_tensor_tensor(out=left[:, :, 0:E], in0=first[:, :, 0:E], scalar=-BIG,
                                                        in1=v[:, :, 0:E], op0=ALU.mult, op1=ALU.add))
                    v = left
            link(nc.vector.tensor_tensor(chosen[:, :, 0:E], first[:, :, 0:E], second[:, :, 0:E], ALU.add))

        def shift_dve(link, values, E):
            link(nc.vector.tensor_reduce(peak[:], values[:, :, 0:E], X, ALU.max))
            nc.vector.tensor_tensor(shifted[:, :, 0:E], values[:, :, 0:E], wide(peak[:], E), ALU.subtract).then_inc(gate_shifted, 1)

        def gate_act(act, n, E):
            act.wait_ge(gate_shifted, n)
            nc.scalar.activation(gate[:, :, 0:E], shifted[:, :, 0:E], ACT.Exp).then_inc(gate_exp, 1)

        def weights_dve(link, E, eps_of_all=0.0, eps=0.0):
            link(nc.vector.tensor_tensor(comb[:, :, 0:E], gate[:, :, 0:E], chosen[:, :, 0:E], ALU.mult))
            link(nc.vector.tensor_reduce(total[:], comb[:, :, 0:E], X, ALU.add))
            if eps_of_all:
                link(nc.vector.tensor_reduce(total2[:], gate[:, :, 0:E], X, ALU.add))
                link(nc.vector.scalar_tensor_tensor(out=total[:], in0=total2[:], scalar=eps_of_all, in1=total[:],
                                                    op0=ALU.mult, op1=ALU.add))
            if eps:
                link(nc.vector.tensor_scalar(total[:], total[:], eps, None, ALU.add))
            link(nc.vector.reciprocal(total[:], total[:]))
            link(nc.vector.tensor_tensor(comb[:, :, 0:E], comb[:, :, 0:E], wide(total[:], E), ALU.mult))

        E1 = 8
        we = place_weights(5888, [P, E1, D])
        weT = place_weights(6912, [P, E1, D])
        wg1 = sb("wg1", [P, E1])
        bg1 = sb("bg1", [P, E1])
        be1 = sb("be1", [E1, D])
        combT = sb("combT", [16, N])
        l1_loaded = sem("l1_loaded")
        l1_we_turned = sem("l1_we_turned")
        l1_weT = sem("l1_weT")
        l1_logits = sem("l1_logits")
        l1_comb = sem("l1_comb")
        l1_combT_ps = sem("l1_combT_ps")
        l1_combT = sem("l1_combT")
        l1_bias = sem("l1_bias")
        l1_y = sem("l1_y")
        l1_used = sem("l1_used")
        l1_added = sem("l1_added")

        def l1_prepare_pe(pe):
            pe.wait_ge(l1_loaded, 16 * 4)
            for half in range(2):
                for q in range(4):
                    ins = nc.tensor.transpose(bank(half)[:, q * P:(q + 1) * P], we[:, 4 * half + q, :], ident[:])
                ins.then_inc(l1_we_turned, 1)

        def l1_prepare_act(act):
            for half in range(2):
                act.wait_ge(l1_we_turned, half + 1)
                act_copy(weT[:, 4 * half:4 * half + 4, :], quarters(half)).then_inc(l1_weT, 1)

        def l1_pe(pe):
            pe.wait_ge(ln_xT, 2)
            for t in range(T):
                ins = nc.tensor.matmul(bank(6)[:, t * E1:(t + 1) * E1], xT[:, t * P:(t + 1) * P], wg1[:], start=True, stop=True)
            ins.then_inc(l1_logits, 1)
            pe.wait_ge(l1_weT, 2)
            for g in range(6):
                half, t = g // T, g % T
                nc.tensor.matmul(bank(g), xT[:, t * P:(t + 1) * P], weT[:, 4 * half:4 * half + 4, :],
                                 start=True, stop=True).then_inc(l1_y, 1)
            pe.wait_ge(l1_comb, 1)
            for t in range(T):
                ins = nc.tensor.transpose(bank(6)[0:E1, t * P:(t + 1) * P], comb[:, t, 0:E1], ident[:])
            ins.then_inc(l1_combT_ps, 1)
            pe.wait_ge(l1_combT, 1)
            for t in range(T):
                ins = nc.tensor.matmul(bank(7)[:, t * P:(t + 1) * P], combT[0:E1, t * P:(t + 1) * P], be1[:], start=True, stop=True)
            ins.then_inc(l1_bias, 1)
            for g in (6, 7):
                pe.wait_ge(l1_used, 1)
                nc.tensor.matmul(bank(g - 6), xT[:, (g % T) * P:(g % T + 1) * P], weT[:, 4:8, :],
                                 start=True, stop=True).then_inc(l1_y, 1)

        def l1_dve(dve, link):
            dve.wait_ge(l1_loaded, 16 * 4)
            dve.wait_ge(rev_done, 1)
            dve.wait_ge(l1_logits, 1)
            link(nc.vector.tensor_tensor(logits[:, :, 0:E1], bank(6)[:, 0:T * E1].rearrange("p (t e) -> p t e", t=T),
                                         bg1[:].unsqueeze(1).broadcast_to([P, T, E1]), ALU.add))
            shift_dve(link, logits, E1)
            dve.wait_ge(gate_exp, 1)
            top2_dve(link, gate, E1)
            weights_dve(link, E1)
            dve.sem_inc(l1_comb, 1)
            dve.wait_ge(l1_bias, 1)
            link(nc.vector.tensor_tensor(x[:], x[:], quarters(7), ALU.add))
            for e in range(E1):
                half, q = e // 4, e % 4
                for t in range(T):
                    g = T * half + t
                    dve.wait_ge(l1_y, g + 1)
                    ins = nc.vector.scalar_tensor_tensor(out=x[:, t, :], in0=quarters(g % 6)[:, q, :], scalar=comb[:, t, e:e + 1],
                                                         in1=x[:, t, :], op0=ALU.mult, op1=ALU.add)
                    if e == E1 - 1:
                        ins.then_inc(x_updated, 1)
                if e == 3:
                    ins.then_inc(l1_used, 1)
                    dve.wait_ge(l1_used, 1)
                elif e < E1 - 1:
                    link(ins)

        def l1_act(act):
            act.wait_ge(l1_combT_ps, 1)
            act_copy(combT[0:E1, :], bank(6)[0:E1, :]).then_inc(l1_combT, 1)

        S2 = float(D) ** -0.5
        wq2 = sb("wq2", [P, D])
        wk2 = sb("wk2", [C, D])
        wv2 = sb("wv2", [C, D])
        bq2 = sb("bq2", [P, 1])
        bk2 = sb("bk2", [P, 1])
        bv2 = sb("bv2", [P, D])
        queryT = sb("queryT", [P, N])
        keyT = place(4096, [P, M])
        value = place(5120, [P, MT, D])
        att = place(0, [P, T, KB])
        attT = place(2048, [P, T, KB]).rearrange("p t (k q) -> p t k q", q=P)
        l2_loaded = sem("l2_loaded")
        l2_kv_ps = sem("l2_kv_ps")
        l2_keyT = sem("l2_keyT")
        l2_value = sem("l2_value")
        l2_query_ps = sem("l2_query_ps")
        l2_query = sem("l2_query")
        att_scores = sem("att_scores")
        att_negmax = sem("att_negmax")
        att_exp = sem("att_exp")
        att_ready = sem("att_ready")
        att_turned = sem("att_turned")
        att_copied = sem("att_copied")
        att_out = sem("att_out")

        def l2_prepare_pe(pe):
            pe.wait_ge(l2_loaded, 16 * 6)
            pe.wait_ge(x_updated, 2 * T)
            for half in range(2):
                nc.tensor.matmul(bank(2 + half), wk2[:], ctxT[:, half * 512:(half + 1) * 512],
                                 start=True, stop=True).then_inc(l2_kv_ps, 1)
            for half in range(2):
                for q in range(4):
                    k = 4 * half + q
                    ins = nc.tensor.matmul(bank(4 + half)[:, q * P:(q + 1) * P], ctxT[:, k * P:(k + 1) * P], wv2[:],
                                           start=True, stop=True)
                ins.then_inc(l2_kv_ps, 1)

        def l2_prepare_act(act):
            act.wait_ge(l2_loaded, 16 * 6)
            for half in range(2):
                act.wait_ge(l2_kv_ps, half + 1)
                nc.scalar.activation(keyT[:, half * 512:(half + 1) * 512], bank(2 + half), ACT.Identity,
                                     bias=bk2[:]).then_inc(l2_keyT, 1)

        def l2_prepare_dve(dve):
            dve.wait_ge(l2_loaded, 16 * 6)
            for half in range(2):
                dve.wait_ge(l2_kv_ps, half + 3)
                nc.vector.tensor_tensor(value[:, 4 * half:4 * half + 4, :], quarters(4 + half),
                                        bv2[:].unsqueeze(1).broadcast_to([P, 4, D]), ALU.add).then_inc(l2_value, 1)

        def att_scores_pe(pe, n, qT, kT, keys):
            for t in range(T):
                b = t // 2
                nc.tensor.matmul(bank(t)[:, 0:keys], qT[:, t * P:(t + 1) * P], kT[:, b * keys:(b + 1) * keys],
                                 start=True, stop=True).then_inc(att_scores, 1)

        def att_turn_pe(pe, n, t, keys, ready, count):
            pe.wait_ge(ready, count + t + 1)
            if T * n + t >= 2:
                pe.wait_ge(att_copied, T * n + t - 1)
            for k in range(keys // P):
                ins = nc.tensor.transpose(bank(4 + t % 2)[:, k * P:(k + 1) * P], att[:, t, k * P:(k + 1) * P], ident[:])
            ins.then_inc(att_turned, 1)

        def att_out_pe(pe, n, t, keys, v):
            pe.wait_ge(att_copied, T * n + t + 1)
            K = keys // P
            for k in range(K):
                ins = nc.tensor.matmul(bank(6)[:, t * P:(t + 1) * P], attT[:, t, k, :], v[:, K * (t // 2) + k, :],
                                       start=(k == 0), stop=(k == K - 1))
            ins.then_inc(att_out, 1)

        def att_max_dve(dve, link, n, t, keys, scale):
            dve.wait_ge(att_scores, T * n + t + 1)
            link(nc.vector.tensor_reduce(row_max[:, t:t + 1], bank(t)[:, 0:keys], X, ALU.max))
            nc.vector.tensor_scalar(neg_max[:, t:t + 1], row_max[:, t:t + 1], -scale, None, ALU.mult).then_inc(att_negmax, 1)

        def att_copy_dve(dve, n, t, keys):
            dve.wait_ge(att_turned, T * n + t + 1)
            nc.vector.tensor_copy(attT[:, t, 0:keys // P, :], bank(4 + t % 2)[:, 0:keys].rearrange("p (k q) -> p k q", q=P)).then_inc(att_copied, 1)

        def att_exp_act(act, n, keys, scale):
            for t in range(T):
                act.wait_ge(att_negmax, T * n + t + 1)
                nc.scalar.activation(att[:, t, 0:keys], bank(t)[:, 0:keys], ACT.Exp, bias=neg_max[:, t:t + 1], scale=scale,
                                     accum_out=row_sum[:, t:t + 1]).then_inc(att_exp, 1)

        def l2_pe(pe):
            pe.wait_ge(ln_xT, 3)
            nc.tensor.matmul(bank(6), wq2[:], xT[:], start=True, stop=True).then_inc(l2_query_ps, 1)
            pe.wait_ge(l2_keyT, 2)
            pe.wait_ge(l2_value, 2)
            pe.wait_ge(l2_query, 1)
            att_scores_pe(pe, 0, queryT, keyT, KB)
            for t in range(T):
                att_turn_pe(pe, 0, t, KB, att_exp, 0)
                if t >= 1:
                    att_out_pe(pe, 0, t - 1, KB, value)
            att_out_pe(pe, 0, T - 1, KB, value)

        def l2_act(act):
            act.wait_ge(l2_query_ps, 1)
            nc.scalar.activation(queryT[:], bank(6), ACT.Identity, bias=bq2[:]).then_inc(l2_query, 1)
            att_exp_act(act, 0, KB, S2)

        def l2_dve(dve, link):
            for t in range(T):
                att_max_dve(dve, link, 0, t, KB, S2)
            for t in range(T):
                att_copy_dve(dve, 0, t, KB)
            link(nc.vector.reciprocal(row_inv[:], row_sum[:]))
            dve.wait_ge(att_out, T)
            for t in range(T):
                nc.vector.scalar_tensor_tensor(out=x[:, t, :], in0=quarters(6)[:, t, :], scalar=row_inv[:, t:t + 1],
                                               in1=x[:, t, :], op0=ALU.mult, op1=ALU.add).then_inc(x_updated, 1)

        E3 = 8
        H3 = 256
        room2 = sb("room2", [P, 8192])
        w1 = room2[:, 0:4096].rearrange("p (e c d) -> p e c d", e=E3, c=4)
        w1T = room2[:, 4096:8192].rearrange("p (e h) -> p e h", e=E3)
        wg3 = sb("wg3", [E3, D])
        wg3T = sb("wg3T", [P, E3])
        wo3 = sb("wo3", [P, H3])
        wo3T = sb("wo3T", [P, 2, D])
        bo3 = sb("bo3", [P, D])
        b1 = sb("b1", [E3, 2 * H3])
        b1_hi = sb("b1_hi", [E3, 2 * H3], BF16)
        b1_mid = sb("b1_mid", [E3, 2 * H3], BF16)
        b1_lo = sb("b1_lo", [E3, 2 * H3], BF16)
        b1_rows = sb("b1_rows", [3, E3, 2 * H3], BF16)
        ones3 = sb("ones3", [3, P], BF16)
        sig = place(4096, [P, T, H3])
        gated = place(5120, [P, T, H3])
        mixed = place(6144, [P, T, H3])
        mixedT = place(7168, [P, 2, N])
        l3_loaded = sem("l3_loaded")
        l3_b1_parts = sem("l3_b1_parts")
        l3_b1_rows = sem("l3_b1_rows")
        l3_w_turned = sem("l3_w_turned")
        l3_w = sem("l3_w")
        l3_logits = sem("l3_logits")
        l3_hidden = sem("l3_hidden")
        l3_sig = sem("l3_sig")
        l3_used = sem("l3_used")
        l3_mixed = sem("l3_mixed")
        l3_turned = sem("l3_turned")
        l3_mixedT = sem("l3_mixedT")
        l3_out = sem("l3_out")

        def l3_parts_dve(dve, link):
            dve.wait_ge(l3_loaded, 16 * 5)
            link(nc.vector.tensor_copy(b1_hi[:], b1[:]))
            link(nc.vector.tensor_tensor(b1[:], b1[:], b1_hi[:], ALU.subtract))
            link(nc.vector.tensor_copy(b1_mid[:], b1[:]))
            link(nc.vector.tensor_tensor(b1[:], b1[:], b1_mid[:], ALU.subtract))
            nc.vector.memset(ones3[:], 1.0)
            nc.vector.tensor_copy(b1_lo[:], b1[:]).then_inc(l3_b1_parts, 1)

        def l3_prepare_pe(pe):
            pe.wait_ge(l3_loaded, 16 * 5)
            pe.wait_ge(x_updated, 3 * T)
            nc.tensor.transpose(bank(4)[:, 0:E3], wg3[:], ident[0:E3, 0:E3])
            for k in range(2):
                ins = nc.tensor.transpose(bank(4)[:, (k + 1) * P:(k + 2) * P], wo3[:, k * P:(k + 1) * P], ident[:])
            ins.then_inc(l3_w_turned, 1)
            for e in range(E3):
                if e >= 4:
                    pe.wait_ge(l3_w, 2 + e - 3)
                for c in range(4):
                    ins = nc.tensor.transpose(bank(e % 4)[:, c * P:(c + 1) * P], w1[:, e, c, :], ident[:])
                ins.then_inc(l3_w_turned, 1)

        def l3_prepare_act(act):
            act.wait_ge(l3_w_turned, 1)
            act_copy(wg3T[:], bank(4)[:, 0:E3]).then_inc(l3_w, 1)
            act_copy(wo3T[:], bank(4)[:, P:3 * P].rearrange("p (k d) -> p k d", k=2)).then_inc(l3_w, 1)
            for e in range(E3):
                act.wait_ge(l3_w_turned, e + 2)
                act_copy(w1T[:, e, :], bank(e % 4)).then_inc(l3_w, 1)

        def l3_pe(pe):
            pe.wait_ge(ln_xT, 4)
            pe.wait_ge(l3_w, 2 + E3)
            for t in range(T):
                ins = nc.tensor.matmul(bank(6)[:, t * E3:(t + 1) * E3], xT[:, t * P:(t + 1) * P], wg3T[:], start=True, stop=True)
            ins.then_inc(l3_logits, 1)
            pe.wait_ge(l3_b1_rows, 16 * 3)
            with pe.Fori(0, E3) as e:
                for t in range(T):
                    pe.wait_ge(l3_used, T * e + (t + 1))
                    nc.tensor.matmul(bank(t), xT[:, t * P:(t + 1) * P], w1T[:, bass.ds(e, 1), :], start=True, stop=False)
                    nc.tensor.matmul(bank(t), ones3[:], b1_rows[:, bass.ds(e, 1), :], start=False, stop=True).then_inc(l3_hidden, 1)
            for k in range(2):
                for t in range(T):
                    pe.wait_ge(l3_mixed, T * E3 + t + 1)
                    ins = nc.tensor.transpose(bank(4 + k)[:, t * P:(t + 1) * P], mixed[:, t, k * P:(k + 1) * P], ident[:])
                ins.then_inc(l3_turned, 1)
            pe.wait_ge(l3_mixedT, 2)
            for t in range(T):
                for k in range(2):
                    ins = nc.tensor.matmul(bank(6)[:, t * P:(t + 1) * P], mixedT[:, k, t * P:(t + 1) * P], wo3T[:, k, :],
                                           start=(k == 0), stop=(k == 1))
            ins.then_inc(l3_out, 1)

        def l3_act(act):
            with act.Fori(0, E3) as e:
                for t in range(T):
                    act.wait_ge(l3_hidden, T * e + (t + 1))
                    nc.scalar.activation(sig[:, t, :], bank(t)[:, H3:2 * H3], ACT.Sigmoid).then_inc(l3_sig, 1)
            for k in range(2):
                act.wait_ge(l3_turned, k + 1)
                act_copy(mixedT[:, k, :], bank(4 + k)).then_inc(l3_mixedT, 1)

        def l3_dve(dve, link):
            dve.sem_inc(l3_used, T)
            for t in range(T):
                nc.vector.memset(mixed[:, t, :], 0.0).then_inc(l3_mixed, 1)
            dve.wait_ge(l3_logits, 1)
            link(nc.vector.tensor_copy(logits[:, :, 0:E3], bank(6)[:, 0:T * E3].rearrange("p (t e) -> p t e", t=T)))
            shift_dve(link, logits, E3)
            dve.wait_ge(gate_exp, 2)
            top2_dve(link, gate, E3)
            weights_dve(link, E3, eps_of_all=1e-9)
            link(nc.vector.tensor_reduce(total[:], comb[:, :, 0:E3], X, ALU.add))
            for t in range(T):
                ins = nc.vector.scalar_tensor_tensor(out=x[:, t, :], in0=bo3[:], scalar=total[:, t:t + 1], in1=x[:, t, :],
                                                     op0=ALU.mult, op1=ALU.add)
            link(ins)
            with dve.Fori(0, E3) as e:
                for t in range(T + 1):
                    if t < T:
                        dve.wait_ge(l3_sig, T * e + (t + 1))
                        nc.vector.tensor_tensor(gated[:, t, :], bank(t)[:, 0:H3], sig[:, t, :], ALU.mult).then_inc(l3_used, 1)
                    if t >= 1:
                        u = t - 1
                        dve.wait_ge(l3_used, T * e + (T + u + 1))
                        dve.wait_ge(l3_mixed, T * e + (u + 1))
                        nc.vector.scalar_tensor_tensor(out=mixed[:, u, :], in0=gated[:, u, :], scalar=comb[:, u, bass.ds(e, 1)],
                                                       in1=mixed[:, u, :], op0=ALU.mult, op1=ALU.add).then_inc(l3_mixed, 1)
            dve.wait_ge(l3_out, 1)
            for t in range(T):
                nc.vector.tensor_tensor(x[:, t, :], x[:, t, :], quarters(6)[:, t, :], ALU.add).then_inc(x_updated, 1)

        S4 = float(D) ** -0.5
        F4 = 512
        D2V, IMG, TXT, ATT0, ATT1, FF1, FF2 = range(7)
        wd4 = sb("wd4", [P, C])
        wi4 = sb("wi4", [P, D])
        wt4 = sb("wt4", [P, D])
        wa4 = sb("wa4", [64, 2, D])
        wf14 = sb("wf14", [P, 4, 2 * D])
        wf24 = sb("wf24", [P, F4])
        bd4 = sb("bd4", [P, 1])
        bi4 = sb("bi4", [P, 1])
        bt4 = sb("bt4", [P, 1])
        ba4 = sb("ba4", [P, 2])
        ba4_rows = sb("ba4_rows", [P, 2, 64])
        bf14 = sb("bf14", [P, 4])
        bf24 = sb("bf24", [P, D])
        below = place(9216, [P, 4 * 2 * D])
        td4 = sb("td4", [P, C], BF16)
        ti4 = sb("ti4", [P, D], BF16)
        tt4 = sb("tt4", [P, D], BF16)
        ta4 = sb("ta4", [64, 2, D], BF16)
        tf14 = sb("tf14", [P, 4, 2 * D], BF16)
        tf24 = sb("tf24", [P, F4], BF16)
        tdT = sb("tdT", [C, D], BF16)
        tiT = sb("tiT", [P, D], BF16)
        ttT = sb("ttT", [P, D], BF16)
        taT = sb("taT", [P, 2, 2, 64], BF16)
        tf1T = sb("tf1T", [P, 2, F4], BF16)
        tf2T = sb("tf2T", [P, 4, D], BF16)
        abs_sum = sb("abs_sum", [P, 7])
        one_over = sb("one_over", [P, 7])
        ones = sb("ones", [P, P])
        w_scale = sb("w_scale", [P, 7])
        w_above = sb("w_above", [P, 7])
        w_below = sb("w_below", [P, 7])
        part_max = sb("part_max", [P, 8])
        whole_max = sb("whole_max", [P, 8])
        i_scale = sb("i_scale", [P, 8])
        i_inv = sb("i_inv", [P, 8])
        both = sb("both", [P, 8])
        rounded = place(4096, [P, 4 * N])
        ints = sb("ints", [P, 4 * N], BF16)
        ctx_feat = place(8192, [P, M])
        key4 = room2[:, 0:2048].rearrange("p (l k) -> p l k", l=2)
        value4 = room2[:, 2048:4096].rearrange("p (l k d) -> p l k d", l=2, d=D)
        cat = sb("cat", [P, N + B])
        hid4 = place(6144, [P, 4, N])
        l4_loaded = sem("l4_loaded")
        l4_ba = sem("l4_ba")
        l4_const = sem("l4_const")
        l4_sums = sem("l4_sums")
        l4_sums_ps = sem("l4_sums_ps")
        l4_ternary = sem("l4_ternary")
        l4_w_turned = sem("l4_w_turned")
        l4_wT = sem("l4_wT")
        l4_part_max = sem("l4_part_max")
        l4_whole_max = sem("l4_whole_max")
        l4_ints = sem("l4_ints")
        l4_both = sem("l4_both")
        l4_ps = sem("l4_ps")
        l4_feat = sem("l4_feat")
        l4_value = sem("l4_value")
        l4_fused = sem("l4_fused")

        def l4_const_pool():
            for j, size in ((D2V, D * C), (IMG, D * D), (TXT, D * D), (ATT0, 64 * D), (ATT1, 64 * D), (FF1, F4 * 2 * D), (FF2, D * F4)):
                nc.gpsimd.memset(one_over[:, j:j + 1], 1.0 / size)
            nc.gpsimd.memset(abs_sum[:], 0.0)
            nc.gpsimd.memset(part_max[:], 0.0)
            nc.gpsimd.memset(ones[:], 1.0).then_inc(l4_const, 1)

        WEIGHTS4 = ((wd4, td4, D2V, P), (wi4, ti4, IMG, P), (wt4, tt4, TXT, P), (wf14, tf14, FF1, P), (wf24, tf24, FF2, P))

        def l4_ternary_dve(dve, link):
            dve.wait_ge(l4_loaded, 16 * 17)
            dve.wait_ge(l4_const, 1)
            for w, _, j, rows in WEIGHTS4:
                axis = mybir.AxisListType.XY if w is wf14 else X
                nc.vector.tensor_reduce(abs_sum[:, j:j + 1], w[:], axis, ALU.add, apply_absolute_value=True)
            nc.vector.tensor_reduce(abs_sum[0:64, ATT0:ATT1 + 1], wa4[:], X, ALU.add, apply_absolute_value=True).then_inc(l4_sums, 1)
            dve.wait_ge(l4_sums_ps, 1)
            link(nc.vector.tensor_tensor(w_scale[:], bank(6)[:, 0:7], one_over[:], ALU.mult))
            link(nc.vector.tensor_scalar(w_scale[:], w_scale[:], 1e-5, None, ALU.max))
            nc.vector.tensor_scalar(w_above[:], w_scale[:], 0.5, None, ALU.mult)
            link(nc.vector.tensor_scalar(w_below[:], w_scale[:], -0.5, None, ALU.mult))

            def ternary(w, q, j, rows, size):
                link(nc.vector.tensor_scalar(below[0:rows, 0:size], w, w_below[0:rows, j:j + 1], None, ALU.is_lt))
                return link(nc.vector.scalar_tensor_tensor(out=q, in0=w, scalar=w_above[0:rows, j:j + 1], in1=below[0:rows, 0:size],
                                                           op0=ALU.is_gt, op1=ALU.subtract))

            ternary(wd4[:], td4[:], D2V, P, C)
            ternary(wi4[:], ti4[:], IMG, P, D)
            ternary(wt4[:], tt4[:], TXT, P, D)
            ternary(wa4[:, 0, :], ta4[:, 0, :], ATT0, 64, D)
            ternary(wa4[:, 1, :], ta4[:, 1, :], ATT1, 64, D)
            ternary(wf14[:].rearrange("p c i -> p (c i)"), tf14[:].rearrange("p c i -> p (c i)"), FF1, P, 4 * 2 * D)
            ternary(wf24[:], tf24[:], FF2, P, F4)
            dve.sem_inc(l4_ternary, 1)

        def l4_ternary_pe(pe):
            pe.wait_ge(l4_sums, 1)
            pe.wait_ge(x_updated, 4 * T)
            nc.tensor.matmul(bank(6)[:, 0:7], ones[:], abs_sum[:], start=True, stop=True).then_inc(l4_sums_ps, 1)
            pe.wait_ge(l4_ternary, 1)
            b0, b1_, b2 = (bank(n).bitcast(BF16) for n in range(3))
            nc.tensor.transpose(b0[0:C, 0:P], td4[:], identb[:])
            nc.tensor.transpose(b0[:, P:2 * P], ti4[:], identb[:])
            nc.tensor.transpose(b0[:, 2 * P:3 * P], tt4[:], identb[:])
            for l in range(2):
                nc.tensor.transpose(b0[:, 3 * P + 64 * l:3 * P + 64 * (l + 1)], ta4[:, l, :], identb[0:64, 0:64])
            for half in range(2):
                for c in range(4):
                    nc.tensor.transpose(b1_[:, (4 * half + c) * P:(4 * half + c + 1) * P], tf14[:, c, half * P:(half + 1) * P], identb[:])
            for c in range(4):
                ins = nc.tensor.transpose(b2[:, c * P:(c + 1) * P], tf24[:, c * P:(c + 1) * P], identb[:])
            ins.then_inc(l4_w_turned, 1)

        def l4_ternary_act(act):
            act.wait_ge(l4_w_turned, 1)
            b0, b1_, b2 = (bank(n).bitcast(BF16) for n in range(3))
            act_copy(tdT[:], b0[0:C, 0:P])
            act_copy(tiT[:], b0[:, P:2 * P])
            act_copy(ttT[:], b0[:, 2 * P:3 * P])
            for copy in range(2):
                act_copy(taT[:, :, copy, :], b0[:, 3 * P:4 * P].rearrange("p (l o) -> p l o", l=2))
            act_copy(tf1T[:], b1_.rearrange("p (h f) -> p h f", h=2))
            act_copy(tf2T[:], b2[:, 0:4 * P].rearrange("p (c o) -> p c o", c=4)).then_inc(l4_wT, 1)

        def scale_dve(dve, link, n, weight):
            dve.wait_ge(l4_whole_max, n + 1)
            link(nc.vector.tensor_scalar(i_scale[:, n:n + 1], whole_max[:, n:n + 1], 1e-8, 1.0 / 127.0, ALU.max, ALU.mult))
            link(nc.vector.reciprocal(i_inv[:, n:n + 1], i_scale[:, n:n + 1]))
            nc.vector.tensor_tensor(both[:, n:n + 1], i_scale[:, n:n + 1], w_scale[:, weight:weight + 1], ALU.mult).then_inc(l4_both, 1)

        def ints_dve(link, n, src, size, rows=P):
            link(nc.vector.tensor_scalar(rounded[0:rows, 0:size], src, i_inv[0:rows, n:n + 1], ROUND, ALU.mult, ALU.add))
            link(nc.vector.tensor_scalar(rounded[0:rows, 0:size], rounded[0:rows, 0:size], ROUND + 127.0, ROUND - 128.0, ALU.min, ALU.max))
            nc.vector.tensor_scalar(ints[0:rows, 0:size], rounded[0:rows, 0:size], ROUND, None, ALU.subtract).then_inc(l4_ints, 1)

        def abs_max_dve(n, src, rows=P, axis=X):
            nc.vector.tensor_reduce(part_max[0:rows, n:n + 1], src, axis, ALU.max, apply_absolute_value=True).then_inc(l4_part_max, 1)

        def whole_max_pool(pool, n):
            pool.wait_ge(l4_part_max, n + 1)
            nc.gpsimd.partition_all_reduce(whole_max[:, n:n + 1], part_max[:, n:n + 1], P, RMAX).then_inc(l4_whole_max, 1)

        def l4_ctx_dve(dve, link):
            abs_max_dve(0, ctxT[:], rows=C)
            scale_dve(dve, link, 0, D2V)
            ints_dve(link, 0, ctxT[:], M, rows=C)
            dve.wait_ge(l4_feat, 1)
            abs_max_dve(1, ctx_feat[:])
            scale_dve(dve, link, 1, IMG)
            ints_dve(link, 1, ctx_feat[:], M)
            dve.wait_ge(l4_feat, 2)
            abs_max_dve(2, ctx_feat[:])
            link(nc.vector.tensor_reduce(cat[:, N:N + B], ctx_feat[:].rearrange("p (b k) -> p b k", b=B), X, ALU.add))
            link(nc.vector.tensor_scalar(cat[:, N:N + B], cat[:, N:N + B], 1.0 / KB, None, ALU.mult))
            scale_dve(dve, link, 2, ATT0)
            nc.vector.tensor_tensor(both[:, 6:7], i_scale[:, 2:3], w_scale[:, ATT1:ATT1 + 1], ALU.mult).then_inc(l4_both, 1)
            ints_dve(link, 2, ctx_feat[:], M)
            for l in range(2):
                dve.wait_ge(l4_ps, 5 + l)
                for copy in range(2):
                    nc.vector.scalar_tensor_tensor(
                        out=value4[:, l, :, 64 * copy:64 * (copy + 1)], in0=bank(4 + l).rearrange("p (k o) -> p k o", k=MT),
                        scalar=both[:, (2, 6)[l]:(2, 6)[l] + 1],
                        in1=ba4_rows[:, l, :].unsqueeze(1).broadcast_to([P, MT, 64]), op0=ALU.mult, op1=ALU.add).then_inc(l4_value, 1)

        def l4_ctx_pe(pe):
            pe.wait_ge(l4_wT, 1)
            for n, w in ((0, tdT), (1, tiT)):
                pe.wait_ge(l4_ints, n + 1)
                rows = C if n == 0 else P
                for half in range(2):
                    ins = nc.tensor.matmul(bank(half), w[:], ints[0:rows, half * 512:(half + 1) * 512], start=True, stop=True)
                ins.then_inc(l4_ps, 1)
            pe.wait_ge(l4_ints, 3)
            for l in range(2):
                for half in range(2):
                    ins = nc.tensor.matmul(bank(2 * l + half), taT[:, l, :, :], ints[:, half * 512:(half + 1) * 512], start=True, stop=True)
                ins.then_inc(l4_ps, 1)
            for l in range(2):
                for k in range(MT):
                    ins = nc.tensor.matmul(bank(4 + l)[:, k * 64:(k + 1) * 64], ints[:, k * P:(k + 1) * P], taT[:, l, 0, :], start=True, stop=True)
                ins.then_inc(l4_ps, 1)

        def l4_ctx_act(act):
            for n, b in ((0, bd4), (1, bi4)):
                act.wait_ge(l4_ps, n + 1)
                act.wait_ge(l4_both, n + 1)
                nc.scalar.activation(ctx_feat[:].rearrange("p (b k) -> p b k", b=2), PS[:, 0:2, :], ACT.Identity,
                                     bias=b[:], scale=both[:, n:n + 1]).then_inc(l4_feat, 1)
            act.wait_ge(l4_both, 4)
            act.wait_ge(l4_ba, 16 * 4)
            for l in range(2):
                act.wait_ge(l4_ps, 3 + l)
                nc.scalar.activation(key4[:, l, :].rearrange("p (b k) -> p b k", b=2), PS[:, 2 * l:2 * l + 2, :], ACT.Identity,
                                     bias=ba4[:, l:l + 1], scale=both[:, (2, 6)[l]:(2, 6)[l] + 1]).then_inc(l4_feat, 1)

        def l4_dve(dve, link):
            dve.wait_ge(ln_xT, 5)
            abs_max_dve(3, xT[:])
            scale_dve(dve, link, 3, TXT)
            dve.wait_ge(l4_ps, 6)
            ints_dve(link, 3, xT[:], N)
            for l in range(2):
                n = l + 1
                for t in range(T):
                    att_max_dve(dve, link, n, t, KB, S4)
                for t in range(T):
                    dve.wait_ge(att_exp, T * n + t + 1)
                    link(nc.vector.reciprocal(row_inv[:, t:t + 1], row_sum[:, t:t + 1]))
                    nc.vector.tensor_scalar(att[:, t, :], att[:, t, :], row_inv[:, t:t + 1], 0.1, ALU.mult, ALU.mult).then_inc(att_ready, 1)
                for t in range(T):
                    att_copy_dve(dve, n, t, KB)
                dve.wait_ge(att_out, T * (n + 1))
                nc.vector.tensor_tensor(cat[:, 0:N], cat[:, 0:N], bank(6), ALU.add).then_inc(l4_fused, 1)
            dve.wait_ge(l4_fused, 2)
            abs_max_dve(4, cat[:])
            scale_dve(dve, link, 4, FF1)
            ints_dve(link, 4, cat[:], N + B)
            dve.wait_ge(l4_feat, 9)
            abs_max_dve(5, hid4[:], axis=mybir.AxisListType.XY)
            link(nc.vector.tensor_tensor(x[:], x[:], bf24[:].unsqueeze(1).broadcast_to([P, T, D]), ALU.add))
            scale_dve(dve, link, 5, FF2)
            ints_dve(link, 5, hid4[:].rearrange("p c n -> p (c n)"), 4 * N)
            dve.wait_ge(l4_both, 7)
            dve.wait_ge(l4_ps, 12)
            for t in range(T):
                nc.vector.scalar_tensor_tensor(out=x[:, t, :], in0=quarters(7)[:, t, :], scalar=both[:, 5:6], in1=x[:, t, :],
                                               op0=ALU.mult, op1=ALU.add).then_inc(x_updated, 1)

        def l4_pe(pe):
            pe.wait_ge(l4_ints, 4)
            nc.tensor.matmul(bank(7), ttT[:], ints[:, 0:N], start=True, stop=True).then_inc(l4_ps, 1)
            for l in range(2):
                n = l + 1
                if l == 0:
                    pe.wait_ge(l4_feat, 5)
                    pe.wait_ge(l4_value, 4)
                else:
                    pe.wait_ge(l4_fused, 1)
                att_scores_pe(pe, n, cat, key4[:, l, :], KB)
                for t in range(T):
                    att_turn_pe(pe, n, t, KB, att_ready, T * l)
                    if t >= 1:
                        l4_attended_pe(pe, n, l, t - 1)
                l4_attended_pe(pe, n, l, T - 1)
            pe.wait_ge(l4_ints, 5)
            for c in range(4):
                nc.tensor.matmul(bank(c), tf1T[:, 0, c * P:(c + 1) * P], ints[:, 0:N], start=True, stop=False)
                nc.tensor.matmul(bank(c), tf1T[:, 1, c * P:(c + 1) * P], wide(ints[:, N:N + B], N // B),
                                 start=False, stop=True).then_inc(l4_ps, 1)
            pe.wait_ge(l4_ints, 6)
            for t in range(T):
                for c in range(4):
                    ins = nc.tensor.matmul(bank(7)[:, t * P:(t + 1) * P], ints[:, c * N + t * P:c * N + (t + 1) * P], tf2T[:, c, :],
                                           start=(c == 0), stop=(c == 3))
            ins.then_inc(l4_ps, 1)

        def l4_attended_pe(pe, n, l, t):
            pe.wait_ge(att_copied, T * n + t + 1)
            K = KB // P
            for k in range(K):
                ins = nc.tensor.matmul(bank(6)[:, t * P:(t + 1) * P], value4[:, l, K * (t // 2) + k, :], attT[:, t, k, :],
                                       start=(k == 0), stop=(k == K - 1))
            ins.then_inc(att_out, 1)

        def l4_act(act):
            act.wait_ge(l4_ps, 7)
            act.wait_ge(l4_both, 5)
            nc.scalar.activation(cat[:, 0:N], bank(7), ACT.Identity, bias=bt4[:], scale=both[:, 3:4]).then_inc(l4_feat, 1)
            for l in range(2):
                att_exp_act(act, l + 1, KB, S4)
            act.wait_ge(l4_both, 6)
            for c in range(4):
                act.wait_ge(l4_ps, 8 + c)
                nc.scalar.activation(hid4[:, c, :], bank(c), ACT.Relu, bias=bf14[:, c:c + 1], scale=both[:, 4:5]).then_inc(l4_feat, 1)

        E5 = 16
        K5 = N // B
        S5 = float(D) ** -0.5
        proj5 = place_weights(0, [P, E5, 3 * D])
        oproj5 = place_weights(6144, [P, E5, D])
        sim5 = sb("sim5", [P, E5])
        squares5 = sb("squares5", [P, E5])
        norm5 = sb("norm5", [P, E5])
        gates5 = sb("gates5", [P, E5])
        xnorm5 = sb("xnorm5", [P, T])
        idle5 = sb("idle5", [P, T])
        parts5 = sb("parts5", [P, T, 3 * E5], BF16)
        comb5T = sb("comb5T", [P, N], BF16)
        pick5 = sb("pick5", [P, E5, P], BF16)
        scaled = place(4096, [P, 2, N])
        qkv5 = place(5120, [P, T, 3 * D])
        key5T = place(6656, [P, N])
        o5 = place(7168, [P, T, D])
        o5T = place(7680, [P, N])
        junk5 = place(8192, [P, T, D])
        l5_loaded = sem("l5_loaded")
        l5_pick = sem("l5_pick")
        l5_squares = sem("l5_squares")
        l5_norm_ps = sem("l5_norm_ps")
        l5_norm2 = sem("l5_norm2")
        l5_norm = sem("l5_norm")
        l5_gate = sem("l5_gate")
        l5_xsum = sem("l5_xsum")
        l5_xnorm = sem("l5_xnorm")
        l5_sim = sem("l5_sim")
        l5_logits = sem("l5_logits")
        l5_parts = sem("l5_parts")
        l5_parts_ps = sem("l5_parts_ps")
        l5_combT = sem("l5_combT")
        l5_weight = [sem("l5_weight"), sem("l5_weight_o")]
        l5_scaled = [sem("l5_scaled"), sem("l5_scaled_o")]
        l5_used = [sem("l5_used"), sem("l5_used_o")]
        l5_qkv = sem("l5_qkv")
        l5_qk_turned = sem("l5_qk_turned")
        l5_qk = sem("l5_qk")
        l5_o = sem("l5_o")
        l5_o_turned = sem("l5_o_turned")
        l5_oT = sem("l5_oT")

        def l5_const_pool(pool, link):
            link(nc.gpsimd.memset(pick5[:], 0.0))
            for k in range(3):
                link(nc.gpsimd.affine_select(out=pick5[:], in_=pick5[:], compare_op=ALU.not_equal, fill=1.0, base=-E5 * k,
                                             pattern=[[-1, E5], [0, P]], channel_multiplier=1))
            nc.gpsimd.memset(comb5T[:], 0.0).then_inc(l5_pick, 1)

        def l5_sim_dve(dve, link):
            dve.wait_ge(l5_loaded, 16 * 6)
            nc.vector.tensor_tensor(squares5[:], sim5[:], sim5[:], ALU.mult).then_inc(l5_squares, 1)
            dve.wait_ge(l5_norm_ps, 1)
            nc.vector.tensor_scalar(norm5[:], bank(5)[:, 0:E5], 1e-24, None, ALU.max).then_inc(l5_norm2, 1)
            dve.wait_ge(l5_gate, 1)
            link(nc.vector.tensor_scalar(gates5[:], gates5[:], 1.0, None, ALU.add))
            link(nc.vector.reciprocal(gates5[:], gates5[:]))
            dve.wait_ge(l5_norm, 1)
            nc.vector.tensor_tensor(sim5[:], sim5[:], norm5[:], ALU.mult).then_inc(l5_sim, 1)

        def l5_sim_pe(pe):
            pe.wait_ge(l5_squares, 1)
            pe.wait_ge(x_updated, 5 * T)
            nc.tensor.matmul(bank(5)[:, 0:E5], ones[:], squares5[:], start=True, stop=True).then_inc(l5_norm_ps, 1)

        def l5_sim_act(act):
            act.wait_ge(l5_loaded, 16 * 6)
            nc.scalar.activation(gates5[:], gates5[:], ACT.Exp, scale=-1.0).then_inc(l5_gate, 1)

        def l5_norm_pool(pool):
            pool.wait_ge(l5_norm2, 1)
            nc.gpsimd.tensor_tensor(norm5[:], norm5[:], minus_half[:], ALU.pow).then_inc(l5_norm, 1)

        def l5_xnorm_pool(pool):
            pool.wait_ge(l5_xsum, 1)
            nc.gpsimd.tensor_tensor(xnorm5[:], xnorm5[:], minus_half[:, 0:T], ALU.pow).then_inc(l5_xnorm, 1)

        def l5_router_dve(dve, link):
            dve.wait_ge(ln_rows, 6 * T)
            link(nc.vector.tensor_tensor(junk5[:], xn[:], xn[:], ALU.mult))
            link(nc.vector.tensor_reduce(xnorm5[:], junk5[:], X, ALU.add))
            nc.vector.tensor_scalar(xnorm5[:], xnorm5[:], 1e-24, None, ALU.max).then_inc(l5_xsum, 1)
            dve.wait_ge(l5_logits, 1)
            dve.wait_ge(l5_xnorm, 1)
            link(nc.vector.tensor_tensor(logits[:], bank(6)[:, 0:T * E5].rearrange("p (t e) -> p t e", t=T), wide(xnorm5[:], E5), ALU.mult))
            link(nc.vector.tensor_tensor(logits[:], logits[:], gates5[:].unsqueeze(1).broadcast_to([P, T, E5]), ALU.subtract))
            top2_dve(link, logits, E5)
            link(nc.vector.tensor_scalar(logits[:], logits[:], 0.0, None, ALU.max))
            shift_dve(link, logits, E5)
            link(nc.vector.tensor_scalar(equal[:], logits[:], 0.0, None, ALU.is_gt))
            link(nc.vector.tensor_reduce(total2[:], equal[:], X, ALU.add))
            link(nc.vector.tensor_scalar(idle5[:], total2[:], 0.0, None, ALU.is_equal))
            link(nc.vector.tensor_tensor(chosen[:], chosen[:], wide(idle5[:], E5), ALU.mult))
            link(nc.vector.tensor_tensor(chosen[:], chosen[:], equal[:], ALU.add))
            dve.wait_ge(gate_exp, 3)
            weights_dve(link, E5)
            for k in range(3):
                part = parts5[:, :, k * E5:(k + 1) * E5]
                link(nc.vector.tensor_copy(part, comb[:]))
                if k < 2:
                    link(nc.vector.tensor_tensor(comb[:], comb[:], part, ALU.subtract))
            dve.sem_inc(l5_parts, 1)
            dve.wait_ge(l5_parts_ps, 1)
            dve.wait_ge(l5_pick, 1)
            nc.vector.tensor_copy(comb5T[0:3 * E5, :], bank(5).bitcast(BF16)[0:3 * E5, 0:N]).then_inc(l5_combT, 1)

        def l5_router_pe(pe):
            pe.wait_ge(ln_xT, 6)
            pe.wait_ge(l5_sim, 1)
            for t in range(T):
                ins = nc.tensor.matmul(bank(6)[:, t * E5:(t + 1) * E5], xT[:, t * P:(t + 1) * P], sim5[:], start=True, stop=True)
            ins.then_inc(l5_logits, 1)
            l6_prepare_pe(pe)
            pe.wait_ge(l5_parts, 1)
            for t in range(T):
                ins = nc.tensor.transpose(bank(5).bitcast(BF16)[0:3 * E5, t * P:(t + 1) * P], parts5[:, t, :], identb[:])
            ins.then_inc(l5_parts_ps, 1)

        def l5_weight_pe(pe, phase, e, static, slot):
            pe.wait_ge(l5_scaled[phase], e + 1)
            nc.tensor.matmul(bank(4 + slot), pick5[:, e, :] if static else pick5[:, bass.ds(e, 1), :], comb5T[:],
                             start=True, stop=True).then_inc(l5_weight[phase], 1)

        def l5_expert_pe(pe, phase, e, static, slot, first, last):
            if not last:
                l5_weight_pe(pe, phase, e + 1, static, 1 - slot)
            pe.wait_ge(l5_scaled[phase], e + 3)
            width, w = ((3 * D, proj5), (D, oproj5))[phase]
            for t in range(T):
                ins = nc.tensor.matmul(bank(t)[:, 0:width], scaled[:, slot, t * P:(t + 1) * P],
                                       w[:, e, :] if static else w[:, bass.ds(e, 1), :], start=first, stop=last)
            ins.then_inc(l5_used[phase], 1)

        def l5_sum_pe(pe, phase):
            l5_weight_pe(pe, phase, 0, True, 0)
            for e in range(2):
                l5_expert_pe(pe, phase, e, True, e, e == 0, False)
            with pe.Fori(1, E5 // 2 - 1) as pair:
                for k in range(2):
                    l5_expert_pe(pe, phase, 2 * pair + k, False, k, False, False)
            for e in range(E5 - 2, E5):
                l5_expert_pe(pe, phase, e, True, e % 2, False, e == E5 - 1)

        def l5_sum_dve(dve, phase, source):
            dve.sem_inc(l5_scaled[phase], 2)
            with dve.Fori(0, E5 // 2) as pair:
                for k in range(2):
                    dve.wait_ge(l5_weight[phase], 2 * pair + (k + 1))
                    dve.wait_ge(l5_used[phase], 2 * pair + (k + 1))
                    nc.vector.tensor_tensor(scaled[:, k, :], source[:], bank(4 + k), ALU.mult).then_inc(l5_scaled[phase], 1)

        def l5_pe(pe):
            pe.wait_ge(l5_combT, 1)
            pe.wait_ge(l6_v_raw, 2)
            pe.sem_inc(l5_used[0], 2)
            l5_sum_pe(pe, 0)
            pe.wait_ge(l5_qkv, 4)
            for k in range(2):
                for t in range(T):
                    ins = nc.tensor.transpose(bank(4 + k)[:, t * P:(t + 1) * P], qkv5[:, t, k * D:(k + 1) * D], ident[:])
                ins.then_inc(l5_qk_turned, 1)
            pe.wait_ge(l5_qk, 2)
            att_scores_pe(pe, 3, queryT, key5T, K5)
            for t in range(T):
                att_turn_pe(pe, 3, t, K5, att_exp, 3 * T)
                if t >= 1:
                    att_out_pe(pe, 3, t - 1, K5, qkv5[:, :, 2 * D:3 * D])
            att_out_pe(pe, 3, T - 1, K5, qkv5[:, :, 2 * D:3 * D])
            pe.wait_ge(l5_o, T)
            for t in range(T):
                ins = nc.tensor.transpose(bank(7)[:, t * P:(t + 1) * P], o5[:, t, :], ident[:])
            ins.then_inc(l5_o_turned, 1)
            pe.wait_ge(l5_oT, 1)
            pe.sem_inc(l5_used[1], 2)
            l5_sum_pe(pe, 1)

        def l5_act(act):
            act.wait_ge(l5_used[0], E5 + 2)
            for t in (1, 3):
                act_copy(qkv5[:, t, :], bank(t)[:, 0:3 * D]).then_inc(l5_qkv, 1)
            act.wait_ge(l5_qk_turned, 2)
            act_copy(key5T[:], bank(5)).then_inc(l5_qk, 1)
            att_exp_act(act, 3, K5, S5)
            act.wait_ge(l5_o_turned, 1)
            act_copy(o5T[:], bank(7)).then_inc(l5_oT, 1)

        def l5_dve(dve, link):
            l5_sum_dve(dve, 0, xT)
            dve.wait_ge(l5_used[0], E5 + 2)
            for t in (0, 2):
                nc.vector.tensor_copy(qkv5[:, t, :], bank(t)[:, 0:3 * D]).then_inc(l5_qkv, 1)
            dve.wait_ge(l5_qk_turned, 1)
            nc.vector.tensor_copy(queryT[:], bank(4)).then_inc(l5_qk, 1)
            for t in range(T):
                att_max_dve(dve, link, 3, t, K5, S5)
            for t in range(T):
                att_copy_dve(dve, 3, t, K5)
            dve.wait_ge(att_exp, 4 * T)
            link(nc.vector.reciprocal(row_inv[:], row_sum[:]))
            for t in range(T):
                dve.wait_ge(att_out, 4 * T)
                nc.vector.tensor_scalar(o5[:, t, :], quarters(6)[:, t, :], row_inv[:, t:t + 1], None, ALU.mult).then_inc(l5_o, 1)
            dve.wait_ge(l5_oT, 1)
            l5_sum_dve(dve, 1, o5T)
            dve.wait_ge(l5_used[1], E5 + 2)
            for t in range(T):
                nc.vector.tensor_tensor(x[:, t, :], x[:, t, :], bank(t)[:, 0:D], ALU.add).then_inc(x_updated, 1)

        H6 = 16
        J6 = D // H6
        KT6 = MT // B
        R6 = 9 * J6
        S6 = float(J6) ** -0.5
        wq6 = sb("wq6", [P, D])
        wkv6 = sb("wkv6", [P, 2, C])
        wo6 = sb("wo6", [P, D])
        bq6 = sb("bq6", [P, 1])
        bk6 = sb("bk6", [P, 1])
        bkv6 = sb("bkv6", [P, 2 * D])
        bo6 = sb("bo6", [P, D])
        wq6T = sb("wq6T", [P, D])
        wk6T = sb("wk6T", [C, D])
        wv6T = sb("wv6T", [C, D])
        wo6T = sb("wo6T", [P, D])
        value6 = sb("value6", [P, MT, H6, J6])
        value_head = sb("value_head", [P, MT, 2 * J6])
        max6 = sb("max6", [P, T])
        rest6 = sb("rest6", [P, T])
        max_parts = sb("max_parts", [P, T, 3], BF16)
        max_rows = sb("max_rows", [3, N], BF16)
        key6 = place(9216, [P, M])
        k6_parts = room[:, 10240:11776].bitcast(BF16).rearrange("p (a n) -> p a n", a=3)
        key6_stack = room2[0:R6 + 3, :].bitcast(BF16).rearrange("p (h n) -> p h n", h=H6)
        query6_stack = room[0:R6 + 3, 8192:12288].bitcast(BF16).rearrange("p (h n) -> p h n", h=H6)
        o6_rows = room[0:2 * J6, 0:8192].rearrange("p (h n) -> p h n", h=H6)
        probs6 = place_weights(3072, [P, 2, M])
        query6 = place_weights(5120, [P, N])
        q6_parts = weight_room[:, 5632:6400].bitcast(BF16).rearrange("p (a n) -> p a n", a=3)
        o6_stack = room2[:, 0:512]
        sum6_stack = room2[:, 512:1024]
        inv6 = room2[:, 1024:1536]
        o6T = room2[:, 1536:2048]
        l6_loaded = sem("l6_loaded")
        l6_wo_order = sem("l6_wo_order")
        l6_w_turned = sem("l6_w_turned")
        l6_w = sem("l6_w")
        l6_k_ps = sem("l6_k_ps")
        l6_key = sem("l6_key")
        l6_k_parts = sem("l6_k_parts")
        l6_k_stack = sem("l6_k_stack")
        l6_v_ps = sem("l6_v_ps")
        l6_v_raw = sem("l6_v_raw")
        l6_value = sem("l6_value")
        l6_q_ps = sem("l6_q_ps")
        l6_query = sem("l6_query")
        l6_q_parts = sem("l6_q_parts")
        l6_q_stack = sem("l6_q_stack")
        l6_row_scores = sem("l6_row_scores")
        l6_max = sem("l6_max")
        l6_max_parts = sem("l6_max_parts")
        l6_max_turned = sem("l6_max_turned")
        l6_max_rows = sem("l6_max_rows")
        l6_max_stack = sem("l6_max_stack")
        l6_scores = sem("l6_scores")
        l6_probs = sem("l6_probs")
        l6_value_head = sem("l6_value_head")
        l6_o_ps = sem("l6_o_ps")
        l6_o_rows = sem("l6_o_rows")
        l6_o_stack = sem("l6_o_stack")
        l6_oT = sem("l6_oT")
        l6_y = sem("l6_y")

        def l6_prepare_pe(pe):
            pe.wait_ge(l6_loaded, 16 * 7)
            nc.tensor.transpose(bank(0)[:, 0:P], wq6[:], ident[:])
            pe.wait_ge(l6_wo_order, 1)
            nc.tensor.transpose(bank(0)[:, P:2 * P], wo6T[:], ident[:])
            for k in range(2):
                ins = nc.tensor.transpose(bank(0)[0:C, (2 + k) * P:(3 + k) * P], wkv6[:, k, :], ident[:])
            ins.then_inc(l6_w_turned, 1)
            pe.wait_ge(l6_w, 4)
            for half in range(2):
                ins = nc.tensor.matmul(bank(1 + half), wk6T[:], ctxT[:, half * 512:(half + 1) * 512], start=True, stop=True)
            ins.then_inc(l6_k_ps, 1)
            for half in range(2):
                for q in range(4):
                    k = 4 * half + q
                    ins = nc.tensor.matmul(bank(3 + half)[:, q * P:(q + 1) * P], ctxT[:, k * P:(k + 1) * P], wv6T[:], start=True, stop=True)
            ins.then_inc(l6_v_ps, 1)

        def l6_prepare_act(act):
            act.wait_ge(l6_w_turned, 1)
            b0 = bank(0)
            act_copy(wq6T[:].rearrange("p (j h) -> p j h", j=J6), b0[:, 0:P].rearrange("p (h j) -> p j h", j=J6)).then_inc(l6_w, 1)
            act_copy(wo6T[:], b0[:, P:2 * P]).then_inc(l6_w, 1)
            kv = b0[0:C, 2 * P:4 * P].rearrange("p (h s j) -> p s j h", s=2, j=J6)
            act_copy(wk6T[:].rearrange("p (j h) -> p j h", j=J6), kv[:, 0]).then_inc(l6_w, 1)
            act_copy(wv6T[:].rearrange("p (h j) -> p j h", j=J6), kv[:, 1]).then_inc(l6_w, 1)
            act.wait_ge(l6_k_ps, 1)
            act.wait_ge(l6_loaded, 16 * 7)
            nc.scalar.activation(key6.rearrange("p (b n) -> p b n", b=2), PS[:, 1:3, :], ACT.Identity, bias=bk6[:]).then_inc(l6_key, 1)
            act.wait_ge(l6_v_ps, 1)
            for half in range(2):
                act_copy(value6[:, 4 * half:4 * half + 4, :, :],
                         bank(3 + half).rearrange("p (k h j) -> p k h j", k=4, j=J6)).then_inc(l6_v_raw, 1)

        def split_parts(engine, link, parts, whole, done):
            for a in range(3):
                ins = engine.tensor_copy(parts[:, a, :], whole)
                if a < 2:
                    link(ins)
                    link(engine.tensor_tensor(whole, whole, parts[:, a, :], ALU.subtract))
            ins.then_inc(done, 1)

        def l6_prepare_pool(pool, link):
            pool.wait_ge(l6_loaded, 16 * 7)
            nc.gpsimd.tensor_copy(wo6T[:].rearrange("p (j h) -> p j h", j=J6),
                                  wo6[:].rearrange("p (h j) -> p j h", j=J6)).then_inc(l6_wo_order, 1)
            pool.wait_ge(l6_key, 1)
            split_parts(nc.gpsimd, link, k6_parts, key6, l6_k_parts)
            pool.wait_ge(l6_v_raw, 2)
            bv = bkv6[:].rearrange("p (h s j) -> p s h j", s=2, j=J6)[:, 1]
            for k in range(MT):
                nc.gpsimd.tensor_tensor(value6[:, k, :, :], value6[:, k, :, :], bv, ALU.add).then_inc(l6_value, 1)
            nc.gpsimd.memset(value_head[:, :, J6:2 * J6], 1.0).then_inc(l6_value, 1)

        def l6_k_stack_sp(sp):
            sp.wait_ge(x_updated, 5 * T)
            sp.wait_ge(l7_const, 1)
            sp.dma_start(key6_stack[R6:R6 + 3, :, :], onesb[0:3, :].unsqueeze(1).broadcast_to([3, P, P])).then_inc(l6_k_stack, 16)
            sp.wait_ge(l6_k_parts, 1)
            for a in range(3):
                for b in range(3):
                    r = (3 * a + b) * J6
                    sp.dma_start(key6_stack[r:r + J6, :, :], k6_parts[:, b, :]).then_inc(l6_k_stack, 16)

        def l6_q_stack_dma(eng, a):
            for b in range(3):
                r = (3 * a + b) * J6
                eng.dma_start(query6_stack[r:r + J6, :, :], q6_parts[:, a, :]).then_inc(l6_q_stack, 16)

        def l6_sp(sp):
            sp.wait_ge(l6_k_stack, 16 * 10)
            sp.wait_ge(l6_q_parts, 1)
            for a in range(3):
                l6_q_stack_dma(sp, a)
            with sp.Fori(0, H6) as g:
                sp.wait_ge(l6_max_rows, g + 1)
                sp.dma_start(query6_stack[R6:R6 + 3, bass.ds(g, 1), :], max_rows[:]).then_inc(l6_max_stack, 16)
            sp.wait_ge(l6_o_rows, H6 + 1)
            sp.dma_start(o6_stack, o6_rows[0:J6, :, :]).then_inc(l6_o_stack, 16)
            sp.dma_start(sum6_stack, o6_rows[J6:2 * J6, :, :]).then_inc(l6_o_stack, 16)

        def at(g):
            return g if isinstance(g, int) else bass.ds(g, 1)

        def l6_row_scores_pe(pe, g, b, free=True):
            if free:
                pe.wait_ge(l6_max, 2 * g + b)
            for t in range(2):
                q = (2 * b + t) * P
                ins = nc.tensor.matmul(bank(t), query6_stack[0:R6, at(g), q:q + P], key6_stack[0:R6, at(g), b * KB:(b + 1) * KB],
                                       start=True, stop=True)
            ins.then_inc(l6_row_scores, 1)

        def l6_turn_pe(pe, g):
            pe.wait_ge(l6_max_parts, g + 1)
            for t in range(T):
                ins = nc.tensor.transpose(bank(2).bitcast(BF16)[0:3, t * P:(t + 1) * P], max_parts[:, t, :], identb[:])
            ins.then_inc(l6_max_turned, 1)

        def l6_st_pe(pe, g, b):
            if b == 0:
                pe.wait_ge(l6_max_stack, 16 * g + 16)
            for k in range(4):
                ins = nc.tensor.matmul(bank(3 + 2 * b + k // 2)[:, (k % 2) * K5:(k % 2 + 1) * K5],
                                       key6_stack[:, at(g), b * KB + k * P:b * KB + (k + 1) * P],
                                       query6_stack[:, at(g), b * K5:(b + 1) * K5], start=True, stop=True)
            ins.then_inc(l6_scores, 1)

        def l6_pv_pe(pe, g, b):
            if b == 0:
                pe.wait_ge(l6_o_rows, g + 1)
            pe.wait_ge(l6_value_head, 2 * g + (b + 1))
            pe.wait_ge(l6_probs, 2 * g + (b + 1))
            for k in range(4):
                ins = nc.tensor.matmul(bank(7)[0:2 * J6, b * K5:(b + 1) * K5], value_head[:, 4 * b + k, :],
                                       probs6[:, b, k * K5:(k + 1) * K5], start=(k == 0), stop=(k == 3))
            ins.then_inc(l6_o_ps, 1)

        def l6_head_pe(pe, g, first=False, turn=True, rows=True):
            l6_st_pe(pe, g, 0)
            if not first:
                l6_pv_pe(pe, g - 1, 1)
            l6_st_pe(pe, g, 1)
            if turn:
                l6_turn_pe(pe, g + 1)
            if rows:
                l6_row_scores_pe(pe, g + 2, 0)
            l6_pv_pe(pe, g, 0)
            if rows:
                l6_row_scores_pe(pe, g + 2, 1)

        def l6_pe(pe):
            pe.wait_ge(ln_xT, 7)
            nc.tensor.matmul(bank(5), wq6T[:], xT[:], start=True, stop=True).then_inc(l6_q_ps, 1)
            pe.wait_ge(l6_value, MT + 1)
            pe.wait_ge(l6_k_stack, 16 * 10)
            pe.wait_ge(l6_q_stack, 16 * 9)
            l6_row_scores_pe(pe, 0, 0, free=False)
            l6_row_scores_pe(pe, 0, 1)
            l6_row_scores_pe(pe, 1, 0)
            l6_turn_pe(pe, 0)
            l6_row_scores_pe(pe, 1, 1)
            l6_head_pe(pe, 0, first=True)
            with pe.Fori(1, H6 - 2) as g:
                l6_head_pe(pe, g)
            l6_head_pe(pe, H6 - 2, rows=False)
            l6_head_pe(pe, H6 - 1, turn=False, rows=False)
            l6_pv_pe(pe, H6 - 1, 1)
            pe.wait_ge(l6_oT, 1)
            for t in range(T):
                ins = nc.tensor.matmul(bank(5)[:, t * P:(t + 1) * P], o6T[:, t * P:(t + 1) * P], wo6T[:], start=True, stop=True)
            ins.then_inc(l6_y, 1)

        def l6_max_dve(dve, link, g):
            for b in range(2):
                dve.wait_ge(l6_row_scores, 2 * g + (b + 1))
                nc.vector.tensor_reduce(max6[:, 2 * b:2 * b + 2], PS[:, 0:2, :], X, ALU.max).then_inc(l6_max, 1)
            dve.wait_ge(l6_max, 2 * g + 2)
            link(nc.vector.tensor_scalar(max_parts[:, :, 0], max6[:], -1.0, None, ALU.mult))
            link(nc.vector.scalar_tensor_tensor(out=rest6[:], in0=max6[:], scalar=-1.0, in1=max_parts[:, :, 0],
                                                op0=ALU.mult, op1=ALU.subtract))
            link(nc.vector.tensor_copy(max_parts[:, :, 1], rest6[:]))
            link(nc.vector.tensor_tensor(rest6[:], rest6[:], max_parts[:, :, 1], ALU.subtract))
            nc.vector.tensor_copy(max_parts[:, :, 2], rest6[:]).then_inc(l6_max_parts, 1)

        def l6_rows_dve(dve, g, first=False):
            dve.wait_ge(l6_max_turned, g + 1)
            if not first:
                dve.wait_ge(l6_max_stack, 16 * g)
            nc.vector.tensor_copy(max_rows[:], bank(2).bitcast(BF16)[0:3, 0:N]).then_inc(l6_max_rows, 1)

        def l6_dve(dve, link):
            dve.wait_ge(l6_query, 1)
            split_parts(nc.vector, link, q6_parts, query6, l6_q_parts)
            link(nc.vector.tensor_tensor(x[:], x[:], bo6[:].unsqueeze(1).broadcast_to([P, T, D]), ALU.add))
            l6_max_dve(dve, link, 0)
            l6_rows_dve(dve, 0, first=True)
            l6_max_dve(dve, link, 1)
            l6_rows_dve(dve, 1)
            l6_max_dve(dve, link, 2)
            with dve.Fori(0, H6 - 3) as g:
                link.enter(g, 4)
                l6_rows_dve(dve, g + 2)
                l6_max_dve(dve, link, g + 3)
            link.leave(H6 - 3)
            l6_rows_dve(dve, H6 - 1)
            dve.wait_ge(l6_o_stack, 32)
            link(nc.vector.reciprocal(inv6, sum6_stack))
            nc.vector.tensor_tensor(o6T, o6_stack, inv6, ALU.mult).then_inc(l6_oT, 1)
            dve.wait_ge(l6_y, 1)
            for t in range(T):
                nc.vector.tensor_tensor(x[:, t, :], x[:, t, :], quarters(5)[:, t, :], ALU.add).then_inc(x_updated, 1)

        def l6_exp_act(act, g, b):
            act.wait_ge(l6_scores, 2 * g + (b + 1))
            nc.scalar.activation(probs6[:, b, :].rearrange("p (c n) -> p c n", c=2), PS[:, 3 + 2 * b:5 + 2 * b, :], ACT.Exp,
                                 scale=S6).then_inc(l6_probs, 1)

        def l6_o_act(act, g):
            act.wait_ge(l6_o_ps, 2 * g + 2)
            act_copy(o6_rows[:, at(g), :], bank(7)[0:2 * J6, :]).then_inc(l6_o_rows, 1)

        def l6_act(act):
            act.wait_ge(l6_q_ps, 1)
            nc.scalar.activation(query6, bank(5), ACT.Identity, bias=bq6[:]).then_inc(l6_query, 1)
            act.sem_inc(l6_o_rows, 1)
            for b in range(2):
                l6_exp_act(act, 0, b)
            with act.Fori(1, H6) as g:
                l6_exp_act(act, g, 0)
                l6_o_act(act, g - 1)
                l6_exp_act(act, g, 1)
            l6_o_act(act, H6 - 1)

        def l6_pool(pool):
            pool.wait_ge(l6_value, MT + 1)
            for b in range(2):
                half = slice(b * KT6, (b + 1) * KT6)
                nc.gpsimd.tensor_copy(value_head[:, half, 0:J6], value6[:, half, 0, :]).then_inc(l6_value_head, 1)
            with pool.Fori(1, H6) as g:
                for b in range(2):
                    half = slice(b * KT6, (b + 1) * KT6)
                    pool.wait_ge(l6_o_ps, 2 * g - (1 - b))
                    nc.gpsimd.tensor_copy(value_head[:, half, 0:J6], value6[:, half, bass.ds(g, 1), :].rearrange("p k a j -> p k (a j)")).then_inc(l6_value_head, 1)

        E7 = 8
        F7 = 512
        CAP7 = 160
        wr7 = sb("wr7", [P, E7])
        w17 = [place_weights(1536 * s, [P, F7]) for s in range(2)]
        w37 = [place_weights(1536 * s + 512, [P, F7]) for s in range(2)]
        w27 = [place_weights(1536 * s + 1024, [P, 4, D]) for s in range(2)]
        chosen7 = sb("chosen7", [P, T, E7], BF16)
        earlier7 = sb("earlier7", [P, P], BF16)
        onesb = sb("onesb", [P, P], BF16)
        silu7 = place(0, [P, 2, N])
        hiddenT7 = place(1024, [P, 2 * 4, N]).rearrange("p (s c) n -> p s c n", s=2)
        l7_const = sem("l7_const")
        l7_router_loaded = sem("l7_router_loaded")
        l7_loaded = [sem("l7_loaded_even"), sem("l7_loaded_odd")]
        l7_logits = sem("l7_logits")
        l7_chosen = sem("l7_chosen")
        l7_before = sem("l7_before")
        l7_h = sem("l7_h")
        l7_silu = sem("l7_silu")
        l7_hidden = sem("l7_hidden")
        l7_y = sem("l7_y")
        l7_added = sem("l7_added")

        def l7_const_pool(pool, link):
            link(nc.gpsimd.memset(earlier7[:], 1.0))
            link(nc.gpsimd.affine_select(out=earlier7[:], in_=earlier7[:], compare_op=ALU.is_gt, fill=0.0, base=0,
                                         pattern=[[1, P]], channel_multiplier=-1))
            nc.gpsimd.memset(onesb[:], 1.0).then_inc(l7_const, 1)

        def l7_load(sp, w1, w3, w2, slot):
            sp.dma_start(w17[slot], w1).then_inc(l7_loaded[slot], 16)
            sp.dma_start(w37[slot], w3).then_inc(l7_loaded[slot], 16)
            sp.dma_start(w27[slot], w2).then_inc(l7_loaded[slot], 16)

        def l7_loads_sp(sp):
            W1, W3 = i["L3_ffn_W1"], i["L3_ffn_W3"]
            W2 = i["L3_ffn_W2"].rearrange("e (c p) d -> e p c d", p=P)
            sp.wait_ge(x_updated, 6 * T)
            l7_load(sp, W1[0], W3[0], W2[0], 0)
            with sp.Fori(0, E7 // 2 - 1) as pair:
                for k in range(2):
                    sp.wait_ge(l7_added, 2 * pair + (k + 2))
                    e = 2 * pair + (k + 1)
                    l7_load(sp, W1[bass.ds(e, 1)].rearrange("a d f -> d (a f)"), W3[bass.ds(e, 1)].rearrange("a d f -> d (a f)"),
                            W2[bass.ds(e, 1)].rearrange("a p c d -> p (a c) d"), 1 - k)
            sp.wait_ge(l7_added, E7)
            l7_load(sp, W1[E7 - 1], W3[E7 - 1], W2[E7 - 1], 1)

        def l7_router_pe(pe):
            pe.wait_ge(ln_xT, 8)
            pe.wait_ge(l7_router_loaded, 16)
            for t in range(T):
                ins = nc.tensor.matmul(bank(6)[:, t * E7:(t + 1) * E7], xT[:, t * P:(t + 1) * P], wr7[:], start=True, stop=True)
            ins.then_inc(l7_logits, 1)
            pe.wait_ge(l7_chosen, 1)
            pe.wait_ge(l7_const, 1)
            for t in range(T):
                cols = bank(6)[:, t * E7:(t + 1) * E7]
                for u in range(t):
                    nc.tensor.matmul(cols, onesb[:], chosen7[:, u, :], start=(u == 0), stop=False)
                ins = nc.tensor.matmul(cols, earlier7[:], chosen7[:, t, :], start=(t == 0), stop=True)
            ins.then_inc(l7_before, 1)

        def l7_router_dve(dve, link):
            dve.wait_ge(l7_logits, 1)
            link(nc.vector.tensor_scalar(logits[:, :, 0:E7], bank(6)[:, 0:T * E7].rearrange("p (t e) -> p t e", t=T),
                                         1e4, -1e4, ALU.min, ALU.max))
            shift_dve(link, logits, E7)
            top2_dve(link, logits, E7)
            nc.vector.tensor_copy(chosen7[:], chosen[:, :, 0:E7]).then_inc(l7_chosen, 1)
            dve.wait_ge(gate_exp, 4)
            weights_dve(link, E7, eps=1e-12)
            dve.wait_ge(l7_before, 1)
            link(nc.vector.tensor_scalar(equal[:, :, 0:E7], bank(6)[:, 0:T * E7].rearrange("p (t e) -> p t e", t=T), float(CAP7), None, ALU.is_lt))
            link(nc.vector.tensor_tensor(comb[:, :, 0:E7], comb[:, :, 0:E7], equal[:, :, 0:E7], ALU.mult))

        def l7_chunk_pe(pe, e, slot, c, loads):
            if c == 0:
                pe.wait_ge(l7_loaded[slot], 48 * loads)
            pe.wait_ge(l7_hidden, 4 * e + (c + 1))
            b = 2 * (c % 2)
            nc.tensor.matmul(bank(b), w17[slot][:, c * P:(c + 1) * P], xT[:], start=True, stop=True)
            nc.tensor.matmul(bank(b + 1), w37[slot][:, c * P:(c + 1) * P], xT[:], start=True, stop=True).then_inc(l7_h, 1)

        def l7_out_pe(pe, e, slot):
            pe.wait_ge(l7_hidden, 4 * e + 6)
            pe.wait_ge(l7_added, e + 1)
            for t in range(T):
                for c in range(4):
                    ins = nc.tensor.matmul(bank(4 + slot)[:, t * P:(t + 1) * P], hiddenT7[:, slot, c, t * P:(t + 1) * P],
                                           w27[slot][:, c, :], start=(c == 0), stop=(c == 3))
            ins.then_inc(l7_y, 1)

        def l7_pe(pe):
            for c in range(4):
                l7_chunk_pe(pe, 0, 0, c, 1)
            with pe.Fori(0, E7 // 2 - 1) as pair:
                for k in range(2):
                    e = 2 * pair + (k + 1)
                    l7_chunk_pe(pe, e, 1 - k, 0, pair + (k + 1))
                    l7_out_pe(pe, 2 * pair + k, k)
                    for c in range(1, 4):
                        l7_chunk_pe(pe, e, 1 - k, c, pair + (k + 1))
            l7_chunk_pe(pe, E7 - 1, 1, 0, E7 // 2)
            l7_out_pe(pe, E7 - 2, 0)
            for c in range(1, 4):
                l7_chunk_pe(pe, E7 - 1, 1, c, E7 // 2)
            l7_out_pe(pe, E7 - 1, 1)

        def l7_act(act):
            with act.Fori(0, E7) as e:
                for c in range(4):
                    act.wait_ge(l7_h, 4 * e + (c + 1))
                    nc.scalar.activation(silu7[:, c % 2, :], bank(2 * (c % 2)), ACT.Silu).then_inc(l7_silu, 1)

        def l7_hidden_dve(dve, e, slot):
            for c in range(4):
                dve.wait_ge(l7_silu, 4 * e + (c + 1))
                nc.vector.tensor_tensor(hiddenT7[:, slot, c, :], silu7[:, c % 2, :], bank(2 * (c % 2) + 1), ALU.mult).then_inc(l7_hidden, 1)

        def l7_add_dve(dve, e, static, slot, last):
            dve.wait_ge(l7_y, e + 1)
            dve.wait_ge(l7_added, e + 2)
            for t in range(T):
                ins = nc.vector.scalar_tensor_tensor(out=x[:, t, :], in0=quarters(4 + slot)[:, t, :],
                                                     scalar=comb[:, t, e:e + 1] if static else comb[:, t, bass.ds(e, 1)],
                                                     in1=x[:, t, :], op0=ALU.mult, op1=ALU.add)
                if last:
                    ins.then_inc(x_updated, 1)
            if not last:
                ins.then_inc(l7_added, 1)

        def l7_dve(dve):
            dve.sem_inc(l7_hidden, 2)
            dve.sem_inc(l7_added, 2)
            l7_hidden_dve(dve, 0, 0)
            with dve.Fori(0, E7 // 2 - 1) as pair:
                for k in range(2):
                    l7_hidden_dve(dve, 2 * pair + (k + 1), 1 - k)
                    l7_add_dve(dve, 2 * pair + k, False, k, False)
            l7_hidden_dve(dve, E7 - 1, 1)
            l7_add_dve(dve, E7 - 2, True, 0, False)
            l7_add_dve(dve, E7 - 1, True, 1, True)

        x_dram = i["x"].rearrange("b (t p) d -> p (b t) d", p=P)
        out_dram = out.rearrange("b (t p) d -> p (b t) d", p=P)
        ctx_dram = i["ctx_768"].rearrange("b (t p) c -> p (b t) c", p=P)

        def row(v, n):
            return v.unsqueeze(0).broadcast_to([n, v.shape[0]])

        block = ctx.enter_context(nc.Block())

        @block.sync
        def _(sp):
            sp.dma_start(x[:], x_dram).then_inc(x_loaded, 16)
            sp.dma_start(ctx_rows[:], ctx_dram).then_inc(ctx_loaded, 16)
            sp.dma_start(wq[:], i["L0_xattn_Wq"]).then_inc(l0_loaded, 16)
            sp.dma_start(wk[:], i["L0_xattn_Wk"]).then_inc(l0_loaded, 16)
            sp.dma_start(wv[:], i["L0_xattn_Wv"]).then_inc(l0_loaded, 16)
            sp.dma_start(wout[:], i["L0_xattn_Wout"].rearrange("(h p) d -> p h d", p=P)).then_inc(l0_loaded, 16)
            sp.dma_start(bout[:], row(i["L0_xattn_bout"], P)).then_inc(l0_loaded, 16)
            sp.dma_start(we[:], i["L0_ffn_We"].rearrange("e o i -> o e i")).then_inc(l1_loaded, 16)
            sp.dma_start(wg1[:], i["L0_ffn_Wg"]).then_inc(l1_loaded, 16)
            sp.dma_start(bg1[:], row(i["L0_ffn_bg"], P)).then_inc(l1_loaded, 16)
            sp.dma_start(be1[:], i["L0_ffn_be"]).then_inc(l1_loaded, 16)
            sp.dma_start(wq2[:], i["L1_xattn_Wq"]).then_inc(l2_loaded, 16)
            sp.dma_start(wk2[:], i["L1_xattn_Wk"]).then_inc(l2_loaded, 16)
            sp.dma_start(wv2[:], i["L1_xattn_Wv"]).then_inc(l2_loaded, 16)
            sp.dma_start(bq2[:], i["L1_xattn_bq"].unsqueeze(1)).then_inc(l2_loaded, 16)
            sp.dma_start(bk2[:], i["L1_xattn_bk"].unsqueeze(1)).then_inc(l2_loaded, 16)
            sp.dma_start(bv2[:], row(i["L1_xattn_bv"], P)).then_inc(l2_loaded, 16)
            sp.dma_start(b1[:], i["L1_ffn_b1"]).then_inc(l3_loaded, 16)
            sp.dma_start(wg3[:], i["L1_ffn_Wg"]).then_inc(l3_loaded, 16)
            sp.dma_start(wo3[:], i["L1_ffn_Wo"]).then_inc(l3_loaded, 16)
            sp.dma_start(bo3[:], row(i["L1_ffn_bo"], P)).then_inc(l3_loaded, 16)
            sp.dma_start(w1[:], i["L1_ffn_W1"].rearrange("e (c p) d -> p e c d", p=P)).then_inc(l3_loaded, 16)
            sp.dma_start(wd4[:], i["L2_xattn_W_d2v"]).then_inc(l4_loaded, 16)
            sp.dma_start(wi4[:], i["L2_xattn_W_img"]).then_inc(l4_loaded, 16)
            sp.dma_start(wt4[:], i["L2_xattn_W_txt"]).then_inc(l4_loaded, 16)
            sp.dma_start(wf14[:], i["L2_xattn_W_f1"].rearrange("(c p) i -> p c i", p=P)).then_inc(l4_loaded, 16)
            sp.dma_start(wf24[:], i["L2_xattn_W_f2"]).then_inc(l4_loaded, 16)
            for l in range(2):
                wa, ba = i[f"L2_xattn_W_att{l}"], i[f"L2_xattn_b_att{l}"]
                sp.dma_start(wa4[:, l, :], wa).then_inc(l4_loaded, 16)
                sp.dma_start(ba4_rows[:, l, :], row(ba, P)).then_inc(l4_loaded, 16)
                for copy in range(2):
                    sp.dma_start(ba4[64 * copy:64 * (copy + 1), l:l + 1], ba.unsqueeze(1)).then_inc(l4_ba, 16)
            sp.dma_start(bd4[:], i["L2_xattn_b_d2v"].unsqueeze(1)).then_inc(l4_loaded, 16)
            sp.dma_start(bi4[:], i["L2_xattn_b_img"].unsqueeze(1)).then_inc(l4_loaded, 16)
            sp.dma_start(bt4[:], i["L2_xattn_b_txt"].unsqueeze(1)).then_inc(l4_loaded, 16)
            for c in range(4):
                sp.dma_start(bf14[:, c:c + 1], i["L2_xattn_b_f1"][c * P:(c + 1) * P].unsqueeze(1)).then_inc(l4_loaded, 16)
            sp.dma_start(bf24[:], row(i["L2_xattn_b_f2"], P)).then_inc(l4_loaded, 16)
            sp.wait_ge(l3_b1_parts, 1)
            for k, part in enumerate((b1_hi, b1_mid, b1_lo)):
                sp.dma_start(b1_rows[k:k + 1, :, :], part[:]).then_inc(l3_b1_rows, 16)
            sp.wait_ge(x_updated, 2 * T)
            for k, name in enumerate(("q", "k", "v")):
                sp.dma_start(proj5[:, :, k * D:(k + 1) * D], i[f"L2_ffn_{name}_proj"].rearrange("e c h -> c e h")).then_inc(l5_loaded, 16)
            sp.dma_start(oproj5[:], i["L2_ffn_o_proj"].rearrange("e h c -> h e c")).then_inc(l5_loaded, 16)
            sp.dma_start(sim5[:], i["L2_ffn_sim_matrix"]).then_inc(l5_loaded, 16)
            sp.dma_start(gates5[:], row(i["L2_ffn_gates"], P)).then_inc(l5_loaded, 16)
            sp.dma_start(wq6[:], i["L3_xattn_Wq"]).then_inc(l6_loaded, 16)
            sp.dma_start(wkv6[:], i["L3_xattn_Wkv"].rearrange("(k p) c -> p k c", p=P)).then_inc(l6_loaded, 16)
            sp.dma_start(wo6[:], i["L3_xattn_Wo"]).then_inc(l6_loaded, 16)
            with nc.allow_non_contiguous_dma(reason="128 elements, in the features' new order"):
                sp.dma_start(bq6[:], i["L3_xattn_bq"].rearrange("(h j) -> j h", j=J6)).then_inc(l6_loaded, 16)
                sp.dma_start(bk6[:], i["L3_xattn_bkv"].rearrange("(h s j) -> s j h", s=2, j=J6)[0]).then_inc(l6_loaded, 16)
            sp.dma_start(bkv6[:], row(i["L3_xattn_bkv"], P)).then_inc(l6_loaded, 16)
            sp.dma_start(bo6[:], row(i["L3_xattn_bo"], P)).then_inc(l6_loaded, 16)
            sp.dma_start(wr7[:], i["L3_ffn_Wr"]).then_inc(l7_router_loaded, 16)
            l6_k_stack_sp(sp)
            l6_sp(sp)
            l7_loads_sp(sp)
            sp.wait_ge(x_updated, T * 8)
            sp.dma_start(out_dram, x[:]).then_inc(stored, 16)
            sp.wait_ge(stored, 16)

        @block.gpsimd
        def _(pool):
            link = Chain(pool, pool_chain)
            const_pool(pool)
            rev_pool()
            l4_const_pool()
            l5_const_pool(pool, link)
            l7_const_pool(pool, link)
            ln_pool(pool, link, 0)
            l0_pool(pool)
            for n in range(1, 8):
                if n == 5:
                    l5_norm_pool(pool)
                ln_pool(pool, link, n)
                if n == 5:
                    l5_xnorm_pool(pool)
                    l6_prepare_pool(pool, link)
                if n == 6:
                    l6_pool(pool)
                if n == 4:
                    for k in range(6):
                        whole_max_pool(pool, k)

        @block.tensor
        def _(pe):
            fold_pe(pe)
            ln_pe(pe, 0)
            l0_pe(pe)
            l1_prepare_pe(pe)
            ln_pe(pe, 1)
            l1_pe(pe)
            l2_prepare_pe(pe)
            ln_pe(pe, 2)
            l2_pe(pe)
            l3_prepare_pe(pe)
            ln_pe(pe, 3)
            l3_pe(pe)
            l4_ternary_pe(pe)
            ln_pe(pe, 4)
            l4_ctx_pe(pe)
            l4_pe(pe)
            l5_sim_pe(pe)
            ln_pe(pe, 5)
            l5_router_pe(pe)
            l5_pe(pe)
            ln_pe(pe, 6)
            l6_pe(pe)
            ln_pe(pe, 7)
            l7_router_pe(pe)
            l7_pe(pe)

        @block.scalar
        def _(act):
            fold_copy(act, act_copy, 1, fold_act)
            ln_act(act, 0)
            l0_act(act)
            l1_prepare_act(act)
            ln_act(act, 1)
            gate_act(act, 1, E1)
            l1_act(act)
            l2_prepare_act(act)
            ln_act(act, 2)
            l2_act(act)
            l3_prepare_act(act)
            ln_act(act, 3)
            gate_act(act, 2, E3)
            l3_act(act)
            l4_ternary_act(act)
            ln_act(act, 4)
            l4_ctx_act(act)
            l4_act(act)
            l5_sim_act(act)
            ln_act(act, 5)
            l6_prepare_act(act)
            gate_act(act, 3, E5)
            l5_act(act)
            ln_act(act, 6)
            l6_act(act)
            ln_act(act, 7)
            gate_act(act, 4, E7)
            l7_act(act)

        @block.vector
        def _(dve):
            link = Chain(dve, dve_chain)
            ln_dve(dve, link, 0)
            fold_copy(dve, nc.vector.tensor_copy, 0, fold_dve)
            l0_dve(dve, link)
            ln_dve(dve, link, 1)
            l1_dve(dve, link)
            ln_dve(dve, link, 2)
            l2_prepare_dve(dve)
            l2_dve(dve, link)
            l3_parts_dve(dve, link)
            ln_dve(dve, link, 3)
            l3_dve(dve, link)
            l4_ternary_dve(dve, link)
            ln_dve(dve, link, 4)
            l4_ctx_dve(dve, link)
            l4_dve(dve, link)
            l5_sim_dve(dve, link)
            ln_dve(dve, link, 5)
            l5_router_dve(dve, link)
            l5_dve(dve, link)
            ln_dve(dve, link, 6)
            l6_dve(dve, link)
            ln_dve(dve, link, 7)
            l7_router_dve(dve, link)
            l7_dve(dve)


def kernel(**inputs):
    import numpy as np
    import concourse.bacc as bacc
    from concourse.bass_utils import run_bass_kernel_spmd

    nc = bacc.Bacc("TRN2", target_bir_lowering=False, num_devices=1)
    arrays, given = {}, {}
    for name, value in inputs.items():
        a = np.ascontiguousarray(value)
        arrays[f"in_{name}"] = a
        given[name] = nc.dram_tensor(f"in_{name}", a.shape, mybir.dt.from_np(a.dtype), kind="ExternalInput").ap()
    out = nc.dram_tensor("out_x", given["x"].shape, F32, kind="ExternalOutput").ap()
    build(nc, given, out)
    return run_bass_kernel_spmd(nc, [arrays], core_ids=[0]).results[0]["out_x"]
```

```python
from contextlib import ExitStack

import concourse.bass as bass
from concourse import mybir

F32 = mybir.dt.float32
BF16 = mybir.dt.bfloat16
ALU = mybir.AluOpType
ACT = mybir.ActivationFunctionType
X = mybir.AxisListType.X
RADD = bass.bass_isa.ReduceOp.add
RMAX = bass.bass_isa.ReduceOp.max

P = 128
B = 2
D = 128
C = 96
N = 512
T = N // P
M = 1024
MT = M // P
KB = M // B
BIG = 3.0e38
ROUND = 12582912.0


class Chain:

    def __init__(self, engine, semaphore):
        self.engine, self.semaphore = engine, semaphore
        self.base, self.step, self.turn, self.per = 0, 0, None, 0

    def __call__(self, ins):
        ins.then_inc(self.semaphore, 1)
        self.step += 1
        if self.turn is None:
            self.engine.wait_ge(self.semaphore, self.base + self.step)
        else:
            self.engine.wait_ge(self.semaphore, self.turn * self.per + (self.base + self.step))
        return ins

    def enter(self, turn, per):
        self.base, self.step, self.turn, self.per = self.base + self.step, 0, turn, per

    def leave(self, turns):
        assert self.step == self.per, (self.step, self.per)
        self.base, self.step, self.turn = self.base + turns * self.per, 0, None


def wide(ap, n):
    return ap.unsqueeze(2).broadcast_to([ap.shape[0], ap.shape[1], n])


def build(nc, i, out):
    with ExitStack() as ctx:
        def sb(name, shape, dt=F32):
            return ctx.enter_context(nc.sbuf_tensor(name, shape, dt))

        def sem(name):
            return ctx.enter_context(nc.semaphore(name))

        PS = ctx.enter_context(nc.psum_tensor("PS", [P, 8, 512], F32))

        def bank(b):
            return PS[:, b, :]

        def quarters(b):
            return PS[:, b, :].rearrange("p (t d) -> p t d", t=4)

        x = sb("x", [P, T, D])
        xn = sb("xn", [P, T, D])
        xT = sb("xT", [P, N])
        ident = sb("ident", [P, P])
        identb = sb("identb", [P, P], BF16)
        ctx_rows = sb("ctx_rows", [P, MT, C])
        ctxT = sb("ctxT", [C, M])
        stats = sb("stats", [P, T, 6])
        moments = sb("moments", [P, T, 2])
        rstd = sb("rstd", [P, T])
        minus_half = sb("minus_half", [P, 16])

        room = sb("room", [P, 12288])

        weight_room = sb("weight_room", [P, 8192])

        def place_in(whole, at, shape):
            size = 1
            for n in shape[1:]:
                size *= n
            ap = whole[0:shape[0], at:at + size]
            if len(shape) == 3:
                ap = ap.rearrange("p (a b) -> p a b", a=shape[1])
            return ap

        def place(at, shape):
            return place_in(room, at, shape)

        def place_weights(at, shape):
            return place_in(weight_room, at, shape)

        x_loaded = sem("x_loaded")
        ctx_loaded = sem("ctx_loaded")
        early_loaded = sem("early_loaded")
        late_loaded = sem("late_loaded")
        ident_zero = sem("ident_zero")
        ident_done = sem("ident_done")
        dve_chain = sem("dve_chain")
        act_chain = sem("act_chain")
        pool_chain = sem("pool_chain")
        x_updated = sem("x_updated")
        ln_moments = sem("ln_moments")
        ln_rstd = sem("ln_rstd")
        ln_rows = sem("ln_rows")
        ln_turned = sem("ln_turned")
        ln_xT = sem("ln_xT")
        stored = sem("stored")

        def const_pool(pool):
            nc.gpsimd.memset(ident[:], 0.0).then_inc(ident_zero, 1)
            nc.gpsimd.memset(minus_half[:], -0.5).then_inc(ident_done, 1)
            pool.wait_ge(ident_zero, 1)
            nc.gpsimd.affine_select(out=ident[:], in_=ident[:], compare_op=ALU.not_equal, fill=1.0, base=0,
                                    pattern=[[-1, P]], channel_multiplier=1).then_inc(ident_done, 1)
            pool.wait_ge(ident_done, 2)
            nc.gpsimd.tensor_copy(identb[:], ident[:]).then_inc(ident_done, 1)

        LN_BANK = 7

        def ln_dve(dve, link, n):
            if n == 0:
                dve.wait_ge(x_loaded, 16)
            else:
                dve.wait_ge(x_updated, T * n)
            for t in range(T):
                ins = nc.vector.bn_stats(stats[:, t, :], x[:, t, :])
            link(ins)
            for t in range(T):
                ins = nc.vector.bn_aggr(moments[:, t, :], stats[:, t, :])
            ins.then_inc(ln_moments, 1)
            dve.wait_ge(ln_rstd, n + 1)
            for t in range(T):
                nc.vector.tensor_scalar(xn[:, t, :], x[:, t, :], moments[:, t, 0:1], rstd[:, t:t + 1],
                                        ALU.subtract, ALU.mult).then_inc(ln_rows, 1)

        def ln_pool(pool, link, n):
            pool.wait_ge(ln_moments, n + 1)
            link(nc.gpsimd.tensor_scalar(rstd[:], moments[:, :, 1], 1e-5, None, ALU.add))
            nc.gpsimd.tensor_tensor(rstd[:], rstd[:], minus_half[:, 0:T], ALU.pow).then_inc(ln_rstd, 1)

        def ln_pe(pe, n):
            for t in range(T):
                pe.wait_ge(ln_rows, T * n + t + 1)
                ins = nc.tensor.transpose(bank(LN_BANK)[:, t * P:(t + 1) * P], xn[:, t, :], ident[:])
            ins.then_inc(ln_turned, 1)

        def ln_act(act, n):
            act.wait_ge(ln_turned, n + 1)
            nc.scalar.activation(xT[:], bank(LN_BANK), ACT.Copy).then_inc(ln_xT, 1)

        H0 = 8
        L0_LOOP = 3
        S0 = 1.5 * float(D) ** -0.5
        wq = place_weights(0, [P, H0 * D])
        wk = place_weights(1024, [C, H0 * D])
        wv = place_weights(2048, [C, H0 * D])
        wout = place_weights(3072, [P, H0, D])
        wqT = place(6144, [P, H0, D])
        wkT = place(7168, [P, H0, C])
        wvT = place(7936, [P, H0, C])
        A_all = place_weights(4096, [P, H0, C])
        M_all = place_weights(4864, [C, H0, D])
        A_head = sb("A_head", [P, C])
        T_head = place(8704, [C, N])
        probs = place(0, [P, 2, M])
        probsT = place(2048, [P, MT, N])
        mixT = place(9216, [C, N])
        row_max = sb("row_max", [P, T])
        neg_max = sb("neg_max", [P, T])
        row_sum = sb("row_sum", [P, T])
        row_inv = sb("row_inv", [P, T])
        bout = sb("bout", [P, D])
        l0_loaded = sem("l0_loaded")
        fold_turned = sem("fold_turned")
        fold_dve = sem("fold_dve")
        fold_act = sem("fold_act")
        l0_A = sem("l0_A")
        l0_query = sem("l0_query")
        l0_T = sem("l0_T")
        l0_scores = sem("l0_scores")
        l0_negmax = sem("l0_negmax")
        l0_probs = sem("l0_probs")
        l0_turned = sem("l0_turned")
        l0_free_a = sem("l0_free_a")
        l0_free_b = sem("l0_free_b")
        l0_mixed = sem("l0_mixed")
        l0_mixT = sem("l0_mixT")
        l0_headout = sem("l0_headout")
        l0_added = sem("l0_added")

        def fold_turn_pe(pe, w, rows, banks):
            for half in range(2):
                for q in range(4):
                    h = 4 * half + q
                    ins = nc.tensor.transpose(bank(banks[half])[:, q * P:q * P + rows], w[:, h * D:(h + 1) * D],
                                              ident[0:rows, 0:rows])
                ins.then_inc(fold_turned, 1)

        def fold_pe(pe):
            pe.wait_ge(ident_done, 2)
            pe.wait_ge(ctx_loaded, 16)
            for half in range(2):
                for q in range(4):
                    ins = nc.tensor.transpose(bank(half)[0:C, q * P:(q + 1) * P], ctx_rows[:, 4 * half + q, :], ident[:])
                ins.then_inc(fold_turned, 1)
            pe.wait_ge(l0_loaded, 16 * 5)
            fold_turn_pe(pe, wq, P, (2, 3))
            fold_turn_pe(pe, wk, C, (4, 5))
            pe.wait_ge(fold_dve, 3)
            pe.wait_ge(fold_act, 3)
            for half in range(2):
                for q in range(4):
                    h = 4 * half + q
                    ins = nc.tensor.matmul(bank(half)[:, q * P:q * P + C], wqT[:, h, :], wkT[:, h, :],
                                           start=True, stop=True)
                ins.then_inc(fold_turned, 1)

        def fold_M_pe(pe):
            pe.wait_ge(fold_dve, 5)
            pe.wait_ge(fold_act, 5)
            for half in range(2):
                for q in range(4):
                    h = 4 * half + q
                    ins = nc.tensor.matmul(bank(4 + half)[0:C, q * P:(q + 1) * P], wvT[:, h, :], wout[:, h, :],
                                           start=True, stop=True)
                ins.then_inc(fold_turned, 1)

        def fold_copy(eng, copy, half, done):
            lo = 4 * half
            eng.wait_ge(fold_turned, 1 + half)
            copy(ctxT[:, half * 512:(half + 1) * 512], bank(half)[0:C, :]).then_inc(done, 1)
            eng.wait_ge(fold_turned, 3 + half)
            copy(wqT[:, lo:lo + 4, :], quarters(2 + half)).then_inc(done, 1)
            eng.wait_ge(fold_turned, 5 + half)
            copy(wkT[:, lo:lo + 4, :], quarters(4 + half)[:, :, 0:C]).then_inc(done, 1)
            eng.wait_ge(fold_turned, 7 + half)
            copy(A_all[:, lo:lo + 4, :], quarters(half)[:, :, 0:C]).then_inc(done, 1)

        def fold_wv_copy(eng, copy, half, done):
            eng.wait_ge(fold_turned, 9 + half)
            copy(wvT[:, 4 * half:4 * half + 4, :], quarters((6, 5)[half])[:, :, 0:C]).then_inc(done, 1)

        def fold_M_copy(eng, copy, half, done):
            eng.wait_ge(fold_turned, 11 + half)
            copy(M_all[:, 4 * half:4 * half + 4, :], quarters(4 + half)[0:C]).then_inc(done, 1)

        def at(g):
            return slice(g, g + 1) if isinstance(g, int) else bass.ds(g, 1)

        def act_copy(dst, src):
            return nc.scalar.activation(dst, src, ACT.Copy)

        def l0_scores_pe(pe, t):
            for half in range(2):
                ins = nc.tensor.matmul(bank(2 * (t % 2) + half), T_head[:, t * P:(t + 1) * P],
                                       ctxT[:, half * 512:(half + 1) * 512], start=True, stop=True)
            ins.then_inc(l0_scores, 1)

        def l0_query_pe(pe, h):
            pe.wait_ge(l0_A, h + 1)
            nc.tensor.matmul(bank(7)[0:C, :], A_head[:], xT[:], start=True, stop=True).then_inc(l0_query, 1)

        def l0_turn_pe(pe, h, t):
            pe.wait_ge(l0_probs, T * h + (t + 1))
            for half, free in ((0, l0_free_a), (1, l0_free_b)):
                pe.wait_ge(free, T * h + (t + 1))
                for q in range(4):
                    k = 4 * half + q
                    ins = nc.tensor.transpose(bank(4 + half)[:, q * P:(q + 1) * P],
                                              probs[:, t % 2, k * P:(k + 1) * P], ident[:])
                ins.then_inc(l0_turned, 1)

        def l0_mixed_pe(pe, h, half):
            if half == 0:
                pe.wait_ge(l0_added, h + 1)
            for free in (l0_free_a, l0_free_b):
                pe.wait_ge(free, T * h + (2 * half + 3))
            cols = slice(half * 2 * P, (half + 1) * 2 * P)
            for k in range(MT):
                ins = nc.tensor.matmul(bank(6)[0:C, cols], ctx_rows[:, k, :], probsT[:, k, cols],
                                       start=(k == 0), stop=(k == MT - 1))
            ins.then_inc(l0_mixed, 1)

        def l0_head_pe(pe, h, last):
            l0_turn_pe(pe, h, 0)
            l4_early_pe(pe, h, 0)
            l0_scores_pe(pe, 2)
            l0_turn_pe(pe, h, 1)
            l4_early_pe(pe, h, 1)
            l0_scores_pe(pe, 3)
            if not last:
                l4_early_pe(pe, h, 2)
                l0_query_pe(pe, h + 1)
            l0_turn_pe(pe, h, 2)
            l0_mixed_pe(pe, h, 0)
            l0_turn_pe(pe, h, 3)
            if not last:
                pe.wait_ge(l0_T, h + 2)
                l0_scores_pe(pe, 0)
            l0_mixed_pe(pe, h, 1)
            if not last:
                l0_scores_pe(pe, 1)
            pe.wait_ge(l0_mixT, h + 1)
            for t in range(T):
                ins = nc.tensor.matmul(bank(6)[:, t * P:(t + 1) * P], mixT[:, t * P:(t + 1) * P],
                                       M_all[:, at(h), :], start=True, stop=True)
            ins.then_inc(l0_headout, 1)

        def l0_pe(pe):
            fold_turn_pe(pe, wv, C, (6, 5))
            pe.wait_ge(ln_xT, 1)
            l0_query_pe(pe, 0)
            fold_M_pe(pe)
            pe.wait_ge(l0_T, 1)
            l0_scores_pe(pe, 0)
            l0_scores_pe(pe, 1)
            pe.wait_ge(fold_dve, 6)
            pe.wait_ge(fold_act, 6)
            with pe.Fori(0, L0_LOOP) as h:
                l0_head_pe(pe, h, False)
            for h in range(L0_LOOP, H0):
                l0_head_pe(pe, h, h == H0 - 1)

        def l0_max_dve(dve, link, h, t):
            dve.wait_ge(l0_scores, T * h + (t + 1))
            link(nc.vector.tensor_reduce(row_max[:, t:t + 1], PS[:, 2 * (t % 2):2 * (t % 2) + 2, :],
                                         mybir.AxisListType.XY, ALU.max))
            nc.vector.tensor_scalar(neg_max[:, t:t + 1], row_max[:, t:t + 1], -S0, None, ALU.mult).then_inc(l0_negmax, 1)

        def l0_turned_dve(dve, h, t):
            dve.wait_ge(l0_turned, 2 * T * h + (2 * t + 1))
            nc.vector.tensor_copy(probsT[:, 0:4, t * P:(t + 1) * P], quarters(4)).then_inc(l0_free_a, 1)

        def l0_head_dve(dve, link, h, last):
            for t in range(T):
                if t == T - 1:
                    l4_early_dve(dve, link, h, 1)
                l0_turned_dve(dve, h, t)
                if t == 0:
                    l4_early_dve(dve, link, h, 0)
                if t < T - 2:
                    l0_max_dve(dve, link, h, t + 2)
            dve.wait_ge(l0_probs, T * h + T)
            link(nc.vector.reciprocal(row_inv[:], row_sum[:]))
            if not last:
                l0_max_dve(dve, link, h + 1, 0)
            l4_early_dve(dve, link, h, 2)
            if not last:
                l0_max_dve(dve, link, h + 1, 1)
            dve.wait_ge(l0_headout, h + 1)
            dve.wait_ge(l0_added, h + 1)
            for t in range(T):
                ins = nc.vector.scalar_tensor_tensor(out=x[:, t, :], in0=quarters(6)[:, t, :], scalar=row_inv[:, t:t + 1],
                                                     in1=x[:, t, :], op0=ALU.mult, op1=ALU.add)
                if last:
                    ins.then_inc(x_updated, 1)
            if not last:
                ins.then_inc(l0_added, 1)

        def l0_dve(dve, link):
            fold_wv_copy(dve, nc.vector.tensor_copy, 0, fold_dve)
            fold_M_copy(dve, nc.vector.tensor_copy, 0, fold_dve)
            dve.wait_ge(l0_loaded, 16 * 5)
            dve.wait_ge(ln_rows, T)
            dve.sem_inc(l0_free_a, 1)
            nc.vector.tensor_tensor(x[:], x[:], bout[:].unsqueeze(1).broadcast_to([P, T, D]), ALU.add).then_inc(l0_added, 1)
            for t in range(2):
                l0_max_dve(dve, link, 0, t)
            with dve.Fori(0, L0_LOOP) as h:
                link.enter(h, 5)
                l0_head_dve(dve, link, h, False)
            link.leave(L0_LOOP)
            for h in range(L0_LOOP, H0):
                l0_head_dve(dve, link, h, h == H0 - 1)

        def l0_exp_act(act, h, t):
            act.wait_ge(l0_negmax, T * h + (t + 1))
            nc.scalar.activation(probs[:, t % 2, :].rearrange("p (b k) -> p b k", b=2), PS[:, 2 * (t % 2):2 * (t % 2) + 2, :],
                                 ACT.Exp, bias=neg_max[:, t:t + 1], scale=S0,
                                 accum_out=row_sum[:, t:t + 1]).then_inc(l0_probs, 1)

        def l0_head_act(act, h, last):
            for t in range(T):
                act.wait_ge(l0_turned, 2 * T * h + (2 * t + 2))
                act_copy(probsT[:, 4:8, t * P:(t + 1) * P], quarters(5)).then_inc(l0_free_b, 1)
                if t < 2:
                    l4_early_act(act, h, t)
                if t < T - 2:
                    l0_exp_act(act, h, t + 2)
                if t == 1 and not last:
                    act.wait_ge(l0_query, h + 2)
                    act_copy(T_head[:], bank(7)[0:C, :]).then_inc(l0_T, 1)
            if not last:
                l0_exp_act(act, h + 1, 0)
            act.wait_ge(l0_mixed, 2 * h + 2)
            act_copy(mixT[:], bank(6)[0:C, :]).then_inc(l0_mixT, 1)
            if not last:
                l0_exp_act(act, h + 1, 1)

        def l0_act(act):
            act.sem_inc(l0_free_b, 1)
            fold_wv_copy(act, act_copy, 1, fold_act)
            act.wait_ge(l0_query, 1)
            act_copy(T_head[:], bank(7)[0:C, :]).then_inc(l0_T, 1)
            fold_M_copy(act, act_copy, 1, fold_act)
            for t in range(2):
                l0_exp_act(act, 0, t)
            with act.Fori(0, L0_LOOP) as h:
                l0_head_act(act, h, False)
            for h in range(L0_LOOP, H0):
                l0_head_act(act, h, h == H0 - 1)

        def l0_pool(pool):
            pool.wait_ge(fold_dve, 4)
            pool.wait_ge(fold_act, 4)
            nc.gpsimd.tensor_copy(A_head[:], A_all[:, 0, :]).then_inc(l0_A, 1)
            with pool.Fori(1, H0) as h:
                pool.wait_ge(l0_query, h)
                nc.gpsimd.tensor_copy(A_head[:], A_all[:, bass.ds(h, 1), :].rearrange("p a c -> p (a c)")).then_inc(l0_A, 1)

        rev = sb("rev", [P, T, 16])
        logits = sb("logits", [P, T, 16])
        shifted = sb("shifted", [P, T, 16])
        gate = sb("gate", [P, T, 16])
        left = sb("left", [P, T, 16])
        equal = sb("equal", [P, T, 16])
        first = sb("first", [P, T, 16])
        second = sb("second", [P, T, 16])
        chosen = sb("chosen", [P, T, 16])
        comb = sb("comb", [P, T, 16])
        most = sb("most", [P, T])
        peak = sb("peak", [P, T])
        total = sb("total", [P, T])
        total2 = sb("total2", [P, T])
        constants = sem("constants")
        router_logits = sem("router_logits")
        comb_parts = sem("comb_parts")
        comb_parts_ps = sem("comb_parts_ps")
        comb_rows = sem("comb_rows")
        gate_shifted = sem("gate_shifted")
        gate_exp = sem("gate_exp")

        def rev_pool():
            for e in range(16):
                ins = nc.gpsimd.memset(rev[:, :, e], 16.0 - e)
            ins.then_inc(constants, 1)

        def top2_dve(link, values, E):
            v = values
            for pick in (first, second):
                link(nc.vector.tensor_reduce(most[:], v[:, :, 0:E], X, ALU.max))
                link(nc.vector.tensor_tensor(equal[:, :, 0:E], v[:, :, 0:E], wide(most[:], E), ALU.is_equal))
                link(nc.vector.tensor_tensor(equal[:, :, 0:E], equal[:, :, 0:E], rev[:, :, 0:E], ALU.mult))
                link(nc.vector.tensor_reduce(most[:], equal[:, :, 0:E], X, ALU.max))
                link(nc.vector.tensor_tensor(pick[:, :, 0:E], equal[:, :, 0:E], wide(most[:], E), ALU.is_equal))
                if pick is first:
                    link(nc.vector.scalar_tensor_tensor(out=left[:, :, 0:E], in0=first[:, :, 0:E], scalar=-BIG,
                                                        in1=v[:, :, 0:E], op0=ALU.mult, op1=ALU.add))
                    v = left
            link(nc.vector.tensor_tensor(chosen[:, :, 0:E], first[:, :, 0:E], second[:, :, 0:E], ALU.add))

        def shift_dve(link, values, E):
            link(nc.vector.tensor_reduce(peak[:], values[:, :, 0:E], X, ALU.max))
            nc.vector.tensor_tensor(shifted[:, :, 0:E], values[:, :, 0:E], wide(peak[:], E), ALU.subtract).then_inc(gate_shifted, 1)

        def gate_act(act, n, E):
            act.wait_ge(gate_shifted, n)
            nc.scalar.activation(gate[:, :, 0:E], shifted[:, :, 0:E], ACT.Exp).then_inc(gate_exp, 1)

        def weights_dve(link, E, eps_of_all=0.0, eps=0.0):
            link(nc.vector.tensor_tensor(comb[:, :, 0:E], gate[:, :, 0:E], chosen[:, :, 0:E], ALU.mult))
            link(nc.vector.tensor_reduce(total[:], comb[:, :, 0:E], X, ALU.add))
            if eps_of_all:
                link(nc.vector.tensor_reduce(total2[:], gate[:, :, 0:E], X, ALU.add))
                link(nc.vector.scalar_tensor_tensor(out=total[:], in0=total2[:], scalar=eps_of_all, in1=total[:],
                                                    op0=ALU.mult, op1=ALU.add))
            if eps:
                link(nc.vector.tensor_scalar(total[:], total[:], eps, None, ALU.add))
            link(nc.vector.reciprocal(total[:], total[:]))
            link(nc.vector.tensor_tensor(comb[:, :, 0:E], comb[:, :, 0:E], wide(total[:], E), ALU.mult))

        E1 = 8
        we = place_weights(5888, [P, E1, D])
        weT = place_weights(6912, [P, E1, D])
        wg1 = sb("wg1", [P, E1])
        bg1 = sb("bg1", [P, E1])
        be1 = sb("be1", [E1, D])
        combT = sb("combT", [16, N])
        l1_we_turned = sem("l1_we_turned")
        l1_weT = sem("l1_weT")
        l1_comb = sem("l1_comb")
        l1_combT_ps = sem("l1_combT_ps")
        l1_combT = sem("l1_combT")
        l1_bias = sem("l1_bias")
        l1_y = sem("l1_y")
        l1_used = sem("l1_used")
        l1_added = sem("l1_added")

        def l1_prepare_pe(pe):
            pe.wait_ge(early_loaded, 16 * 15)
            for half in range(2):
                for q in range(4):
                    ins = nc.tensor.transpose(bank(half)[:, q * P:(q + 1) * P], we[:, 4 * half + q, :], ident[:])
                ins.then_inc(l1_we_turned, 1)

        def l1_prepare_act(act):
            for half in range(2):
                act.wait_ge(l1_we_turned, half + 1)
                act_copy(weT[:, 4 * half:4 * half + 4, :], quarters(half)).then_inc(l1_weT, 1)

        def l1_pe(pe):
            pe.wait_ge(ln_xT, 2)
            for t in range(T):
                ins = nc.tensor.matmul(bank(6)[:, t * E1:(t + 1) * E1], xT[:, t * P:(t + 1) * P], wg1[:], start=True, stop=True)
            ins.then_inc(router_logits, 1)
            pe.wait_ge(l1_weT, 2)
            for g in range(6):
                half, t = g // T, g % T
                nc.tensor.matmul(bank(g), xT[:, t * P:(t + 1) * P], weT[:, 4 * half:4 * half + 4, :],
                                 start=True, stop=True).then_inc(l1_y, 1)
            pe.wait_ge(l1_comb, 1)
            for t in range(T):
                ins = nc.tensor.transpose(bank(6)[0:E1, t * P:(t + 1) * P], comb[:, t, 0:E1], ident[:])
            ins.then_inc(l1_combT_ps, 1)
            pe.wait_ge(l1_combT, 1)
            for t in range(T):
                ins = nc.tensor.matmul(bank(7)[:, t * P:(t + 1) * P], combT[0:E1, t * P:(t + 1) * P], be1[:], start=True, stop=True)
            ins.then_inc(l1_bias, 1)
            for g in (6, 7):
                pe.wait_ge(l1_used, 1)
                nc.tensor.matmul(bank(g - 6), xT[:, (g % T) * P:(g % T + 1) * P], weT[:, 4:8, :],
                                 start=True, stop=True).then_inc(l1_y, 1)

        def l1_dve(dve, link):
            dve.wait_ge(early_loaded, 16 * 15)
            dve.wait_ge(constants, 1)
            dve.wait_ge(router_logits, 1)
            link(nc.vector.tensor_tensor(logits[:, :, 0:E1], bank(6)[:, 0:T * E1].rearrange("p (t e) -> p t e", t=T),
                                         bg1[:].unsqueeze(1).broadcast_to([P, T, E1]), ALU.add))
            shift_dve(link, logits, E1)
            dve.wait_ge(gate_exp, 1)
            top2_dve(link, gate, E1)
            weights_dve(link, E1)
            dve.sem_inc(l1_comb, 1)
            dve.wait_ge(l1_bias, 1)
            link(nc.vector.tensor_tensor(x[:], x[:], quarters(7), ALU.add))
            for e in range(E1):
                half, q = e // 4, e % 4
                for t in range(T):
                    g = T * half + t
                    dve.wait_ge(l1_y, g + 1)
                    ins = nc.vector.scalar_tensor_tensor(out=x[:, t, :], in0=quarters(g % 6)[:, q, :], scalar=comb[:, t, e:e + 1],
                                                         in1=x[:, t, :], op0=ALU.mult, op1=ALU.add)
                    if e == E1 - 1:
                        ins.then_inc(x_updated, 1)
                if e == 3:
                    ins.then_inc(l1_used, 1)
                    dve.wait_ge(l1_used, 1)
                elif e < E1 - 1:
                    link(ins)

        def l1_act(act):
            act.wait_ge(l1_combT_ps, 1)
            act_copy(combT[0:E1, :], bank(6)[0:E1, :]).then_inc(l1_combT, 1)

        S2 = float(D) ** -0.5
        wq2 = sb("wq2", [P, D])
        wk2 = sb("wk2", [C, D])
        wv2 = sb("wv2", [C, D])
        bq2 = sb("bq2", [P, 1])
        bk2 = sb("bk2", [P, 1])
        bv2 = sb("bv2", [P, D])
        queryT = sb("queryT", [P, N])
        keyT = place(4096, [P, M])
        value = place(5120, [P, MT, D])
        att = place(0, [P, T, KB])
        attT = place(2048, [P, T, KB]).rearrange("p t (k q) -> p t k q", q=P)
        l2_kv_ps = sem("l2_kv_ps")
        l2_keyT = sem("l2_keyT")
        l2_value = sem("l2_value")
        l2_query_ps = sem("l2_query_ps")
        l2_query = sem("l2_query")
        att_scores = sem("att_scores")
        att_negmax = sem("att_negmax")
        att_exp = sem("att_exp")
        att_ready = sem("att_ready")
        att_turned = sem("att_turned")
        att_copied = sem("att_copied")
        att_out = sem("att_out")

        def l2_prepare_pe(pe):
            pe.wait_ge(early_loaded, 16 * 15)
            pe.wait_ge(x_updated, 2 * T)
            for half in range(2):
                nc.tensor.matmul(bank(2 + half), wk2[:], ctxT[:, half * 512:(half + 1) * 512],
                                 start=True, stop=True).then_inc(l2_kv_ps, 1)
            for half in range(2):
                for q in range(4):
                    k = 4 * half + q
                    ins = nc.tensor.matmul(bank(4 + half)[:, q * P:(q + 1) * P], ctxT[:, k * P:(k + 1) * P], wv2[:],
                                           start=True, stop=True)
                ins.then_inc(l2_kv_ps, 1)

        def l2_prepare_act(act):
            act.wait_ge(early_loaded, 16 * 15)
            for half in range(2):
                act.wait_ge(l2_kv_ps, half + 1)
                nc.scalar.activation(keyT[:, half * 512:(half + 1) * 512], bank(2 + half), ACT.Identity,
                                     bias=bk2[:]).then_inc(l2_keyT, 1)

        def l2_prepare_dve(dve):
            dve.wait_ge(early_loaded, 16 * 15)
            for half in range(2):
                dve.wait_ge(l2_kv_ps, half + 3)
                nc.vector.tensor_tensor(value[:, 4 * half:4 * half + 4, :], quarters(4 + half),
                                        bv2[:].unsqueeze(1).broadcast_to([P, 4, D]), ALU.add).then_inc(l2_value, 1)

        def att_scores_pe(pe, n, qT, kT, keys):
            for t in range(T):
                b = t // 2
                nc.tensor.matmul(bank(t)[:, 0:keys], qT[:, t * P:(t + 1) * P], kT[:, b * keys:(b + 1) * keys],
                                 start=True, stop=True).then_inc(att_scores, 1)

        def att_turn_pe(pe, n, t, keys, ready, count):
            pe.wait_ge(ready, count + t + 1)
            if T * n + t >= 2:
                pe.wait_ge(att_copied, T * n + t - 1)
            for k in range(keys // P):
                ins = nc.tensor.transpose(bank(4 + t % 2)[:, k * P:(k + 1) * P], att[:, t, k * P:(k + 1) * P], ident[:])
            ins.then_inc(att_turned, 1)

        def att_out_pe(pe, n, t, keys, v):
            pe.wait_ge(att_copied, T * n + t + 1)
            K = keys // P
            for k in range(K):
                ins = nc.tensor.matmul(bank(6)[:, t * P:(t + 1) * P], attT[:, t, k, :], v[:, K * (t // 2) + k, :],
                                       start=(k == 0), stop=(k == K - 1))
            ins.then_inc(att_out, 1)

        def att_max_dve(dve, link, n, t, keys, scale):
            dve.wait_ge(att_scores, T * n + t + 1)
            link(nc.vector.tensor_reduce(row_max[:, t:t + 1], bank(t)[:, 0:keys], X, ALU.max))
            nc.vector.tensor_scalar(neg_max[:, t:t + 1], row_max[:, t:t + 1], -scale, None, ALU.mult).then_inc(att_negmax, 1)

        def att_copy_dve(dve, n, t, keys):
            dve.wait_ge(att_turned, T * n + t + 1)
            nc.vector.tensor_copy(attT[:, t, 0:keys // P, :], bank(4 + t % 2)[:, 0:keys].rearrange("p (k q) -> p k q", q=P)).then_inc(att_copied, 1)

        def att_exp_act(act, n, keys, scale):
            for t in range(T):
                act.wait_ge(att_negmax, T * n + t + 1)
                nc.scalar.activation(att[:, t, 0:keys], bank(t)[:, 0:keys], ACT.Exp, bias=neg_max[:, t:t + 1], scale=scale,
                                     accum_out=row_sum[:, t:t + 1]).then_inc(att_exp, 1)

        def l2_pe(pe):
            pe.wait_ge(ln_xT, 3)
            nc.tensor.matmul(bank(6), wq2[:], xT[:], start=True, stop=True).then_inc(l2_query_ps, 1)
            pe.wait_ge(l2_keyT, 2)
            pe.wait_ge(l2_value, 2)
            pe.wait_ge(l2_query, 1)
            att_scores_pe(pe, 0, queryT, keyT, KB)
            for t in range(T):
                att_turn_pe(pe, 0, t, KB, att_exp, 0)
                if t >= 1:
                    att_out_pe(pe, 0, t - 1, KB, value)
            att_out_pe(pe, 0, T - 1, KB, value)

        def l2_act(act):
            act.wait_ge(l2_query_ps, 1)
            nc.scalar.activation(queryT[:], bank(6), ACT.Identity, bias=bq2[:]).then_inc(l2_query, 1)
            att_exp_act(act, 0, KB, S2)

        def l2_dve(dve, link):
            for t in range(T):
                att_max_dve(dve, link, 0, t, KB, S2)
            for t in range(T):
                att_copy_dve(dve, 0, t, KB)
            link(nc.vector.reciprocal(row_inv[:], row_sum[:]))
            dve.wait_ge(att_out, T)
            for t in range(T):
                nc.vector.scalar_tensor_tensor(out=x[:, t, :], in0=quarters(6)[:, t, :], scalar=row_inv[:, t:t + 1],
                                               in1=x[:, t, :], op0=ALU.mult, op1=ALU.add).then_inc(x_updated, 1)

        E3 = 8
        H3 = 256
        room2 = sb("room2", [P, 8192])
        w1 = room2[:, 0:4096].rearrange("p (e c d) -> p e c d", e=E3, c=4)
        w1T = room2[:, 4096:8192].rearrange("p (e h) -> p e h", e=E3)
        wg3 = sb("wg3", [E3, D])
        wg3T = sb("wg3T", [P, E3])
        wo3 = sb("wo3", [P, H3])
        wo3T = sb("wo3T", [P, 2, D])
        bo3 = sb("bo3", [P, D])
        b1 = sb("b1", [E3, 2 * H3])
        b1_hi = sb("b1_hi", [E3, 2 * H3], BF16)
        b1_mid = sb("b1_mid", [E3, 2 * H3], BF16)
        b1_lo = sb("b1_lo", [E3, 2 * H3], BF16)
        b1_rows = sb("b1_rows", [3, E3, 2 * H3], BF16)
        ones3 = sb("ones3", [3, P], BF16)
        sig = place(4096, [P, T, H3])
        gated = place(5120, [P, T, H3])
        mixed = place(6144, [P, T, H3])
        mixedT = place(7168, [P, 2, N])
        l3_b1_parts = sem("l3_b1_parts")
        l3_b1_rows = sem("l3_b1_rows")
        l3_w_turned = sem("l3_w_turned")
        l3_w = sem("l3_w")
        l3_hidden = sem("l3_hidden")
        l3_sig = sem("l3_sig")
        l3_used = sem("l3_used")
        l3_mixed = sem("l3_mixed")
        l3_turned = sem("l3_turned")
        l3_mixedT = sem("l3_mixedT")
        l3_out = sem("l3_out")

        def l3_parts_dve(dve, link):
            dve.wait_ge(early_loaded, 16 * 15)
            link(nc.vector.tensor_copy(b1_hi[:], b1[:]))
            link(nc.vector.tensor_tensor(b1[:], b1[:], b1_hi[:], ALU.subtract))
            link(nc.vector.tensor_copy(b1_mid[:], b1[:]))
            link(nc.vector.tensor_tensor(b1[:], b1[:], b1_mid[:], ALU.subtract))
            nc.vector.memset(ones3[:], 1.0)
            nc.vector.tensor_copy(b1_lo[:], b1[:]).then_inc(l3_b1_parts, 1)

        def l3_prepare_pe(pe):
            pe.wait_ge(early_loaded, 16 * 15)
            pe.wait_ge(x_updated, 3 * T)
            nc.tensor.transpose(bank(4)[:, 0:E3], wg3[:], ident[0:E3, 0:E3])
            for k in range(2):
                ins = nc.tensor.transpose(bank(4)[:, (k + 1) * P:(k + 2) * P], wo3[:, k * P:(k + 1) * P], ident[:])
            ins.then_inc(l3_w_turned, 1)
            for e in range(E3):
                if e >= 4:
                    pe.wait_ge(l3_w, 2 + e - 3)
                for c in range(4):
                    ins = nc.tensor.transpose(bank(e % 4)[:, c * P:(c + 1) * P], w1[:, e, c, :], ident[:])
                ins.then_inc(l3_w_turned, 1)

        def l3_prepare_act(act):
            act.wait_ge(l3_w_turned, 1)
            act_copy(wg3T[:], bank(4)[:, 0:E3]).then_inc(l3_w, 1)
            act_copy(wo3T[:], bank(4)[:, P:3 * P].rearrange("p (k d) -> p k d", k=2)).then_inc(l3_w, 1)
            for e in range(E3):
                act.wait_ge(l3_w_turned, e + 2)
                act_copy(w1T[:, e, :], bank(e % 4)).then_inc(l3_w, 1)

        def l3_pe(pe):
            pe.wait_ge(ln_xT, 4)
            pe.wait_ge(l3_w, 2 + E3)
            for t in range(T):
                ins = nc.tensor.matmul(bank(6)[:, t * E3:(t + 1) * E3], xT[:, t * P:(t + 1) * P], wg3T[:], start=True, stop=True)
            ins.then_inc(router_logits, 1)
            pe.wait_ge(l3_b1_rows, 16 * 3)
            with pe.Fori(0, E3) as e:
                for t in range(T):
                    pe.wait_ge(l3_used, T * e + (t + 1))
                    nc.tensor.matmul(bank(t), xT[:, t * P:(t + 1) * P], w1T[:, bass.ds(e, 1), :], start=True, stop=False)
                    nc.tensor.matmul(bank(t), ones3[:], b1_rows[:, bass.ds(e, 1), :], start=False, stop=True).then_inc(l3_hidden, 1)
            for k in range(2):
                for t in range(T):
                    pe.wait_ge(l3_mixed, T * E3 + t + 1)
                    ins = nc.tensor.transpose(bank(4 + k)[:, t * P:(t + 1) * P], mixed[:, t, k * P:(k + 1) * P], ident[:])
                ins.then_inc(l3_turned, 1)
            pe.wait_ge(l3_mixedT, 2)
            for t in range(T):
                for k in range(2):
                    ins = nc.tensor.matmul(bank(6)[:, t * P:(t + 1) * P], mixedT[:, k, t * P:(t + 1) * P], wo3T[:, k, :],
                                           start=(k == 0), stop=(k == 1))
            ins.then_inc(l3_out, 1)

        def l3_act(act):
            with act.Fori(0, E3) as e:
                for t in range(T):
                    act.wait_ge(l3_hidden, T * e + (t + 1))
                    nc.scalar.activation(sig[:, t, :], bank(t)[:, H3:2 * H3], ACT.Sigmoid).then_inc(l3_sig, 1)
            for k in range(2):
                act.wait_ge(l3_turned, k + 1)
                act_copy(mixedT[:, k, :], bank(4 + k)).then_inc(l3_mixedT, 1)

        def l3_dve(dve, link):
            dve.sem_inc(l3_used, T)
            for t in range(T):
                nc.vector.memset(mixed[:, t, :], 0.0).then_inc(l3_mixed, 1)
            dve.wait_ge(router_logits, 2)
            link(nc.vector.tensor_copy(logits[:, :, 0:E3], bank(6)[:, 0:T * E3].rearrange("p (t e) -> p t e", t=T)))
            shift_dve(link, logits, E3)
            dve.wait_ge(gate_exp, 2)
            top2_dve(link, gate, E3)
            weights_dve(link, E3, eps_of_all=1e-9)
            link(nc.vector.tensor_reduce(total[:], comb[:, :, 0:E3], X, ALU.add))
            for t in range(T):
                ins = nc.vector.scalar_tensor_tensor(out=x[:, t, :], in0=bo3[:], scalar=total[:, t:t + 1], in1=x[:, t, :],
                                                     op0=ALU.mult, op1=ALU.add)
            link(ins)
            with dve.Fori(0, E3) as e:
                for t in range(T + 1):
                    if t < T:
                        dve.wait_ge(l3_sig, T * e + (t + 1))
                        nc.vector.tensor_tensor(gated[:, t, :], bank(t)[:, 0:H3], sig[:, t, :], ALU.mult).then_inc(l3_used, 1)
                    if t >= 1:
                        u = t - 1
                        dve.wait_ge(l3_used, T * e + (T + u + 1))
                        dve.wait_ge(l3_mixed, T * e + (u + 1))
                        nc.vector.scalar_tensor_tensor(out=mixed[:, u, :], in0=gated[:, u, :], scalar=comb[:, u, bass.ds(e, 1)],
                                                       in1=mixed[:, u, :], op0=ALU.mult, op1=ALU.add).then_inc(l3_mixed, 1)
            dve.wait_ge(l3_out, 1)
            for t in range(T):
                nc.vector.tensor_tensor(x[:, t, :], x[:, t, :], quarters(6)[:, t, :], ALU.add).then_inc(x_updated, 1)

        S4 = float(D) ** -0.5
        F4 = 512
        D2V, IMG, TXT, ATT0, ATT1, FF1, FF2 = range(7)
        wd4 = sb("wd4", [P, C])
        wi4 = sb("wi4", [P, D])
        wt4 = sb("wt4", [P, D])
        wa4 = sb("wa4", [64, 2, D])
        wf14 = sb("wf14", [P, 4, 2 * D])
        wf24 = sb("wf24", [P, F4])
        bd4 = sb("bd4", [P, 1])
        bi4 = sb("bi4", [P, 1])
        bt4 = sb("bt4", [P, 1])
        ba4 = sb("ba4", [P, 2])
        ba4_rows = sb("ba4_rows", [P, 2, 64])
        bf14 = sb("bf14", [P, 4])
        bf24 = sb("bf24", [P, D])
        below = place(9728, [P, 4 * 2 * D])
        td4 = sb("td4", [P, C], BF16)
        ti4 = sb("ti4", [P, D], BF16)
        tt4 = sb("tt4", [P, D], BF16)
        ta4 = sb("ta4", [64, 2, D], BF16)
        tf14 = sb("tf14", [P, 4, 2 * D], BF16)
        tf24 = sb("tf24", [P, F4], BF16)
        tdT = sb("tdT", [C, D], BF16)
        tiT = sb("tiT", [P, D], BF16)
        ttT = sb("ttT", [P, D], BF16)
        taT = sb("taT", [P, 2, 2, 64], BF16)
        tf1T = sb("tf1T", [P, 2, F4], BF16)
        tf2T = sb("tf2T", [P, 4, D], BF16)
        abs_sum = sb("abs_sum", [P, 7])
        one_over = sb("one_over", [P, 7])
        ones = sb("ones", [P, P])
        w_scale = sb("w_scale", [P, 7])
        w_above = sb("w_above", [P, 7])
        w_below = sb("w_below", [P, 7])
        part_max = sb("part_max", [P, 8])
        whole_max = sb("whole_max", [P, 8])
        i_scale = sb("i_scale", [P, 8])
        i_inv = sb("i_inv", [P, 8])
        both = sb("both", [P, 8])
        rounded = place(4096, [P, 4 * N])
        ints = sb("ints", [P, 4 * N], BF16)
        rounded_ctx = place(7168, [P, M])
        ctx_feat = place(6144, [P, M])
        key4 = room2[:, 0:2048].rearrange("p (l k) -> p l k", l=2)
        value4 = room2[:, 2048:4096].rearrange("p (l k d) -> p l k d", l=2, d=D)
        cat = sb("cat", [P, N + B])
        hid4 = place(6144, [P, 4, N])
        l4_loaded = sem("l4_loaded")
        l4_ba = sem("l4_ba")
        l4_sums = sem("l4_sums")
        l4_sums_ps = sem("l4_sums_ps")
        l4_ternary = sem("l4_ternary")
        l4_w_turned = sem("l4_w_turned")
        l4_wT = sem("l4_wT")
        l4_part_max = sem("l4_part_max")
        l4_whole_max = sem("l4_whole_max")
        l4_ints = sem("l4_ints")
        l4_both = sem("l4_both")
        l4_ps = sem("l4_ps")
        l4_feat = sem("l4_feat")
        l4_value = sem("l4_value")
        l4_fused = sem("l4_fused")

        def l4_const_pool():
            for j, size in ((D2V, D * C), (IMG, D * D), (TXT, D * D), (ATT0, 64 * D), (ATT1, 64 * D), (FF1, F4 * 2 * D), (FF2, D * F4)):
                nc.gpsimd.memset(one_over[:, j:j + 1], 1.0 / size)
            nc.gpsimd.memset(abs_sum[:], 0.0)
            nc.gpsimd.memset(part_max[:], 0.0)
            nc.gpsimd.memset(ones[:], 1.0).then_inc(constants, 1)

        def ternary(link, w, q, j, rows, size):
            link(nc.vector.tensor_scalar(below[0:rows, 0:size], w, w_below[0:rows, j:j + 1], None, ALU.is_lt))
            link(nc.vector.scalar_tensor_tensor(out=q, in0=w, scalar=w_above[0:rows, j:j + 1], in1=below[0:rows, 0:size],
                                                op0=ALU.is_gt, op1=ALU.subtract))

        def l4_sums_dve(weights):
            for w, j in weights:
                axis = mybir.AxisListType.XY if w is wf14 else X
                ins = nc.vector.tensor_reduce(abs_sum[:, j:j + 1], w[:], axis, ALU.add, apply_absolute_value=True)
            return ins

        def l4_early_dve(dve, link, h, window):
            step = (h, window) if isinstance(h, int) else None
            if step == (3, 1):
                dve.wait_ge(l4_loaded, 16 * 17)
                dve.wait_ge(constants, 2)
                abs_max_dve(0, ctxT[:], rows=C)
                l4_sums_dve(((wd4, D2V), (wi4, IMG), (wt4, TXT)))
            elif step == (3, 2):
                l4_sums_dve(((wf24, FF2), (wf14, FF1)))
                nc.vector.tensor_reduce(abs_sum[0:64, ATT0:ATT1 + 1], wa4[:], X, ALU.add, apply_absolute_value=True).then_inc(l4_sums, 1)
            elif step == (4, 0):
                dve.wait_ge(l4_sums_ps, 1)
                link(nc.vector.tensor_tensor(w_scale[:], bank(7)[:, 0:7], one_over[:], ALU.mult))
                dve.sem_inc(l4_ternary, 1)
                link(nc.vector.tensor_scalar(w_scale[:], w_scale[:], 1e-5, None, ALU.max))
                link(nc.vector.tensor_scalar(w_above[:], w_scale[:], 0.5, None, ALU.mult))
                link(nc.vector.tensor_scalar(w_below[:], w_scale[:], -0.5, None, ALU.mult))
            elif step == (4, 1):
                ternary(link, wd4[:], td4[:], D2V, P, C)
                ternary(link, wi4[:], ti4[:], IMG, P, D)
                ternary(link, wt4[:], tt4[:], TXT, P, D)
            elif step == (4, 2):
                for l in range(2):
                    ternary(link, wa4[:, l, :], ta4[:, l, :], ATT0 + l, 64, D)
                ternary(link, wf24[:], tf24[:], FF2, P, F4)
                dve.sem_inc(l4_ternary, 1)
            elif step == (5, 1):
                ternary(link, wf14[:].rearrange("p c i -> p (c i)"), tf14[:].rearrange("p c i -> p (c i)"), FF1, P, 4 * 2 * D)
                dve.sem_inc(l4_ternary, 1)
            elif step == (5, 2):
                scale_dve(dve, link, 0, D2V)
                ints_dve(link, 0, ctxT[:], M, rows=C, work=rounded_ctx)
            elif step == (6, 1):
                dve.wait_ge(l4_feat, 2)
                abs_max_dve(1, ctx_feat[:])
            elif step == (6, 2):
                scale_dve(dve, link, 1, IMG)
                ints_dve(link, 1, ctx_feat[:], M, work=rounded_ctx)
            elif step == (7, 1):
                dve.wait_ge(l4_feat, 4)
                abs_max_dve(2, ctx_feat[:])
                link(nc.vector.tensor_reduce(cat[:, N:N + B], ctx_feat[:].rearrange("p (b k) -> p b k", b=B), X, ALU.add))
                link(nc.vector.tensor_scalar(cat[:, N:N + B], cat[:, N:N + B], 1.0 / KB, None, ALU.mult))
            elif step == (7, 2):
                scale_dve(dve, link, 2, ATT0)
                nc.vector.tensor_tensor(both[:, 6:7], i_scale[:, 2:3], w_scale[:, ATT1:ATT1 + 1], ALU.mult).then_inc(l4_both, 1)
                ints_dve(link, 2, ctx_feat[:], M, work=rounded_ctx)

        def l4_early_pe(pe, h, point):
            step = (h, point) if isinstance(h, int) else None
            if step == (4, 0):
                pe.wait_ge(l4_sums, 1)
                nc.tensor.matmul(bank(7)[:, 0:7], ones[:], abs_sum[:], start=True, stop=True).then_inc(l4_sums_ps, 1)
            elif step == (4, 2):
                pe.wait_ge(l4_ternary, 1)
            elif step == (5, 0):
                pe.wait_ge(l4_ternary, 2)
                b7 = bank(7).bitcast(BF16)
                nc.tensor.transpose(b7[0:C, 0:P], td4[:], identb[:])
                nc.tensor.transpose(b7[:, P:2 * P], ti4[:], identb[:])
                nc.tensor.transpose(b7[:, 2 * P:3 * P], tt4[:], identb[:])
                for l in range(2):
                    nc.tensor.transpose(b7[:, 3 * P + 64 * l:3 * P + 64 * (l + 1)], ta4[:, l, :], identb[0:64, 0:64])
                for c in range(4):
                    ins = nc.tensor.transpose(b7[:, (4 + c) * P:(5 + c) * P], tf24[:, c * P:(c + 1) * P], identb[:])
                ins.then_inc(l4_w_turned, 1)
            elif step == (5, 2):
                pe.wait_ge(l4_wT, 1)
            elif step == (6, 2):
                pe.wait_ge(l4_feat, 2)
            elif step in ((6, 0), (6, 1), (7, 0), (7, 1)):
                n = 2 * (h - 6) + point
                w, rows = ((tdT, C), (tiT, P))[n // 2]
                pe.wait_ge(l4_ints, n // 2 + 1)
                if n > 0:
                    pe.wait_ge(l4_feat, n)
                half = n % 2
                nc.tensor.matmul(bank(7), w[:], ints[0:rows, half * 512:(half + 1) * 512], start=True, stop=True).then_inc(l4_ps, 1)

        def l4_early_act(act, h, point):
            step = (h, point) if isinstance(h, int) else None
            if step == (5, 0):
                act.wait_ge(l4_w_turned, 1)
                b7 = bank(7).bitcast(BF16)
                act_copy(tdT[:], b7[0:C, 0:P])
                act_copy(tiT[:], b7[:, P:2 * P])
                act_copy(ttT[:], b7[:, 2 * P:3 * P])
                for copy in range(2):
                    act_copy(taT[:, :, copy, :], b7[:, 3 * P:4 * P].rearrange("p (l o) -> p l o", l=2))
                act_copy(tf2T[:], b7[:, 4 * P:8 * P].rearrange("p (c o) -> p c o", c=4)).then_inc(l4_wT, 1)
            elif step in ((6, 0), (6, 1), (7, 0), (7, 1)):
                n = 2 * (h - 6) + point
                act.wait_ge(l4_ps, n + 1)
                act.wait_ge(l4_both, n // 2 + 1)
                half = n % 2
                nc.scalar.activation(ctx_feat[:, half * 512:(half + 1) * 512], bank(7), ACT.Identity,
                                     bias=(bd4, bi4)[n // 2][:], scale=both[:, n // 2:n // 2 + 1]).then_inc(l4_feat, 1)

        def scale_dve(dve, link, n, weight):
            dve.wait_ge(l4_whole_max, n + 1)
            link(nc.vector.tensor_scalar(i_scale[:, n:n + 1], whole_max[:, n:n + 1], 1e-8, 1.0 / 127.0, ALU.max, ALU.mult))
            link(nc.vector.reciprocal(i_inv[:, n:n + 1], i_scale[:, n:n + 1]))
            nc.vector.tensor_tensor(both[:, n:n + 1], i_scale[:, n:n + 1], w_scale[:, weight:weight + 1], ALU.mult).then_inc(l4_both, 1)

        def ints_dve(link, n, src, size, rows=P, work=None):
            work = rounded if work is None else work
            link(nc.vector.tensor_scalar(work[0:rows, 0:size], src, i_inv[0:rows, n:n + 1], ROUND, ALU.mult, ALU.add))
            link(nc.vector.tensor_scalar(work[0:rows, 0:size], work[0:rows, 0:size], ROUND + 127.0, ROUND - 128.0, ALU.min, ALU.max))
            nc.vector.tensor_scalar(ints[0:rows, 0:size], work[0:rows, 0:size], ROUND, None, ALU.subtract).then_inc(l4_ints, 1)

        def abs_max_dve(n, src, rows=P, axis=X):
            nc.vector.tensor_reduce(part_max[0:rows, n:n + 1], src, axis, ALU.max, apply_absolute_value=True).then_inc(l4_part_max, 1)

        def whole_max_pool(pool, n):
            pool.wait_ge(l4_part_max, n + 1)
            nc.gpsimd.partition_all_reduce(whole_max[:, n:n + 1], part_max[:, n:n + 1], P, RMAX).then_inc(l4_whole_max, 1)

        def l4_ctx_dve(dve):
            for l in range(2):
                dve.wait_ge(l4_ps, 7 + l)
                for copy in range(2):
                    nc.vector.scalar_tensor_tensor(
                        out=value4[:, l, :, 64 * copy:64 * (copy + 1)], in0=bank(4 + l).rearrange("p (k o) -> p k o", k=MT),
                        scalar=both[:, (2, 6)[l]:(2, 6)[l] + 1],
                        in1=ba4_rows[:, l, :].unsqueeze(1).broadcast_to([P, MT, 64]), op0=ALU.mult, op1=ALU.add).then_inc(l4_value, 1)

        def l4_ctx_pe(pe):
            pe.wait_ge(x_updated, 4 * T)
            pe.wait_ge(l4_ints, 3)
            for l in range(2):
                for half in range(2):
                    ins = nc.tensor.matmul(bank(2 * l + half), taT[:, l, :, :], ints[:, half * 512:(half + 1) * 512], start=True, stop=True)
                ins.then_inc(l4_ps, 1)
            for l in range(2):
                for k in range(MT):
                    ins = nc.tensor.matmul(bank(4 + l)[:, k * 64:(k + 1) * 64], ints[:, k * P:(k + 1) * P], taT[:, l, 0, :], start=True, stop=True)
                ins.then_inc(l4_ps, 1)
            b6 = bank(6).bitcast(BF16)
            for half in range(2):
                for c in range(4):
                    ins = nc.tensor.transpose(b6[:, (4 * half + c) * P:(4 * half + c + 1) * P], tf14[:, c, half * P:(half + 1) * P], identb[:])
            ins.then_inc(l4_w_turned, 1)

        def l4_ctx_act(act):
            act.wait_ge(l4_both, 4)
            act.wait_ge(l4_ba, 16 * 4)
            for l in range(2):
                act.wait_ge(l4_ps, 5 + l)
                nc.scalar.activation(key4[:, l, :].rearrange("p (b k) -> p b k", b=2), PS[:, 2 * l:2 * l + 2, :], ACT.Identity,
                                     bias=ba4[:, l:l + 1], scale=both[:, (2, 6)[l]:(2, 6)[l] + 1]).then_inc(l4_feat, 1)
            act.wait_ge(l4_w_turned, 2)
            act_copy(tf1T[:], bank(6).bitcast(BF16).rearrange("p (h f) -> p h f", h=2)).then_inc(l4_wT, 1)

        def l4_dve(dve, link):
            dve.wait_ge(ln_xT, 5)
            abs_max_dve(3, xT[:])
            scale_dve(dve, link, 3, TXT)
            dve.wait_ge(l4_ps, 8)
            ints_dve(link, 3, xT[:], N)
            for l in range(2):
                n = l + 1
                for t in range(T):
                    att_max_dve(dve, link, n, t, KB, S4)
                for t in range(T):
                    dve.wait_ge(att_exp, T * n + t + 1)
                    link(nc.vector.reciprocal(row_inv[:, t:t + 1], row_sum[:, t:t + 1]))
                    nc.vector.tensor_scalar(att[:, t, :], att[:, t, :], row_inv[:, t:t + 1], 0.1, ALU.mult, ALU.mult).then_inc(att_ready, 1)
                for t in range(T):
                    att_copy_dve(dve, n, t, KB)
                dve.wait_ge(att_out, T * (n + 1))
                nc.vector.tensor_tensor(cat[:, 0:N], cat[:, 0:N], bank(6), ALU.add).then_inc(l4_fused, 1)
            dve.wait_ge(l4_fused, 2)
            abs_max_dve(4, cat[:])
            scale_dve(dve, link, 4, FF1)
            ints_dve(link, 4, cat[:], N + B)
            dve.wait_ge(l4_feat, 11)
            abs_max_dve(5, hid4[:], axis=mybir.AxisListType.XY)
            link(nc.vector.tensor_tensor(x[:], x[:], bf24[:].unsqueeze(1).broadcast_to([P, T, D]), ALU.add))
            scale_dve(dve, link, 5, FF2)
            ints_dve(link, 5, hid4[:].rearrange("p c n -> p (c n)"), 4 * N)
            dve.wait_ge(l4_both, 7)
            dve.wait_ge(l4_ps, 14)
            for t in range(T):
                nc.vector.scalar_tensor_tensor(out=x[:, t, :], in0=quarters(7)[:, t, :], scalar=both[:, 5:6], in1=x[:, t, :],
                                               op0=ALU.mult, op1=ALU.add).then_inc(x_updated, 1)

        def l4_pe(pe):
            pe.wait_ge(l4_ints, 4)
            pe.wait_ge(l4_wT, 2)
            nc.tensor.matmul(bank(7), ttT[:], ints[:, 0:N], start=True, stop=True).then_inc(l4_ps, 1)
            for l in range(2):
                n = l + 1
                if l == 0:
                    pe.wait_ge(l4_feat, 7)
                    pe.wait_ge(l4_value, 4)
                else:
                    pe.wait_ge(l4_fused, 1)
                att_scores_pe(pe, n, cat, key4[:, l, :], KB)
                for t in range(T):
                    att_turn_pe(pe, n, t, KB, att_ready, T * l)
                    if t >= 1:
                        l4_attended_pe(pe, n, l, t - 1)
                l4_attended_pe(pe, n, l, T - 1)
            pe.wait_ge(l4_ints, 5)
            for c in range(4):
                nc.tensor.matmul(bank(c), tf1T[:, 0, c * P:(c + 1) * P], ints[:, 0:N], start=True, stop=False)
                nc.tensor.matmul(bank(c), tf1T[:, 1, c * P:(c + 1) * P], wide(ints[:, N:N + B], N // B),
                                 start=False, stop=True).then_inc(l4_ps, 1)
            pe.wait_ge(l4_ints, 6)
            for t in range(T):
                for c in range(4):
                    ins = nc.tensor.matmul(bank(7)[:, t * P:(t + 1) * P], ints[:, c * N + t * P:c * N + (t + 1) * P], tf2T[:, c, :],
                                           start=(c == 0), stop=(c == 3))
            ins.then_inc(l4_ps, 1)

        def l4_attended_pe(pe, n, l, t):
            pe.wait_ge(att_copied, T * n + t + 1)
            K = KB // P
            for k in range(K):
                ins = nc.tensor.matmul(bank(6)[:, t * P:(t + 1) * P], value4[:, l, K * (t // 2) + k, :], attT[:, t, k, :],
                                       start=(k == 0), stop=(k == K - 1))
            ins.then_inc(att_out, 1)

        def l4_act(act):
            act.wait_ge(l4_ps, 9)
            act.wait_ge(l4_both, 5)
            nc.scalar.activation(cat[:, 0:N], bank(7), ACT.Identity, bias=bt4[:], scale=both[:, 3:4]).then_inc(l4_feat, 1)
            for l in range(2):
                att_exp_act(act, l + 1, KB, S4)
            act.wait_ge(l4_both, 6)
            for c in range(4):
                act.wait_ge(l4_ps, 10 + c)
                nc.scalar.activation(hid4[:, c, :], bank(c), ACT.Relu, bias=bf14[:, c:c + 1], scale=both[:, 4:5]).then_inc(l4_feat, 1)

        E5 = 16
        K5 = N // B
        S5 = float(D) ** -0.5
        proj5 = place_weights(0, [P, E5, 3 * D])
        oproj5 = place_weights(6144, [P, E5, D])
        sim5 = sb("sim5", [P, E5])
        squares5 = sb("squares5", [P, E5])
        norm5 = sb("norm5", [P, E5])
        gates5 = sb("gates5", [P, E5])
        xnorm5 = sb("xnorm5", [P, T])
        idle5 = sb("idle5", [P, T])
        parts5 = sb("parts5", [P, T, 3 * E5], BF16)
        comb5T = sb("comb5T", [P, N], BF16)
        pick5 = sb("pick5", [P, E5, P], BF16)
        scaled = place(4096, [P, 2, N])
        qkv5 = place(5120, [P, T, 3 * D])
        key5T = place(6656, [P, N])
        o5 = place(7168, [P, T, D])
        o5T = place(7680, [P, N])
        junk5 = place(8192, [P, T, D])
        l5_squares = sem("l5_squares")
        l5_norm_ps = sem("l5_norm_ps")
        l5_norm2 = sem("l5_norm2")
        l5_norm = sem("l5_norm")
        l5_gate = sem("l5_gate")
        l5_xsum = sem("l5_xsum")
        l5_xnorm = sem("l5_xnorm")
        l5_sim = sem("l5_sim")
        l5_weight = [sem("l5_weight"), sem("l5_weight_o")]
        l5_scaled = [sem("l5_scaled"), sem("l5_scaled_o")]
        l5_used = [sem("l5_used"), sem("l5_used_o")]
        l5_qkv = sem("l5_qkv")
        l5_qk_turned = sem("l5_qk_turned")
        l5_qk = sem("l5_qk")
        l5_o = sem("l5_o")
        l5_o_turned = sem("l5_o_turned")
        l5_oT = sem("l5_oT")

        def l5_const_pool(pool, link):
            link(nc.gpsimd.memset(pick5[:], 0.0))
            for k in range(3):
                link(nc.gpsimd.affine_select(out=pick5[:], in_=pick5[:], compare_op=ALU.not_equal, fill=1.0, base=-E5 * k,
                                             pattern=[[-1, E5], [0, P]], channel_multiplier=1))
            nc.gpsimd.memset(comb5T[:], 0.0).then_inc(constants, 1)

        def l5_sim_dve(dve, link):
            dve.wait_ge(late_loaded, 16 * 14)
            nc.vector.tensor_tensor(squares5[:], sim5[:], sim5[:], ALU.mult).then_inc(l5_squares, 1)
            dve.wait_ge(l5_norm_ps, 1)
            nc.vector.tensor_scalar(norm5[:], bank(5)[:, 0:E5], 1e-24, None, ALU.max).then_inc(l5_norm2, 1)
            dve.wait_ge(l5_gate, 1)
            link(nc.vector.tensor_scalar(gates5[:], gates5[:], 1.0, None, ALU.add))
            link(nc.vector.reciprocal(gates5[:], gates5[:]))
            dve.wait_ge(l5_norm, 1)
            nc.vector.tensor_tensor(sim5[:], sim5[:], norm5[:], ALU.mult).then_inc(l5_sim, 1)

        def l5_sim_pe(pe):
            pe.wait_ge(l5_squares, 1)
            pe.wait_ge(x_updated, 5 * T)
            nc.tensor.matmul(bank(5)[:, 0:E5], ones[:], squares5[:], start=True, stop=True).then_inc(l5_norm_ps, 1)

        def l5_sim_act(act):
            act.wait_ge(late_loaded, 16 * 14)
            nc.scalar.activation(gates5[:], gates5[:], ACT.Exp, scale=-1.0).then_inc(l5_gate, 1)

        def l5_norm_pool(pool):
            pool.wait_ge(l5_norm2, 1)
            nc.gpsimd.tensor_tensor(norm5[:], norm5[:], minus_half[:], ALU.pow).then_inc(l5_norm, 1)

        def l5_xnorm_pool(pool):
            pool.wait_ge(l5_xsum, 1)
            nc.gpsimd.tensor_tensor(xnorm5[:], xnorm5[:], minus_half[:, 0:T], ALU.pow).then_inc(l5_xnorm, 1)

        def l5_router_dve(dve, link):
            dve.wait_ge(ln_rows, 6 * T)
            link(nc.vector.tensor_tensor(junk5[:], xn[:], xn[:], ALU.mult))
            link(nc.vector.tensor_reduce(xnorm5[:], junk5[:], X, ALU.add))
            nc.vector.tensor_scalar(xnorm5[:], xnorm5[:], 1e-24, None, ALU.max).then_inc(l5_xsum, 1)
            dve.wait_ge(router_logits, 3)
            dve.wait_ge(l5_xnorm, 1)
            link(nc.vector.tensor_tensor(logits[:], bank(6)[:, 0:T * E5].rearrange("p (t e) -> p t e", t=T), wide(xnorm5[:], E5), ALU.mult))
            link(nc.vector.tensor_tensor(logits[:], logits[:], gates5[:].unsqueeze(1).broadcast_to([P, T, E5]), ALU.subtract))
            top2_dve(link, logits, E5)
            link(nc.vector.tensor_scalar(logits[:], logits[:], 0.0, None, ALU.max))
            shift_dve(link, logits, E5)
            link(nc.vector.tensor_scalar(equal[:], logits[:], 0.0, None, ALU.is_gt))
            link(nc.vector.tensor_reduce(total2[:], equal[:], X, ALU.add))
            link(nc.vector.tensor_scalar(idle5[:], total2[:], 0.0, None, ALU.is_equal))
            link(nc.vector.tensor_tensor(chosen[:], chosen[:], wide(idle5[:], E5), ALU.mult))
            link(nc.vector.tensor_tensor(chosen[:], chosen[:], equal[:], ALU.add))
            dve.wait_ge(gate_exp, 3)
            weights_dve(link, E5)
            for k in range(3):
                part = parts5[:, :, k * E5:(k + 1) * E5]
                link(nc.vector.tensor_copy(part, comb[:]))
                if k < 2:
                    link(nc.vector.tensor_tensor(comb[:], comb[:], part, ALU.subtract))
            dve.sem_inc(comb_parts, 1)
            dve.wait_ge(comb_parts_ps, 1)
            dve.wait_ge(constants, 3)
            nc.vector.tensor_copy(comb5T[0:3 * E5, :], bank(5).bitcast(BF16)[0:3 * E5, 0:N]).then_inc(comb_rows, 1)

        def l5_router_pe(pe):
            pe.wait_ge(ln_xT, 6)
            pe.wait_ge(l5_sim, 1)
            for t in range(T):
                ins = nc.tensor.matmul(bank(6)[:, t * E5:(t + 1) * E5], xT[:, t * P:(t + 1) * P], sim5[:], start=True, stop=True)
            ins.then_inc(router_logits, 1)
            l6_prepare_pe(pe)
            pe.wait_ge(comb_parts, 1)
            for t in range(T):
                ins = nc.tensor.transpose(bank(5).bitcast(BF16)[0:3 * E5, t * P:(t + 1) * P], parts5[:, t, :], identb[:])
            ins.then_inc(comb_parts_ps, 1)

        def l5_weight_pe(pe, phase, e, static, slot):
            pe.wait_ge(l5_scaled[phase], e + 1)
            nc.tensor.matmul(bank(4 + slot), pick5[:, e, :] if static else pick5[:, bass.ds(e, 1), :], comb5T[:],
                             start=True, stop=True).then_inc(l5_weight[phase], 1)

        def l5_expert_pe(pe, phase, e, static, slot, first, last):
            if not last:
                l5_weight_pe(pe, phase, e + 1, static, 1 - slot)
            pe.wait_ge(l5_scaled[phase], e + 3)
            width, w = ((3 * D, proj5), (D, oproj5))[phase]
            for t in range(T):
                ins = nc.tensor.matmul(bank(t)[:, 0:width], scaled[:, slot, t * P:(t + 1) * P],
                                       w[:, e, :] if static else w[:, bass.ds(e, 1), :], start=first, stop=last)
            ins.then_inc(l5_used[phase], 1)

        def l5_sum_pe(pe, phase):
            l5_weight_pe(pe, phase, 0, True, 0)
            for e in range(2):
                l5_expert_pe(pe, phase, e, True, e, e == 0, False)
            with pe.Fori(1, E5 // 2 - 1) as pair:
                for k in range(2):
                    l5_expert_pe(pe, phase, 2 * pair + k, False, k, False, False)
            for e in range(E5 - 2, E5):
                l5_expert_pe(pe, phase, e, True, e % 2, False, e == E5 - 1)

        def l5_sum_dve(dve, phase, source):
            dve.sem_inc(l5_scaled[phase], 2)
            with dve.Fori(0, E5 // 2) as pair:
                for k in range(2):
                    dve.wait_ge(l5_weight[phase], 2 * pair + (k + 1))
                    dve.wait_ge(l5_used[phase], 2 * pair + (k + 1))
                    nc.vector.tensor_tensor(scaled[:, k, :], source[:], bank(4 + k), ALU.mult).then_inc(l5_scaled[phase], 1)

        def l5_pe(pe):
            pe.wait_ge(comb_rows, 1)
            pe.wait_ge(l6_v_raw, 2)
            pe.sem_inc(l5_used[0], 2)
            l5_sum_pe(pe, 0)
            pe.wait_ge(l5_qkv, 4)
            for k in range(2):
                for t in range(T):
                    ins = nc.tensor.transpose(bank(4 + k)[:, t * P:(t + 1) * P], qkv5[:, t, k * D:(k + 1) * D], ident[:])
                ins.then_inc(l5_qk_turned, 1)
            pe.wait_ge(l5_qk, 2)
            att_scores_pe(pe, 3, queryT, key5T, K5)
            for t in range(T):
                att_turn_pe(pe, 3, t, K5, att_exp, 3 * T)
                if t >= 1:
                    att_out_pe(pe, 3, t - 1, K5, qkv5[:, :, 2 * D:3 * D])
            att_out_pe(pe, 3, T - 1, K5, qkv5[:, :, 2 * D:3 * D])
            pe.wait_ge(l5_o, T)
            for t in range(T):
                ins = nc.tensor.transpose(bank(7)[:, t * P:(t + 1) * P], o5[:, t, :], ident[:])
            ins.then_inc(l5_o_turned, 1)
            pe.wait_ge(l5_oT, 1)
            pe.sem_inc(l5_used[1], 2)
            l5_sum_pe(pe, 1)

        def l5_act(act):
            act.wait_ge(l5_used[0], E5 + 2)
            for t in (1, 3):
                act_copy(qkv5[:, t, :], bank(t)[:, 0:3 * D]).then_inc(l5_qkv, 1)
            act.wait_ge(l5_qk_turned, 2)
            act_copy(key5T[:], bank(5)).then_inc(l5_qk, 1)
            att_exp_act(act, 3, K5, S5)
            act.wait_ge(l5_o_turned, 1)
            act_copy(o5T[:], bank(7)).then_inc(l5_oT, 1)

        def l5_dve(dve, link):
            l5_sum_dve(dve, 0, xT)
            dve.wait_ge(l5_used[0], E5 + 2)
            for t in (0, 2):
                nc.vector.tensor_copy(qkv5[:, t, :], bank(t)[:, 0:3 * D]).then_inc(l5_qkv, 1)
            dve.wait_ge(l5_qk_turned, 1)
            nc.vector.tensor_copy(queryT[:], bank(4)).then_inc(l5_qk, 1)
            for t in range(T):
                att_max_dve(dve, link, 3, t, K5, S5)
            for t in range(T):
                att_copy_dve(dve, 3, t, K5)
            dve.wait_ge(att_exp, 4 * T)
            link(nc.vector.reciprocal(row_inv[:], row_sum[:]))
            for t in range(T):
                dve.wait_ge(att_out, 4 * T)
                nc.vector.tensor_scalar(o5[:, t, :], quarters(6)[:, t, :], row_inv[:, t:t + 1], None, ALU.mult).then_inc(l5_o, 1)
            dve.wait_ge(l5_oT, 1)
            l5_sum_dve(dve, 1, o5T)
            dve.wait_ge(l5_used[1], E5 + 2)
            for t in range(T):
                nc.vector.tensor_tensor(x[:, t, :], x[:, t, :], bank(t)[:, 0:D], ALU.add).then_inc(x_updated, 1)

        H6 = 16
        J6 = D // H6
        KT6 = MT // B
        R6 = 9 * J6
        S6 = float(J6) ** -0.5
        wq6 = sb("wq6", [P, D])
        wkv6 = sb("wkv6", [P, 2, C])
        wo6 = sb("wo6", [P, D])
        bq6 = sb("bq6", [P, 1])
        bk6 = sb("bk6", [P, 1])
        bkv6 = sb("bkv6", [P, 2 * D])
        bo6 = sb("bo6", [P, D])
        wq6T = sb("wq6T", [P, D])
        wk6T = sb("wk6T", [C, D])
        wv6T = sb("wv6T", [C, D])
        wo6T = sb("wo6T", [P, D])
        value6 = sb("value6", [P, MT, H6, J6])
        value_head = sb("value_head", [P, MT, 2 * J6])
        max6 = sb("max6", [P, T])
        rest6 = sb("rest6", [P, T])
        max_parts = sb("max_parts", [P, T, 3], BF16)
        max_rows = sb("max_rows", [3, N], BF16)
        key6 = place(9216, [P, M])
        k6_parts = room[:, 10240:11776].bitcast(BF16).rearrange("p (a n) -> p a n", a=3)
        key6_stack = room2[0:R6 + 3, :].bitcast(BF16).rearrange("p (h n) -> p h n", h=H6)
        query6_stack = room[0:R6 + 3, 8192:12288].bitcast(BF16).rearrange("p (h n) -> p h n", h=H6)
        o6_rows = room[0:2 * J6, 0:8192].rearrange("p (h n) -> p h n", h=H6)
        probs6 = place_weights(3072, [P, 2, M])
        query6 = place_weights(5120, [P, N])
        q6_parts = weight_room[:, 5632:6400].bitcast(BF16).rearrange("p (a n) -> p a n", a=3)
        o6_stack = room2[:, 0:512]
        sum6_stack = room2[:, 512:1024]
        inv6 = room2[:, 1024:1536]
        o6T = room2[:, 1536:2048]
        l6_wo_order = sem("l6_wo_order")
        l6_w_turned = sem("l6_w_turned")
        l6_w = sem("l6_w")
        l6_k_ps = sem("l6_k_ps")
        l6_key = sem("l6_key")
        l6_k_parts = sem("l6_k_parts")
        l6_k_stack = sem("l6_k_stack")
        l6_v_ps = sem("l6_v_ps")
        l6_v_raw = sem("l6_v_raw")
        l6_value = sem("l6_value")
        l6_q_ps = sem("l6_q_ps")
        l6_query = sem("l6_query")
        l6_q_parts = sem("l6_q_parts")
        l6_q_stack = sem("l6_q_stack")
        l6_row_scores = sem("l6_row_scores")
        l6_max = sem("l6_max")
        l6_max_parts = sem("l6_max_parts")
        l6_max_turned = sem("l6_max_turned")
        l6_max_rows = sem("l6_max_rows")
        l6_max_stack = sem("l6_max_stack")
        l6_scores = sem("l6_scores")
        l6_probs = sem("l6_probs")
        l6_value_head = sem("l6_value_head")
        l6_o_ps = sem("l6_o_ps")
        l6_o_rows = sem("l6_o_rows")
        l6_o_stack = sem("l6_o_stack")
        l6_oT = sem("l6_oT")
        l6_y = sem("l6_y")

        def l6_prepare_pe(pe):
            pe.wait_ge(late_loaded, 16 * 14)
            nc.tensor.transpose(bank(0)[:, 0:P], wq6[:], ident[:])
            pe.wait_ge(l6_wo_order, 1)
            nc.tensor.transpose(bank(0)[:, P:2 * P], wo6T[:], ident[:])
            for k in range(2):
                ins = nc.tensor.transpose(bank(0)[0:C, (2 + k) * P:(3 + k) * P], wkv6[:, k, :], ident[:])
            ins.then_inc(l6_w_turned, 1)
            pe.wait_ge(l6_w, 4)
            for half in range(2):
                ins = nc.tensor.matmul(bank(1 + half), wk6T[:], ctxT[:, half * 512:(half + 1) * 512], start=True, stop=True)
            ins.then_inc(l6_k_ps, 1)
            for half in range(2):
                for q in range(4):
                    k = 4 * half + q
                    ins = nc.tensor.matmul(bank(3 + half)[:, q * P:(q + 1) * P], ctxT[:, k * P:(k + 1) * P], wv6T[:], start=True, stop=True)
            ins.then_inc(l6_v_ps, 1)

        def l6_prepare_act(act):
            act.wait_ge(l6_w_turned, 1)
            b0 = bank(0)
            act_copy(wq6T[:].rearrange("p (j h) -> p j h", j=J6), b0[:, 0:P].rearrange("p (h j) -> p j h", j=J6)).then_inc(l6_w, 1)
            act_copy(wo6T[:], b0[:, P:2 * P]).then_inc(l6_w, 1)
            kv = b0[0:C, 2 * P:4 * P].rearrange("p (h s j) -> p s j h", s=2, j=J6)
            act_copy(wk6T[:].rearrange("p (j h) -> p j h", j=J6), kv[:, 0]).then_inc(l6_w, 1)
            act_copy(wv6T[:].rearrange("p (h j) -> p j h", j=J6), kv[:, 1]).then_inc(l6_w, 1)
            act.wait_ge(l6_k_ps, 1)
            act.wait_ge(late_loaded, 16 * 14)
            nc.scalar.activation(key6.rearrange("p (b n) -> p b n", b=2), PS[:, 1:3, :], ACT.Identity, bias=bk6[:]).then_inc(l6_key, 1)
            act.wait_ge(l6_v_ps, 1)
            for half in range(2):
                act_copy(value6[:, 4 * half:4 * half + 4, :, :],
                         bank(3 + half).rearrange("p (k h j) -> p k h j", k=4, j=J6)).then_inc(l6_v_raw, 1)

        def split_parts(engine, link, parts, whole, done):
            for a in range(3):
                ins = engine.tensor_copy(parts[:, a, :], whole)
                if a < 2:
                    link(ins)
                    link(engine.tensor_tensor(whole, whole, parts[:, a, :], ALU.subtract))
            ins.then_inc(done, 1)

        def l6_prepare_pool(pool, link):
            pool.wait_ge(late_loaded, 16 * 14)
            nc.gpsimd.tensor_copy(wo6T[:].rearrange("p (j h) -> p j h", j=J6),
                                  wo6[:].rearrange("p (h j) -> p j h", j=J6)).then_inc(l6_wo_order, 1)
            pool.wait_ge(l6_key, 1)
            split_parts(nc.gpsimd, link, k6_parts, key6, l6_k_parts)
            pool.wait_ge(l6_v_raw, 2)
            bv = bkv6[:].rearrange("p (h s j) -> p s h j", s=2, j=J6)[:, 1]
            for k in range(MT):
                nc.gpsimd.tensor_tensor(value6[:, k, :, :], value6[:, k, :, :], bv, ALU.add).then_inc(l6_value, 1)
            nc.gpsimd.memset(value_head[:, :, J6:2 * J6], 1.0).then_inc(l6_value, 1)

        def l6_k_stack_sp(sp):
            sp.wait_ge(x_updated, 5 * T)
            sp.wait_ge(constants, 4)
            sp.dma_start(key6_stack[R6:R6 + 3, :, :], onesb[0:3, :].unsqueeze(1).broadcast_to([3, P, P])).then_inc(l6_k_stack, 16)
            sp.wait_ge(l6_k_parts, 1)
            for a in range(3):
                for b in range(3):
                    r = (3 * a + b) * J6
                    sp.dma_start(key6_stack[r:r + J6, :, :], k6_parts[:, b, :]).then_inc(l6_k_stack, 16)

        def l6_q_stack_dma(eng, a):
            for b in range(3):
                r = (3 * a + b) * J6
                eng.dma_start(query6_stack[r:r + J6, :, :], q6_parts[:, a, :]).then_inc(l6_q_stack, 16)

        def l6_sp(sp):
            sp.wait_ge(l6_k_stack, 16 * 10)
            sp.wait_ge(l6_q_parts, 1)
            for a in range(3):
                l6_q_stack_dma(sp, a)
            with sp.Fori(0, H6) as g:
                sp.wait_ge(l6_max_rows, g + 1)
                sp.dma_start(query6_stack[R6:R6 + 3, bass.ds(g, 1), :], max_rows[:]).then_inc(l6_max_stack, 16)
            sp.wait_ge(l6_o_rows, H6 + 1)
            sp.dma_start(o6_stack, o6_rows[0:J6, :, :]).then_inc(l6_o_stack, 16)
            sp.dma_start(sum6_stack, o6_rows[J6:2 * J6, :, :]).then_inc(l6_o_stack, 16)

        def l6_row_scores_pe(pe, g, b, free=True):
            if free:
                pe.wait_ge(l6_max, 2 * g + b)
            for t in range(2):
                q = (2 * b + t) * P
                ins = nc.tensor.matmul(bank(t), query6_stack[0:R6, at(g), q:q + P], key6_stack[0:R6, at(g), b * KB:(b + 1) * KB],
                                       start=True, stop=True)
            ins.then_inc(l6_row_scores, 1)

        def l6_turn_pe(pe, g):
            pe.wait_ge(l6_max_parts, g + 1)
            for t in range(T):
                ins = nc.tensor.transpose(bank(2).bitcast(BF16)[0:3, t * P:(t + 1) * P], max_parts[:, t, :], identb[:])
            ins.then_inc(l6_max_turned, 1)

        def l6_st_pe(pe, g, b):
            if b == 0:
                pe.wait_ge(l6_max_stack, 16 * g + 16)
            for k in range(4):
                ins = nc.tensor.matmul(bank(3 + 2 * b + k // 2)[:, (k % 2) * K5:(k % 2 + 1) * K5],
                                       key6_stack[:, at(g), b * KB + k * P:b * KB + (k + 1) * P],
                                       query6_stack[:, at(g), b * K5:(b + 1) * K5], start=True, stop=True)
            ins.then_inc(l6_scores, 1)

        def l6_pv_pe(pe, g, b):
            if b == 0:
                pe.wait_ge(l6_o_rows, g + 1)
            pe.wait_ge(l6_value_head, 2 * g + (b + 1))
            pe.wait_ge(l6_probs, 2 * g + (b + 1))
            for k in range(4):
                ins = nc.tensor.matmul(bank(7)[0:2 * J6, b * K5:(b + 1) * K5], value_head[:, 4 * b + k, :],
                                       probs6[:, b, k * K5:(k + 1) * K5], start=(k == 0), stop=(k == 3))
            ins.then_inc(l6_o_ps, 1)

        def l6_head_pe(pe, g, first=False, turn=True, rows=True):
            l6_st_pe(pe, g, 0)
            if not first:
                l6_pv_pe(pe, g - 1, 1)
            l6_st_pe(pe, g, 1)
            if turn:
                l6_turn_pe(pe, g + 1)
            if rows:
                l6_row_scores_pe(pe, g + 2, 0)
            l6_pv_pe(pe, g, 0)
            if rows:
                l6_row_scores_pe(pe, g + 2, 1)

        def l6_pe(pe):
            pe.wait_ge(ln_xT, 7)
            nc.tensor.matmul(bank(5), wq6T[:], xT[:], start=True, stop=True).then_inc(l6_q_ps, 1)
            pe.wait_ge(l6_value, MT + 1)
            pe.wait_ge(l6_k_stack, 16 * 10)
            pe.wait_ge(l6_q_stack, 16 * 9)
            l6_row_scores_pe(pe, 0, 0, free=False)
            l6_row_scores_pe(pe, 0, 1)
            l6_row_scores_pe(pe, 1, 0)
            l6_turn_pe(pe, 0)
            l6_row_scores_pe(pe, 1, 1)
            l6_head_pe(pe, 0, first=True)
            with pe.Fori(1, H6 - 2) as g:
                l6_head_pe(pe, g)
            l6_head_pe(pe, H6 - 2, rows=False)
            l6_head_pe(pe, H6 - 1, turn=False, rows=False)
            l6_pv_pe(pe, H6 - 1, 1)
            pe.wait_ge(l6_oT, 1)
            for t in range(T):
                ins = nc.tensor.matmul(bank(5)[:, t * P:(t + 1) * P], o6T[:, t * P:(t + 1) * P], wo6T[:], start=True, stop=True)
            ins.then_inc(l6_y, 1)

        def l6_max_dve(dve, link, g):
            for b in range(2):
                dve.wait_ge(l6_row_scores, 2 * g + (b + 1))
                nc.vector.tensor_reduce(max6[:, 2 * b:2 * b + 2], PS[:, 0:2, :], X, ALU.max).then_inc(l6_max, 1)
            dve.wait_ge(l6_max, 2 * g + 2)
            link(nc.vector.tensor_scalar(max_parts[:, :, 0], max6[:], -1.0, None, ALU.mult))
            link(nc.vector.scalar_tensor_tensor(out=rest6[:], in0=max6[:], scalar=-1.0, in1=max_parts[:, :, 0],
                                                op0=ALU.mult, op1=ALU.subtract))
            link(nc.vector.tensor_copy(max_parts[:, :, 1], rest6[:]))
            link(nc.vector.tensor_tensor(rest6[:], rest6[:], max_parts[:, :, 1], ALU.subtract))
            nc.vector.tensor_copy(max_parts[:, :, 2], rest6[:]).then_inc(l6_max_parts, 1)

        def l6_rows_dve(dve, g, first=False):
            dve.wait_ge(l6_max_turned, g + 1)
            if not first:
                dve.wait_ge(l6_max_stack, 16 * g)
            nc.vector.tensor_copy(max_rows[:], bank(2).bitcast(BF16)[0:3, 0:N]).then_inc(l6_max_rows, 1)

        def l6_dve(dve, link):
            dve.wait_ge(l6_query, 1)
            split_parts(nc.vector, link, q6_parts, query6, l6_q_parts)
            link(nc.vector.tensor_tensor(x[:], x[:], bo6[:].unsqueeze(1).broadcast_to([P, T, D]), ALU.add))
            l6_max_dve(dve, link, 0)
            l6_rows_dve(dve, 0, first=True)
            l6_max_dve(dve, link, 1)
            l6_rows_dve(dve, 1)
            l6_max_dve(dve, link, 2)
            with dve.Fori(0, H6 - 3) as g:
                link.enter(g, 4)
                l6_rows_dve(dve, g + 2)
                l6_max_dve(dve, link, g + 3)
            link.leave(H6 - 3)
            l6_rows_dve(dve, H6 - 1)
            dve.wait_ge(l6_o_stack, 32)
            link(nc.vector.reciprocal(inv6, sum6_stack))
            nc.vector.tensor_tensor(o6T, o6_stack, inv6, ALU.mult).then_inc(l6_oT, 1)
            dve.wait_ge(l6_y, 1)
            for t in range(T):
                nc.vector.tensor_tensor(x[:, t, :], x[:, t, :], quarters(5)[:, t, :], ALU.add).then_inc(x_updated, 1)

        def l6_exp_act(act, g, b):
            act.wait_ge(l6_scores, 2 * g + (b + 1))
            nc.scalar.activation(probs6[:, b, :].rearrange("p (c n) -> p c n", c=2), PS[:, 3 + 2 * b:5 + 2 * b, :], ACT.Exp,
                                 scale=S6).then_inc(l6_probs, 1)

        def l6_o_act(act, g):
            act.wait_ge(l6_o_ps, 2 * g + 2)
            act_copy(o6_rows[:, at(g), :], bank(7)[0:2 * J6, :]).then_inc(l6_o_rows, 1)

        def l6_act(act):
            act.wait_ge(l6_q_ps, 1)
            nc.scalar.activation(query6, bank(5), ACT.Identity, bias=bq6[:]).then_inc(l6_query, 1)
            act.sem_inc(l6_o_rows, 1)
            for b in range(2):
                l6_exp_act(act, 0, b)
            with act.Fori(1, H6) as g:
                l6_exp_act(act, g, 0)
                l6_o_act(act, g - 1)
                l6_exp_act(act, g, 1)
            l6_o_act(act, H6 - 1)

        def l6_pool(pool):
            pool.wait_ge(l6_value, MT + 1)
            for b in range(2):
                half = slice(b * KT6, (b + 1) * KT6)
                nc.gpsimd.tensor_copy(value_head[:, half, 0:J6], value6[:, half, 0, :]).then_inc(l6_value_head, 1)
            with pool.Fori(1, H6) as g:
                for b in range(2):
                    half = slice(b * KT6, (b + 1) * KT6)
                    pool.wait_ge(l6_o_ps, 2 * g - (1 - b))
                    nc.gpsimd.tensor_copy(value_head[:, half, 0:J6], value6[:, half, bass.ds(g, 1), :].rearrange("p k a j -> p k (a j)")).then_inc(l6_value_head, 1)

        E7 = 8
        F7 = 512
        CAP7 = 160
        NS7 = CAP7 - P
        wr7 = sb("wr7", [P, E7])
        w17 = [place_weights(1536 * s, [P, F7]) for s in range(2)]
        w37 = [place_weights(1536 * s + 512, [P, F7]) for s in range(2)]
        w27 = [place_weights(1536 * s + 1024, [P, 4, D]) for s in range(2)]
        chosen7 = sb("chosen7", [P, T, E7], BF16)
        earlier7 = sb("earlier7", [P, P], BF16)
        onesb = sb("onesb", [P, P], BF16)
        place7 = sb("place7", [P, T, E7])
        places7b = sb("places7b", [P, T, E7], BF16)
        slot7 = sb("slot7", [P, 2])
        gather7 = place(0, [P, T, CAP7])
        x7T = place(640, [P, CAP7])
        silu7 = place(800, [P, 2, 2 * CAP7])
        hidden7T = place(1440, [P, 4, CAP7])
        spread7 = place(2080, [P, 4, N]).rearrange("p (s c) n -> p s c n", s=2)
        y7 = place(4128, [P, 2, D])
        out7T = place(4384, [P, N])
        place7T = place(4896, [P, N // 2]).bitcast(BF16)
        places7 = place(5152, [P, CAP7])
        token_place7 = place(5376, [P, N])
        l7_loaded = [sem("l7_loaded_even"), sem("l7_loaded_odd")]
        l7_zero = sem("l7_zero")
        l7_chosen = sem("l7_chosen")
        l7_before = sem("l7_before")
        l7_gather = sem("l7_gather")
        l7_x_ps = sem("l7_x_ps")
        l7_x = sem("l7_x")
        l7_broad = sem("l7_broad")
        l7_token_place = sem("l7_token_place")
        l7_spread = sem("l7_spread")
        l7_h = sem("l7_h")
        l7_silu = sem("l7_silu")
        l7_hidden = sem("l7_hidden")
        l7_y_ps = sem("l7_y_ps")
        l7_y = sem("l7_y")
        l7_out = sem("l7_out")
        l7_outT = sem("l7_outT")
        l7_turned = sem("l7_turned")

        def l7_const_pool(pool, link):
            link(nc.gpsimd.memset(earlier7[:], 1.0))
            link(nc.gpsimd.affine_select(out=earlier7[:], in_=earlier7[:], compare_op=ALU.is_gt, fill=0.0, base=0,
                                         pattern=[[1, P]], channel_multiplier=-1))
            nc.gpsimd.memset(onesb[:], 1.0).then_inc(constants, 1)

        def l7_load(sp, w1, w3, w2, slot):
            sp.dma_start(w17[slot], w1).then_inc(l7_loaded[slot], 16)
            sp.dma_start(w37[slot], w3).then_inc(l7_loaded[slot], 16)
            sp.dma_start(w27[slot], w2).then_inc(l7_loaded[slot], 16)

        def l7_loads_sp(sp):
            W1, W3 = i["L3_ffn_W1"], i["L3_ffn_W3"]
            W2 = i["L3_ffn_W2"].rearrange("e (c p) d -> e p c d", p=P)
            sp.wait_ge(x_updated, 6 * T)
            for e in range(2):
                l7_load(sp, W1[e], W3[e], W2[e], e)
            with sp.Fori(0, E7 // 2 - 1) as pair:
                for k in range(2):
                    sp.wait_ge(l7_y_ps, 2 * pair + (k + 1))
                    e = 2 * pair + (k + 2)
                    l7_load(sp, W1[bass.ds(e, 1)].rearrange("a d f -> d (a f)"), W3[bass.ds(e, 1)].rearrange("a d f -> d (a f)"),
                            W2[bass.ds(e, 1)].rearrange("a p c d -> p (a c) d"), k)

        def l7_router_pe(pe):
            pe.wait_ge(ln_xT, 8)
            pe.wait_ge(late_loaded, 16 * 14)
            for t in range(T):
                ins = nc.tensor.matmul(bank(6)[:, t * E7:(t + 1) * E7], xT[:, t * P:(t + 1) * P], wr7[:], start=True, stop=True)
            ins.then_inc(router_logits, 1)
            pe.wait_ge(constants, 4)
            nc.tensor.matmul(bank(7)[:, 0:P], onesb[:], earlier7[:], start=True, stop=True)
            nc.tensor.matmul(bank(7)[:, P:P + 1], earlier7[:], onesb[:, 0:1], start=True, stop=True)
            pe.wait_ge(l7_chosen, 1)
            for t in range(T):
                cols = bank(7)[:, 2 * P + t * E7:2 * P + (t + 1) * E7]
                for u in range(t):
                    nc.tensor.matmul(cols, onesb[:], chosen7[:, u, :], start=(u == 0), stop=False)
                ins = nc.tensor.matmul(cols, earlier7[:], chosen7[:, t, :], start=(t == 0), stop=True)
            ins.then_inc(l7_before, 1)
            pe.wait_ge(comb_parts, 2)
            b5 = bank(5).bitcast(BF16)
            for t in range(T):
                nc.tensor.transpose(b5[0:3 * E5, t * P:(t + 1) * P], parts5[:, t, :], identb[:])
                ins = nc.tensor.transpose(b5[0:E7, N + t * P:N + (t + 1) * P], places7b[:, t, :], identb[:])
            ins.then_inc(comb_parts_ps, 1)

        def l7_router_dve(dve, link):
            dve.wait_ge(router_logits, 4)
            link(nc.vector.tensor_scalar(logits[:, :, 0:E7], bank(6)[:, 0:T * E7].rearrange("p (t e) -> p t e", t=T),
                                         1e4, -1e4, ALU.min, ALU.max))
            shift_dve(link, logits, E7)
            top2_dve(link, logits, E7)
            nc.vector.tensor_copy(chosen7[:], chosen[:, :, 0:E7]).then_inc(l7_chosen, 1)
            dve.wait_ge(l7_before, 1)
            before = bank(7)[:, 2 * P:2 * P + T * E7].rearrange("p (t e) -> p t e", t=T)
            link(nc.vector.scalar_tensor_tensor(out=place7[:], in0=before, scalar=1.0, in1=chosen[:, :, 0:E7],
                                                op0=ALU.add, op1=ALU.mult))
            link(nc.vector.tensor_scalar(places7[:, 0:P], bank(7)[:, 0:P], 1.0, None, ALU.add))
            link(nc.vector.tensor_scalar(places7[:, P:CAP7], bank(7)[:, 0:NS7], float(P + 1), None, ALU.add))
            l7_gather_dve(dve, 0, first=True)
            for c in range(2):
                link(nc.vector.tensor_scalar(slot7[:, c:c + 1], bank(7)[:, P:P + 1], float(c * P + 1), None, ALU.add))
            dve.wait_ge(gate_exp, 4)
            weights_dve(link, E7, eps=1e-12)
            for k in range(3):
                part = parts5[:, :, k * E5:k * E5 + E7]
                link(nc.vector.tensor_copy(part, comb[:, :, 0:E7]))
                if k < 2:
                    link(nc.vector.tensor_tensor(comb[:, :, 0:E7], comb[:, :, 0:E7], part, ALU.subtract))
            nc.vector.tensor_copy(places7b[:], place7[:]).then_inc(comb_parts, 1)
            dve.wait_ge(comb_parts_ps, 2)
            dve.wait_ge(l7_zero, 1)
            b5 = bank(5).bitcast(BF16)
            nc.vector.tensor_copy(comb5T[0:3 * E5, :], b5[0:3 * E5, 0:N]).then_inc(comb_rows, 1)
            nc.vector.tensor_copy(place7T[0:E7, :], b5[0:E7, N:2 * N]).then_inc(comb_rows, 1)

        def l7_broad_pe(pe, e):
            nc.tensor.matmul(bank(5), pick5[:, at(e), :], place7T, start=True, stop=True)
            nc.tensor.matmul(bank(6), pick5[:, at(e), :], comb5T[:], start=True, stop=True).then_inc(l7_broad, 1)

        def l7_x_pe(pe, e):
            pe.wait_ge(l7_gather, e + 1)
            for t in range(T):
                ins = nc.tensor.matmul(bank(0)[:, 2 * CAP7:3 * CAP7], xn[:, t, :], gather7[:, t, :], start=(t == 0), stop=(t == T - 1))
            ins.then_inc(l7_x_ps, 1)

        def l7_spread_pe(pe, e, slot, first=False, last=False):
            pe.wait_ge(l7_y, 2 * e + 2)
            pe.wait_ge(l7_spread, e + 1)
            nc.tensor.matmul(bank(7), y7[:, 0, :], spread7[:, slot, 0, :], start=first, stop=False)
            ins = nc.tensor.matmul(bank(7), y7[0:NS7, 1, :], spread7[0:NS7, slot, 1, :], start=False, stop=last)
            if last:
                ins.then_inc(l7_out, 1)

        def l7_expert_pe(pe, e, slot, loads, first=False, second=False, last=False):
            pe.wait_ge(l7_x, e + 1)
            pe.wait_ge(l7_loaded[slot], 48 * loads)
            for p in range(2):
                for half, w in enumerate((w17, w37)):
                    for c in range(2):
                        chunk = (2 * p + c) * P
                        ins = nc.tensor.matmul(bank(2 * p + half)[:, c * CAP7:(c + 1) * CAP7], w[slot][:, chunk:chunk + P], x7T,
                                               start=True, stop=True)
                ins.then_inc(l7_h, 1)
            if not first:
                l7_spread_pe(pe, e - 1, 1 - slot, first=second)
            if not last:
                pe.wait_ge(l7_spread, e + 1)
                l7_broad_pe(pe, e + 1)
                pe.wait_ge(l7_silu, 2 * e + 1)
                l7_x_pe(pe, e + 1)
            pe.wait_ge(l7_hidden, 2 * e + 2)
            for s, n in enumerate((P, NS7)):
                for c in range(4):
                    ins = nc.tensor.matmul(bank(4)[0:n, s * D:(s + 1) * D], hidden7T[:, c, s * P:s * P + n], w27[slot][:, c, :],
                                           start=(c == 0), stop=(c == 3))
            ins.then_inc(l7_y_ps, 1)

        def l7_pe(pe):
            l7_x_pe(pe, 0)
            pe.wait_ge(comb_rows, 3)
            l7_broad_pe(pe, 0)
            l7_expert_pe(pe, 0, 0, 1, first=True)
            l7_expert_pe(pe, 1, 1, 1, second=True)
            with pe.Fori(1, E7 // 2 - 1) as pair:
                for k in range(2):
                    l7_expert_pe(pe, 2 * pair + k, k, pair + 1)
            l7_expert_pe(pe, E7 - 2, 0, E7 // 2)
            l7_expert_pe(pe, E7 - 1, 1, E7 // 2, last=True)
            l7_spread_pe(pe, E7 - 1, 1, last=True)
            pe.wait_ge(l7_outT, 1)
            for t in range(T):
                ins = nc.tensor.transpose(bank(4)[:, t * P:(t + 1) * P], out7T[:, t * P:(t + 1) * P], ident[:])
            ins.then_inc(l7_turned, 1)

        def l7_pool(pool):
            pool.wait_ge(x_updated, 7 * T)
            nc.gpsimd.memset(place7T, 0.0).then_inc(l7_zero, 1)

        def l7_x_act(act, e):
            act.wait_ge(l7_x_ps, e + 1)
            act_copy(x7T, bank(0)[:, 2 * CAP7:3 * CAP7]).then_inc(l7_x, 1)

        def l7_place_act(act, e):
            act.wait_ge(l7_broad, e + 1)
            act_copy(token_place7, bank(5)).then_inc(l7_token_place, 1)

        def l7_expert_act(act, e, last=False):
            for p in range(2):
                act.wait_ge(l7_h, 2 * e + (p + 1))
                nc.scalar.activation(silu7[:, p, :], bank(2 * p)[:, 0:2 * CAP7], ACT.Silu).then_inc(l7_silu, 1)
            if not last:
                l7_place_act(act, e + 1)
                l7_x_act(act, e + 1)
            act.wait_ge(l7_y_ps, e + 1)
            for s, n in enumerate((P, NS7)):
                act_copy(y7[0:n, s, :], bank(4)[0:n, s * D:(s + 1) * D]).then_inc(l7_y, 1)

        def l7_act(act):
            l7_x_act(act, 0)
            l7_place_act(act, 0)
            with act.Fori(0, E7 - 1) as e:
                l7_expert_act(act, e)
            l7_expert_act(act, E7 - 1, last=True)

        def l7_gather_dve(dve, e, first=False):
            if not first:
                dve.wait_ge(l7_x_ps, e)
            nc.vector.tensor_tensor(gather7, places7.unsqueeze(1).broadcast_to([P, T, CAP7]), place7[:, :, at(e)].broadcast_to([P, T, CAP7]),
                                    ALU.is_equal).then_inc(l7_gather, 1)

        def l7_spread_dve(dve, e, slot):
            dve.wait_ge(l7_token_place, e + 1)
            for s, n in enumerate((P, NS7)):
                ins = nc.vector.scalar_tensor_tensor(out=spread7[0:n, slot, s, :], in0=token_place7[0:n, :], scalar=slot7[0:n, s:s + 1],
                                                     in1=bank(6)[0:n, :], op0=ALU.is_equal, op1=ALU.mult)
            ins.then_inc(l7_spread, 1)

        def l7_hidden_dve(dve, e):
            for p in range(2):
                dve.wait_ge(l7_silu, 2 * e + (p + 1))
                nc.vector.tensor_tensor(hidden7T[:, 2 * p:2 * p + 2, :], silu7[:, p, :].rearrange("p (c n) -> p c n", c=2),
                                        bank(2 * p + 1)[:, 0:2 * CAP7].rearrange("p (c n) -> p c n", c=2), ALU.mult).then_inc(l7_hidden, 1)

        def l7_dve(dve):
            l7_spread_dve(dve, 0, 0)
            with dve.Fori(0, E7 // 2 - 1) as pair:
                for k in range(2):
                    l7_gather_dve(dve, 2 * pair + (k + 1))
                    l7_hidden_dve(dve, 2 * pair + k)
                    l7_spread_dve(dve, 2 * pair + (k + 1), 1 - k)
            l7_gather_dve(dve, E7 - 1)
            l7_hidden_dve(dve, E7 - 2)
            l7_spread_dve(dve, E7 - 1, 1)
            l7_hidden_dve(dve, E7 - 1)
            dve.wait_ge(l7_out, 1)
            nc.vector.tensor_copy(out7T, bank(7)).then_inc(l7_outT, 1)
            dve.wait_ge(l7_turned, 1)
            for t in range(T):
                nc.vector.tensor_tensor(x[:, t, :], x[:, t, :], quarters(4)[:, t, :], ALU.add).then_inc(x_updated, 1)

        x_dram = i["x"].rearrange("b (t p) d -> p (b t) d", p=P)
        out_dram = out.rearrange("b (t p) d -> p (b t) d", p=P)
        ctx_dram = i["ctx_768"].rearrange("b (t p) c -> p (b t) c", p=P)

        def row(v, n):
            return v.unsqueeze(0).broadcast_to([n, v.shape[0]])

        block = ctx.enter_context(nc.Block())

        @block.sync
        def _(sp):
            sp.dma_start(x[:], x_dram).then_inc(x_loaded, 16)
            sp.dma_start(ctx_rows[:], ctx_dram).then_inc(ctx_loaded, 16)
            sp.dma_start(wq[:], i["L0_xattn_Wq"]).then_inc(l0_loaded, 16)
            sp.dma_start(wk[:], i["L0_xattn_Wk"]).then_inc(l0_loaded, 16)
            sp.dma_start(wv[:], i["L0_xattn_Wv"]).then_inc(l0_loaded, 16)
            sp.dma_start(wout[:], i["L0_xattn_Wout"].rearrange("(h p) d -> p h d", p=P)).then_inc(l0_loaded, 16)
            sp.dma_start(bout[:], row(i["L0_xattn_bout"], P)).then_inc(l0_loaded, 16)
            sp.dma_start(we[:], i["L0_ffn_We"].rearrange("e o i -> o e i")).then_inc(early_loaded, 16)
            sp.dma_start(wg1[:], i["L0_ffn_Wg"]).then_inc(early_loaded, 16)
            sp.dma_start(bg1[:], row(i["L0_ffn_bg"], P)).then_inc(early_loaded, 16)
            sp.dma_start(be1[:], i["L0_ffn_be"]).then_inc(early_loaded, 16)
            sp.dma_start(wq2[:], i["L1_xattn_Wq"]).then_inc(early_loaded, 16)
            sp.dma_start(wk2[:], i["L1_xattn_Wk"]).then_inc(early_loaded, 16)
            sp.dma_start(wv2[:], i["L1_xattn_Wv"]).then_inc(early_loaded, 16)
            sp.dma_start(bq2[:], i["L1_xattn_bq"].unsqueeze(1)).then_inc(early_loaded, 16)
            sp.dma_start(bk2[:], i["L1_xattn_bk"].unsqueeze(1)).then_inc(early_loaded, 16)
            sp.dma_start(bv2[:], row(i["L1_xattn_bv"], P)).then_inc(early_loaded, 16)
            sp.dma_start(b1[:], i["L1_ffn_b1"]).then_inc(early_loaded, 16)
            sp.dma_start(wg3[:], i["L1_ffn_Wg"]).then_inc(early_loaded, 16)
            sp.dma_start(wo3[:], i["L1_ffn_Wo"]).then_inc(early_loaded, 16)
            sp.dma_start(bo3[:], row(i["L1_ffn_bo"], P)).then_inc(early_loaded, 16)
            sp.dma_start(w1[:], i["L1_ffn_W1"].rearrange("e (c p) d -> p e c d", p=P)).then_inc(early_loaded, 16)
            sp.dma_start(wd4[:], i["L2_xattn_W_d2v"]).then_inc(l4_loaded, 16)
            sp.dma_start(wi4[:], i["L2_xattn_W_img"]).then_inc(l4_loaded, 16)
            sp.dma_start(wt4[:], i["L2_xattn_W_txt"]).then_inc(l4_loaded, 16)
            sp.dma_start(wf14[:], i["L2_xattn_W_f1"].rearrange("(c p) i -> p c i", p=P)).then_inc(l4_loaded, 16)
            sp.dma_start(wf24[:], i["L2_xattn_W_f2"]).then_inc(l4_loaded, 16)
            for l in range(2):
                wa, ba = i[f"L2_xattn_W_att{l}"], i[f"L2_xattn_b_att{l}"]
                sp.dma_start(wa4[:, l, :], wa).then_inc(l4_loaded, 16)
                sp.dma_start(ba4_rows[:, l, :], row(ba, P)).then_inc(l4_loaded, 16)
                for copy in range(2):
                    sp.dma_start(ba4[64 * copy:64 * (copy + 1), l:l + 1], ba.unsqueeze(1)).then_inc(l4_ba, 16)
            sp.dma_start(bd4[:], i["L2_xattn_b_d2v"].unsqueeze(1)).then_inc(l4_loaded, 16)
            sp.dma_start(bi4[:], i["L2_xattn_b_img"].unsqueeze(1)).then_inc(l4_loaded, 16)
            sp.dma_start(bt4[:], i["L2_xattn_b_txt"].unsqueeze(1)).then_inc(l4_loaded, 16)
            for c in range(4):
                sp.dma_start(bf14[:, c:c + 1], i["L2_xattn_b_f1"][c * P:(c + 1) * P].unsqueeze(1)).then_inc(l4_loaded, 16)
            sp.dma_start(bf24[:], row(i["L2_xattn_b_f2"], P)).then_inc(l4_loaded, 16)
            sp.wait_ge(l3_b1_parts, 1)
            for k, part in enumerate((b1_hi, b1_mid, b1_lo)):
                sp.dma_start(b1_rows[k:k + 1, :, :], part[:]).then_inc(l3_b1_rows, 16)
            sp.wait_ge(x_updated, 2 * T)
            for k, name in enumerate(("q", "k", "v")):
                sp.dma_start(proj5[:, :, k * D:(k + 1) * D], i[f"L2_ffn_{name}_proj"].rearrange("e c h -> c e h")).then_inc(late_loaded, 16)
            sp.dma_start(oproj5[:], i["L2_ffn_o_proj"].rearrange("e h c -> h e c")).then_inc(late_loaded, 16)
            sp.dma_start(sim5[:], i["L2_ffn_sim_matrix"]).then_inc(late_loaded, 16)
            sp.dma_start(gates5[:], row(i["L2_ffn_gates"], P)).then_inc(late_loaded, 16)
            sp.dma_start(wq6[:], i["L3_xattn_Wq"]).then_inc(late_loaded, 16)
            sp.dma_start(wkv6[:], i["L3_xattn_Wkv"].rearrange("(k p) c -> p k c", p=P)).then_inc(late_loaded, 16)
            sp.dma_start(wo6[:], i["L3_xattn_Wo"]).then_inc(late_loaded, 16)
            with nc.allow_non_contiguous_dma(reason="128 elements, in the features' new order"):
                sp.dma_start(bq6[:], i["L3_xattn_bq"].rearrange("(h j) -> j h", j=J6)).then_inc(late_loaded, 16)
                sp.dma_start(bk6[:], i["L3_xattn_bkv"].rearrange("(h s j) -> s j h", s=2, j=J6)[0]).then_inc(late_loaded, 16)
            sp.dma_start(bkv6[:], row(i["L3_xattn_bkv"], P)).then_inc(late_loaded, 16)
            sp.dma_start(bo6[:], row(i["L3_xattn_bo"], P)).then_inc(late_loaded, 16)
            sp.dma_start(wr7[:], i["L3_ffn_Wr"]).then_inc(late_loaded, 16)
            l6_k_stack_sp(sp)
            l6_sp(sp)
            l7_loads_sp(sp)
            sp.wait_ge(x_updated, T * 8)
            sp.dma_start(out_dram, x[:]).then_inc(stored, 16)
            sp.wait_ge(stored, 16)

        @block.gpsimd
        def _(pool):
            link = Chain(pool, pool_chain)
            const_pool(pool)
            ln_pool(pool, link, 0)
            rev_pool()
            l4_const_pool()
            l5_const_pool(pool, link)
            l7_const_pool(pool, link)
            l0_pool(pool)
            for k in range(3):
                whole_max_pool(pool, k)
            for n in range(1, 8):
                if n == 5:
                    l5_norm_pool(pool)
                ln_pool(pool, link, n)
                if n == 5:
                    l5_xnorm_pool(pool)
                    l6_prepare_pool(pool, link)
                if n == 6:
                    l6_pool(pool)
                if n == 7:
                    l7_pool(pool)
                if n == 4:
                    for k in range(3, 6):
                        whole_max_pool(pool, k)

        @block.tensor
        def _(pe):
            fold_pe(pe)
            ln_pe(pe, 0)
            l0_pe(pe)
            l1_prepare_pe(pe)
            ln_pe(pe, 1)
            l1_pe(pe)
            l2_prepare_pe(pe)
            ln_pe(pe, 2)
            l2_pe(pe)
            l3_prepare_pe(pe)
            ln_pe(pe, 3)
            l3_pe(pe)
            l4_ctx_pe(pe)
            ln_pe(pe, 4)
            l4_pe(pe)
            l5_sim_pe(pe)
            ln_pe(pe, 5)
            l5_router_pe(pe)
            l5_pe(pe)
            ln_pe(pe, 6)
            l6_pe(pe)
            ln_pe(pe, 7)
            l7_router_pe(pe)
            l7_pe(pe)

        @block.scalar
        def _(act):
            fold_copy(act, act_copy, 1, fold_act)
            ln_act(act, 0)
            l0_act(act)
            l1_prepare_act(act)
            ln_act(act, 1)
            gate_act(act, 1, E1)
            l1_act(act)
            l2_prepare_act(act)
            ln_act(act, 2)
            l2_act(act)
            l3_prepare_act(act)
            ln_act(act, 3)
            gate_act(act, 2, E3)
            l3_act(act)
            l4_ctx_act(act)
            ln_act(act, 4)
            l4_act(act)
            l5_sim_act(act)
            ln_act(act, 5)
            l6_prepare_act(act)
            gate_act(act, 3, E5)
            l5_act(act)
            ln_act(act, 6)
            l6_act(act)
            ln_act(act, 7)
            gate_act(act, 4, E7)
            l7_act(act)

        @block.vector
        def _(dve):
            link = Chain(dve, dve_chain)
            ln_dve(dve, link, 0)
            fold_copy(dve, nc.vector.tensor_copy, 0, fold_dve)
            l0_dve(dve, link)
            ln_dve(dve, link, 1)
            l1_dve(dve, link)
            ln_dve(dve, link, 2)
            l2_prepare_dve(dve)
            l2_dve(dve, link)
            l3_parts_dve(dve, link)
            ln_dve(dve, link, 3)
            l3_dve(dve, link)
            ln_dve(dve, link, 4)
            l4_ctx_dve(dve)
            l4_dve(dve, link)
            l5_sim_dve(dve, link)
            ln_dve(dve, link, 5)
            l5_router_dve(dve, link)
            l5_dve(dve, link)
            ln_dve(dve, link, 6)
            l6_dve(dve, link)
            ln_dve(dve, link, 7)
            l7_router_dve(dve, link)
            l7_dve(dve)


def kernel(**inputs):
    import numpy as np
    import concourse.bacc as bacc
    from concourse.bass_utils import run_bass_kernel_spmd

    nc = bacc.Bacc("TRN2", target_bir_lowering=False, num_devices=1)
    arrays, given = {}, {}
    for name, value in inputs.items():
        a = np.ascontiguousarray(value)
        arrays[f"in_{name}"] = a
        given[name] = nc.dram_tensor(f"in_{name}", a.shape, mybir.dt.from_np(a.dtype), kind="ExternalInput").ap()
    out = nc.dram_tensor("out_x", given["x"].shape, F32, kind="ExternalOutput").ap()
    build(nc, given, out)
    return run_bass_kernel_spmd(nc, [arrays], core_ids=[0]).results[0]["out_x"]
```

```python
from contextlib import ExitStack

import concourse.bass as bass
from concourse import mybir

F32 = mybir.dt.float32
BF16 = mybir.dt.bfloat16
ALU = mybir.AluOpType
ACT = mybir.ActivationFunctionType
X = mybir.AxisListType.X
RMAX = bass.bass_isa.ReduceOp.max

P = 128
B = 2
D = 128
C = 96
N = 512
T = N // P
M = 1024
MT = M // P
KB = M // B
BIG = 3.0e38
ROUND = 12582912.0


class Chain:

    def __init__(self, engine, semaphore):
        self.engine, self.semaphore = engine, semaphore
        self.base, self.step, self.turn, self.per = 0, 0, None, 0

    def __call__(self, ins):
        ins.then_inc(self.semaphore, 1)
        self.step += 1
        if self.turn is None:
            self.engine.wait_ge(self.semaphore, self.base + self.step)
        else:
            self.engine.wait_ge(self.semaphore, self.turn * self.per + (self.base + self.step))
        return ins

    def enter(self, turn, per):
        self.base, self.step, self.turn, self.per = self.base + self.step, 0, turn, per

    def leave(self, turns):
        assert self.step == self.per, (self.step, self.per)
        self.base, self.step, self.turn = self.base + turns * self.per, 0, None


def wide(ap, n):
    return ap.unsqueeze(2).broadcast_to([ap.shape[0], ap.shape[1], n])


def build(nc, i, out):
    with ExitStack() as ctx:
        def sb(name, shape, dt=F32):
            return ctx.enter_context(nc.sbuf_tensor(name, shape, dt))

        def sem(name):
            return ctx.enter_context(nc.semaphore(name))

        PS = ctx.enter_context(nc.psum_tensor("PS", [P, 8, 512], F32))

        def bank(b):
            return PS[:, b, :]

        def quarters(b):
            return PS[:, b, :].rearrange("p (t d) -> p t d", t=4)

        x = sb("x", [P, T, D])
        xn = sb("xn", [P, T, D])
        xT = sb("xT", [P, N])
        ident = sb("ident", [P, P])
        identb = sb("identb", [P, P], BF16)
        ctx_rows = sb("ctx_rows", [P, MT, C])
        ctxT = sb("ctxT", [C, M])
        stats = sb("stats", [P, T, 6])
        moments = sb("moments", [P, T, 2])
        rstd = sb("rstd", [P, T])
        minus_half = sb("minus_half", [P, 16])

        room = sb("room", [P, 12288])

        weight_room = sb("weight_room", [P, 8192])

        def place_in(whole, at, shape):
            size = 1
            for n in shape[1:]:
                size *= n
            ap = whole[0:shape[0], at:at + size]
            if len(shape) == 3:
                ap = ap.rearrange("p (a b) -> p a b", a=shape[1])
            return ap

        def place(at, shape):
            return place_in(room, at, shape)

        def place_weights(at, shape):
            return place_in(weight_room, at, shape)

        x_loaded = sem("x_loaded")
        ctx_loaded = sem("ctx_loaded")
        early_loaded = sem("early_loaded")
        late_loaded = sem("late_loaded")
        ident_zero = sem("ident_zero")
        ident_done = sem("ident_done")
        dve_chain = sem("dve_chain")
        pool_chain = sem("pool_chain")
        x_updated = sem("x_updated")
        ln_moments = sem("ln_moments")
        ln_rstd = sem("ln_rstd")
        ln_rows = sem("ln_rows")
        ln_turned = sem("ln_turned")
        ln_xT = sem("ln_xT")
        stored = sem("stored")

        def const_pool(pool):
            nc.gpsimd.memset(ident[:], 0.0).then_inc(ident_zero, 1)
            nc.gpsimd.memset(minus_half[:], -0.5).then_inc(ident_done, 1)
            pool.wait_ge(ident_zero, 1)
            nc.gpsimd.affine_select(out=ident[:], in_=ident[:], compare_op=ALU.not_equal, fill=1.0, base=0,
                                    pattern=[[-1, P]], channel_multiplier=1).then_inc(ident_done, 1)
            pool.wait_ge(ident_done, 2)
            nc.gpsimd.tensor_copy(identb[:], ident[:]).then_inc(ident_done, 1)

        LN_BANK = 7

        def ln_dve(dve, link, n):
            if n == 0:
                dve.wait_ge(x_loaded, 16)
            else:
                dve.wait_ge(x_updated, T * n)
            for t in range(T):
                ins = nc.vector.bn_stats(stats[:, t, :], x[:, t, :])
            link(ins)
            for t in range(T):
                ins = nc.vector.bn_aggr(moments[:, t, :], stats[:, t, :])
            ins.then_inc(ln_moments, 1)
            dve.wait_ge(ln_rstd, n + 1)
            for t in range(T):
                nc.vector.tensor_scalar(xn[:, t, :], x[:, t, :], moments[:, t, 0:1], rstd[:, t:t + 1],
                                        ALU.subtract, ALU.mult).then_inc(ln_rows, 1)

        def ln_pool(pool, link, n):
            pool.wait_ge(ln_moments, n + 1)
            link(nc.gpsimd.tensor_scalar(rstd[:], moments[:, :, 1], 1e-5, None, ALU.add))
            nc.gpsimd.tensor_tensor(rstd[:], rstd[:], minus_half[:, 0:T], ALU.pow).then_inc(ln_rstd, 1)

        def ln_pe(pe, n):
            for t in range(T):
                pe.wait_ge(ln_rows, T * n + t + 1)
                ins = nc.tensor.transpose(bank(LN_BANK)[:, t * P:(t + 1) * P], xn[:, t, :], ident[:])
            ins.then_inc(ln_turned, 1)

        def ln_act(act, n):
            act.wait_ge(ln_turned, n + 1)
            nc.scalar.activation(xT[:], bank(LN_BANK), ACT.Copy).then_inc(ln_xT, 1)

        H0 = 8
        L0_LOOP = 3
        S0 = 1.5 * float(D) ** -0.5
        wq = place_weights(0, [P, H0 * D])
        wk = place_weights(1024, [C, H0 * D])
        wv = place_weights(2048, [C, H0 * D])
        wout = place_weights(3072, [P, H0, D])
        wqT = place(6144, [P, H0, D])
        wkT = place(7168, [P, H0, C])
        wvT = place(7936, [P, H0, C])
        A_all = place_weights(4096, [P, H0, C])
        M_all = place_weights(4864, [C, H0, D])
        A_head = sb("A_head", [P, C])
        T_head = place(8704, [C, N])
        probs = place(0, [P, 2, M])
        probsT = place(2048, [P, MT, N])
        mixT = place(9216, [C, N])
        row_max = sb("row_max", [P, T])
        neg_max = sb("neg_max", [P, T])
        row_sum = sb("row_sum", [P, T])
        row_inv = sb("row_inv", [P, T])
        bout = sb("bout", [P, D])
        l0_qk_loaded = sem("l0_qk_loaded")
        l0_loaded = sem("l0_loaded")
        fold_turned = sem("fold_turned")
        fold_dve = sem("fold_dve")
        fold_act = sem("fold_act")
        l0_A = sem("l0_A")
        l0_query = sem("l0_query")
        l0_T = sem("l0_T")
        l0_scores = sem("l0_scores")
        l0_negmax = sem("l0_negmax")
        l0_probs = sem("l0_probs")
        l0_turned = sem("l0_turned")
        l0_free_a = sem("l0_free_a")
        l0_free_b = sem("l0_free_b")
        l0_mixed = sem("l0_mixed")
        l0_mixT = sem("l0_mixT")
        l0_headout = sem("l0_headout")
        l0_added = sem("l0_added")

        def fold_turn_pe(pe, w, rows, banks):
            for half in range(2):
                for q in range(4):
                    h = 4 * half + q
                    ins = nc.tensor.transpose(bank(banks[half])[:, q * P:q * P + rows], w[:, h * D:(h + 1) * D],
                                              ident[0:rows, 0:rows])
                ins.then_inc(fold_turned, 1)

        def fold_pe(pe):
            pe.wait_ge(ident_done, 2)
            pe.wait_ge(ctx_loaded, 16)
            for half in range(2):
                for q in range(4):
                    ins = nc.tensor.transpose(bank(half)[0:C, q * P:(q + 1) * P], ctx_rows[:, 4 * half + q, :], ident[:])
                ins.then_inc(fold_turned, 1)
            pe.wait_ge(l0_qk_loaded, 16 * 2)
            fold_turn_pe(pe, wq, P, (2, 3))
            fold_turn_pe(pe, wk, C, (4, 5))
            pe.wait_ge(fold_dve, 3)
            pe.wait_ge(fold_act, 3)
            for half in range(2):
                for q in range(4):
                    h = 4 * half + q
                    ins = nc.tensor.matmul(bank(half)[:, q * P:q * P + C], wqT[:, h, :], wkT[:, h, :],
                                           start=True, stop=True)
                ins.then_inc(fold_turned, 1)

        def fold_M_pe(pe):
            pe.wait_ge(fold_dve, 5)
            pe.wait_ge(fold_act, 5)
            for half in range(2):
                for q in range(4):
                    h = 4 * half + q
                    ins = nc.tensor.matmul(bank(4 + half)[0:C, q * P:(q + 1) * P], wvT[:, h, :], wout[:, h, :],
                                           start=True, stop=True)
                ins.then_inc(fold_turned, 1)

        def fold_copy(eng, copy, half, done):
            lo = 4 * half
            eng.wait_ge(fold_turned, 1 + half)
            copy(ctxT[:, half * 512:(half + 1) * 512], bank(half)[0:C, :]).then_inc(done, 1)
            eng.wait_ge(fold_turned, 3 + half)
            copy(wqT[:, lo:lo + 4, :], quarters(2 + half)).then_inc(done, 1)
            eng.wait_ge(fold_turned, 5 + half)
            copy(wkT[:, lo:lo + 4, :], quarters(4 + half)[:, :, 0:C]).then_inc(done, 1)
            eng.wait_ge(fold_turned, 7 + half)
            copy(A_all[:, lo:lo + 4, :], quarters(half)[:, :, 0:C]).then_inc(done, 1)

        def fold_wv_copy(eng, copy, half, done):
            eng.wait_ge(fold_turned, 9 + half)
            copy(wvT[:, 4 * half:4 * half + 4, :], quarters((6, 5)[half])[:, :, 0:C]).then_inc(done, 1)

        def fold_M_copy(eng, copy, half, done):
            eng.wait_ge(fold_turned, 11 + half)
            copy(M_all[:, 4 * half:4 * half + 4, :], quarters(4 + half)[0:C]).then_inc(done, 1)

        def at(g):
            return slice(g, g + 1) if isinstance(g, int) else bass.ds(g, 1)

        def act_copy(dst, src):
            return nc.scalar.activation(dst, src, ACT.Copy)

        def l0_scores_pe(pe, t):
            for half in range(2):
                ins = nc.tensor.matmul(bank(2 * (t % 2) + half), T_head[:, t * P:(t + 1) * P],
                                       ctxT[:, half * 512:(half + 1) * 512], start=True, stop=True)
            ins.then_inc(l0_scores, 1)

        def l0_query_pe(pe, h):
            pe.wait_ge(l0_A, h + 1)
            nc.tensor.matmul(bank(7)[0:C, :], A_head[:], xT[:], start=True, stop=True).then_inc(l0_query, 1)

        def l0_turn_pe(pe, h, t):
            pe.wait_ge(l0_probs, T * h + (t + 1))
            for half, free in ((0, l0_free_a), (1, l0_free_b)):
                pe.wait_ge(free, T * h + (t + 1))
                for q in range(4):
                    k = 4 * half + q
                    ins = nc.tensor.transpose(bank(4 + half)[:, q * P:(q + 1) * P],
                                              probs[:, t % 2, k * P:(k + 1) * P], ident[:])
                ins.then_inc(l0_turned, 1)

        def l0_mixed_pe(pe, h, half):
            if half == 0:
                pe.wait_ge(l0_added, h + 1)
            for free in (l0_free_a, l0_free_b):
                pe.wait_ge(free, T * h + (2 * half + 3))
            cols = slice(half * 2 * P, (half + 1) * 2 * P)
            for k in range(MT):
                ins = nc.tensor.matmul(bank(6)[0:C, cols], ctx_rows[:, k, :], probsT[:, k, cols],
                                       start=(k == 0), stop=(k == MT - 1))
            ins.then_inc(l0_mixed, 1)

        def l0_head_pe(pe, h, last):
            l0_turn_pe(pe, h, 0)
            l4_early_pe(pe, h, 0)
            l0_scores_pe(pe, 2)
            l0_turn_pe(pe, h, 1)
            l4_early_pe(pe, h, 1)
            l0_scores_pe(pe, 3)
            if not last:
                l4_early_pe(pe, h, 2)
                l0_query_pe(pe, h + 1)
            l0_turn_pe(pe, h, 2)
            l0_mixed_pe(pe, h, 0)
            l0_turn_pe(pe, h, 3)
            if not last:
                pe.wait_ge(l0_T, h + 2)
                l0_scores_pe(pe, 0)
            l0_mixed_pe(pe, h, 1)
            if not last:
                l0_scores_pe(pe, 1)
            pe.wait_ge(l0_mixT, h + 1)
            for t in range(T):
                ins = nc.tensor.matmul(bank(6)[:, t * P:(t + 1) * P], mixT[:, t * P:(t + 1) * P],
                                       M_all[:, at(h), :], start=True, stop=True)
            ins.then_inc(l0_headout, 1)

        def l0_pe(pe):
            pe.wait_ge(l0_loaded, 16 * 3)
            fold_turn_pe(pe, wv, C, (6, 5))
            pe.wait_ge(ln_xT, 1)
            l0_query_pe(pe, 0)
            fold_M_pe(pe)
            pe.wait_ge(l0_T, 1)
            l0_scores_pe(pe, 0)
            l0_scores_pe(pe, 1)
            pe.wait_ge(fold_dve, 6)
            pe.wait_ge(fold_act, 6)
            with pe.Fori(0, L0_LOOP) as h:
                l0_head_pe(pe, h, False)
            for h in range(L0_LOOP, H0):
                l0_head_pe(pe, h, h == H0 - 1)

        def l0_max_dve(dve, link, h, t):
            dve.wait_ge(l0_scores, T * h + (t + 1))
            link(nc.vector.tensor_reduce(row_max[:, t:t + 1], PS[:, 2 * (t % 2):2 * (t % 2) + 2, :],
                                         mybir.AxisListType.XY, ALU.max))
            nc.vector.tensor_scalar(neg_max[:, t:t + 1], row_max[:, t:t + 1], -S0, None, ALU.mult).then_inc(l0_negmax, 1)

        def l0_turned_dve(dve, h, t):
            dve.wait_ge(l0_turned, 2 * T * h + (2 * t + 1))
            nc.vector.tensor_copy(probsT[:, 0:4, t * P:(t + 1) * P], quarters(4)).then_inc(l0_free_a, 1)

        def l0_head_dve(dve, link, h, last):
            for t in range(T):
                if t == T - 1:
                    l4_early_dve(dve, link, h, 1)
                l0_turned_dve(dve, h, t)
                if t == 0:
                    l4_early_dve(dve, link, h, 0)
                if t < T - 2:
                    l0_max_dve(dve, link, h, t + 2)
            dve.wait_ge(l0_probs, T * h + T)
            link(nc.vector.reciprocal(row_inv[:], row_sum[:]))
            if not last:
                l0_max_dve(dve, link, h + 1, 0)
            l4_early_dve(dve, link, h, 2)
            if not last:
                l0_max_dve(dve, link, h + 1, 1)
            dve.wait_ge(l0_headout, h + 1)
            dve.wait_ge(l0_added, h + 1)
            for t in range(T):
                ins = nc.vector.scalar_tensor_tensor(out=x[:, t, :], in0=quarters(6)[:, t, :], scalar=row_inv[:, t:t + 1],
                                                     in1=x[:, t, :], op0=ALU.mult, op1=ALU.add)
                if last:
                    ins.then_inc(x_updated, 1)
            if not last:
                ins.then_inc(l0_added, 1)

        def l0_dve(dve, link):
            fold_wv_copy(dve, nc.vector.tensor_copy, 0, fold_dve)
            fold_M_copy(dve, nc.vector.tensor_copy, 0, fold_dve)
            dve.wait_ge(l0_loaded, 16 * 3)
            dve.wait_ge(ln_rows, T)
            dve.sem_inc(l0_free_a, 1)
            nc.vector.tensor_tensor(x[:], x[:], bout[:].unsqueeze(1).broadcast_to([P, T, D]), ALU.add).then_inc(l0_added, 1)
            for t in range(2):
                l0_max_dve(dve, link, 0, t)
            with dve.Fori(0, L0_LOOP) as h:
                link.enter(h, 5)
                l0_head_dve(dve, link, h, False)
            link.leave(L0_LOOP)
            for h in range(L0_LOOP, H0):
                l0_head_dve(dve, link, h, h == H0 - 1)

        def l0_exp_act(act, h, t):
            act.wait_ge(l0_negmax, T * h + (t + 1))
            nc.scalar.activation(probs[:, t % 2, :].rearrange("p (b k) -> p b k", b=2), PS[:, 2 * (t % 2):2 * (t % 2) + 2, :],
                                 ACT.Exp, bias=neg_max[:, t:t + 1], scale=S0,
                                 accum_out=row_sum[:, t:t + 1]).then_inc(l0_probs, 1)

        def l0_head_act(act, h, last):
            for t in range(T):
                act.wait_ge(l0_turned, 2 * T * h + (2 * t + 2))
                act_copy(probsT[:, 4:8, t * P:(t + 1) * P], quarters(5)).then_inc(l0_free_b, 1)
                if t < 2:
                    l4_early_act(act, h, t)
                if t < T - 2:
                    l0_exp_act(act, h, t + 2)
                if t == 1 and not last:
                    act.wait_ge(l0_query, h + 2)
                    act_copy(T_head[:], bank(7)[0:C, :]).then_inc(l0_T, 1)
            if not last:
                l0_exp_act(act, h + 1, 0)
            act.wait_ge(l0_mixed, 2 * h + 2)
            act_copy(mixT[:], bank(6)[0:C, :]).then_inc(l0_mixT, 1)
            if not last:
                l0_exp_act(act, h + 1, 1)

        def l0_act(act):
            act.sem_inc(l0_free_b, 1)
            fold_wv_copy(act, act_copy, 1, fold_act)
            act.wait_ge(l0_query, 1)
            act_copy(T_head[:], bank(7)[0:C, :]).then_inc(l0_T, 1)
            fold_M_copy(act, act_copy, 1, fold_act)
            for t in range(2):
                l0_exp_act(act, 0, t)
            with act.Fori(0, L0_LOOP) as h:
                l0_head_act(act, h, False)
            for h in range(L0_LOOP, H0):
                l0_head_act(act, h, h == H0 - 1)

        def l0_pool(pool):
            pool.wait_ge(fold_dve, 4)
            pool.wait_ge(fold_act, 4)
            nc.gpsimd.tensor_copy(A_head[:], A_all[:, 0, :]).then_inc(l0_A, 1)
            with pool.Fori(1, H0) as h:
                pool.wait_ge(l0_query, h)
                nc.gpsimd.tensor_copy(A_head[:], A_all[:, bass.ds(h, 1), :].rearrange("p a c -> p (a c)")).then_inc(l0_A, 1)

        rev = sb("rev", [P, T, 16])
        logits = sb("logits", [P, T, 16])
        shifted = sb("shifted", [P, T, 16])
        gate = sb("gate", [P, T, 16])
        left = sb("left", [P, T, 16])
        equal = sb("equal", [P, T, 16])
        first = sb("first", [P, T, 16])
        second = sb("second", [P, T, 16])
        chosen = sb("chosen", [P, T, 16])
        comb = sb("comb", [P, T, 16])
        most = sb("most", [P, T])
        peak = sb("peak", [P, T])
        total = sb("total", [P, T])
        total2 = sb("total2", [P, T])
        constants = sem("constants")
        router_logits = sem("router_logits")
        comb_parts = sem("comb_parts")
        comb_parts_ps = sem("comb_parts_ps")
        comb_rows = sem("comb_rows")
        gate_shifted = sem("gate_shifted")
        gate_exp = sem("gate_exp")

        def rev_pool():
            for e in range(16):
                ins = nc.gpsimd.memset(rev[:, :, e], 16.0 - e)
            ins.then_inc(constants, 1)

        def top2_dve(link, values, E):
            v = values
            for pick in (first, second):
                link(nc.vector.tensor_reduce(most[:], v[:, :, 0:E], X, ALU.max))
                link(nc.vector.tensor_tensor(equal[:, :, 0:E], v[:, :, 0:E], wide(most[:], E), ALU.is_equal))
                link(nc.vector.tensor_tensor(equal[:, :, 0:E], equal[:, :, 0:E], rev[:, :, 0:E], ALU.mult))
                link(nc.vector.tensor_reduce(most[:], equal[:, :, 0:E], X, ALU.max))
                link(nc.vector.tensor_tensor(pick[:, :, 0:E], equal[:, :, 0:E], wide(most[:], E), ALU.is_equal))
                if pick is first:
                    link(nc.vector.scalar_tensor_tensor(out=left[:, :, 0:E], in0=first[:, :, 0:E], scalar=-BIG,
                                                        in1=v[:, :, 0:E], op0=ALU.mult, op1=ALU.add))
                    v = left
            link(nc.vector.tensor_tensor(chosen[:, :, 0:E], first[:, :, 0:E], second[:, :, 0:E], ALU.add))

        def shift_dve(link, values, E):
            link(nc.vector.tensor_reduce(peak[:], values[:, :, 0:E], X, ALU.max))
            nc.vector.tensor_tensor(shifted[:, :, 0:E], values[:, :, 0:E], wide(peak[:], E), ALU.subtract).then_inc(gate_shifted, 1)

        def gate_act(act, n, E):
            act.wait_ge(gate_shifted, n)
            nc.scalar.activation(gate[:, :, 0:E], shifted[:, :, 0:E], ACT.Exp).then_inc(gate_exp, 1)

        def weights_dve(link, E, eps_of_all=0.0, eps=0.0):
            link(nc.vector.tensor_tensor(comb[:, :, 0:E], gate[:, :, 0:E], chosen[:, :, 0:E], ALU.mult))
            link(nc.vector.tensor_reduce(total[:], comb[:, :, 0:E], X, ALU.add))
            if eps_of_all:
                link(nc.vector.tensor_reduce(total2[:], gate[:, :, 0:E], X, ALU.add))
                link(nc.vector.scalar_tensor_tensor(out=total[:], in0=total2[:], scalar=eps_of_all, in1=total[:],
                                                    op0=ALU.mult, op1=ALU.add))
            if eps:
                link(nc.vector.tensor_scalar(total[:], total[:], eps, None, ALU.add))
            link(nc.vector.reciprocal(total[:], total[:]))
            link(nc.vector.tensor_tensor(comb[:, :, 0:E], comb[:, :, 0:E], wide(total[:], E), ALU.mult))

        E1 = 8
        we = place_weights(5888, [P, E1, D])
        L1_BANK = (0, 1, 2, 3, 4, 5, 7, 0)
        weighted1 = place(0, [P, T * 4, D]).rearrange("p (t q) d -> p t q d", q=4)
        weT = place_weights(6912, [P, E1, D])
        wg1 = sb("wg1", [P, E1])
        bg1 = sb("bg1", [P, E1])
        be1 = sb("be1", [E1, D])
        combT = sb("combT", [16, N])
        l1_we_turned = sem("l1_we_turned")
        l1_weT = sem("l1_weT")
        l1_comb = sem("l1_comb")
        l1_combT_ps = sem("l1_combT_ps")
        l1_combT = sem("l1_combT")
        l1_bias = sem("l1_bias")
        l1_y = sem("l1_y")
        l1_used = sem("l1_used")
        l1_weighted = sem("l1_weighted")
        l1_summed = sem("l1_summed")

        def l1_prepare_pe(pe):
            pe.wait_ge(early_loaded, 16 * 15)
            for half in range(2):
                for q in range(4):
                    ins = nc.tensor.transpose(bank(half)[:, q * P:(q + 1) * P], we[:, 4 * half + q, :], ident[:])
                ins.then_inc(l1_we_turned, 1)

        def l1_prepare_act(act):
            for half in range(2):
                act.wait_ge(l1_we_turned, half + 1)
                act_copy(weT[:, 4 * half:4 * half + 4, :], quarters(half)).then_inc(l1_weT, 1)

        def l1_pe(pe):
            pe.wait_ge(ln_xT, 2)
            for t in range(T):
                ins = nc.tensor.matmul(bank(6)[:, t * E1:(t + 1) * E1], xT[:, t * P:(t + 1) * P], wg1[:], start=True, stop=True)
            ins.then_inc(router_logits, 1)
            pe.wait_ge(l1_weT, 2)
            for g in range(7):
                half, t = g // T, g % T
                nc.tensor.matmul(bank(L1_BANK[g]), xT[:, t * P:(t + 1) * P], weT[:, 4 * half:4 * half + 4, :],
                                 start=True, stop=True).then_inc(l1_y, 1)
            pe.wait_ge(l1_comb, 1)
            for t in range(T):
                ins = nc.tensor.transpose(bank(6)[0:E1, t * P:(t + 1) * P], comb[:, t, 0:E1], ident[:])
            ins.then_inc(l1_combT_ps, 1)
            pe.wait_ge(l1_combT, 1)
            for t in range(T):
                ins = nc.tensor.matmul(bank(6)[:, t * P:(t + 1) * P], combT[0:E1, t * P:(t + 1) * P], be1[:], start=True, stop=True)
            ins.then_inc(l1_bias, 1)
            pe.wait_ge(l1_used, 1)
            nc.tensor.matmul(bank(L1_BANK[7]), xT[:, 3 * P:4 * P], weT[:, 4:8, :], start=True, stop=True).then_inc(l1_y, 1)
            pe.wait_ge(l1_used, 2)
            l2_key_pe(pe)

        def l1_dve(dve, link):
            dve.wait_ge(early_loaded, 16 * 15)
            dve.wait_ge(constants, 1)
            dve.wait_ge(router_logits, 1)
            link(nc.vector.tensor_tensor(logits[:, :, 0:E1], bank(6)[:, 0:T * E1].rearrange("p (t e) -> p t e", t=T),
                                         bg1[:].unsqueeze(1).broadcast_to([P, T, E1]), ALU.add))
            shift_dve(link, logits, E1)
            dve.wait_ge(gate_exp, 1)
            top2_dve(link, gate, E1)
            weights_dve(link, E1)
            dve.sem_inc(l1_comb, 1)
            dve.wait_ge(l1_bias, 1)
            link(nc.vector.tensor_tensor(x[:], x[:], quarters(6), ALU.add))
            for tiles in ((0,), (1, 2, 3)):
                for e in range(4):
                    for t in tiles:
                        dve.wait_ge(l1_y, t + 1)
                        ins = nc.vector.scalar_tensor_tensor(out=x[:, t, :], in0=quarters(t)[:, e, :], scalar=comb[:, t, e:e + 1],
                                                             in1=x[:, t, :], op0=ALU.mult, op1=ALU.add)
                    if e < 3:
                        link(ins)
                ins.then_inc(l1_used, 1)
            dve.wait_ge(l1_used, 2)
            for t in range(T):
                dve.wait_ge(l1_summed, 2 * t + 2)
                nc.vector.tensor_tensor(x[:, t, :], x[:, t, :], weighted1[:, t, 0, :], ALU.add).then_inc(x_updated, 1)

        def l1_act(act):
            act.wait_ge(l1_combT_ps, 1)
            act_copy(combT[0:E1, :], bank(6)[0:E1, :]).then_inc(l1_combT, 1)
            for t in range(T):
                act.wait_ge(l1_y, T + t + 1)
                for q in range(4):
                    ins = nc.scalar.activation(weighted1[:, t, q, :], quarters(L1_BANK[T + t])[:, q, :], ACT.Copy,
                                               scale=comb[:, t, 4 + q:5 + q])
                ins.then_inc(l1_weighted, 1)

        def l1_pool(pool):
            for t in range(T):
                pool.wait_ge(l1_weighted, t + 1)
                for n in (2, 1):
                    if n == 1:
                        pool.wait_ge(l1_summed, 2 * t + 1)
                    nc.gpsimd.tensor_tensor(weighted1[:, t, 0:n, :], weighted1[:, t, 0:n, :], weighted1[:, t, n:2 * n, :],
                                            ALU.add).then_inc(l1_summed, 1)

        S2 = float(D) ** -0.5
        wq2 = sb("wq2", [P, D])
        wk2 = sb("wk2", [C, D])
        wv2 = sb("wv2", [C, D])
        bq2 = sb("bq2", [P, 1])
        bk2 = sb("bk2", [P, 1])
        bv2 = sb("bv2", [P, D])
        queryT = sb("queryT", [P, N])
        keyT = place(4096, [P, M])
        value = place(5120, [P, MT, D])
        att = place(0, [P, T, KB])
        attT = place(2048, [P, T, KB]).rearrange("p t (k q) -> p t k q", q=P)
        l2_kv_ps = sem("l2_kv_ps")
        l2_keyT = sem("l2_keyT")
        l2_value = sem("l2_value")
        l2_query_ps = sem("l2_query_ps")
        l2_query = sem("l2_query")
        att_scores = sem("att_scores")
        att_negmax = sem("att_negmax")
        att_exp = sem("att_exp")
        att_ready = sem("att_ready")
        att_turned = sem("att_turned")
        att_copied = [sem("att_copied_even"), sem("att_copied_odd")]
        att_out = sem("att_out")

        def l2_key_pe(pe):
            for half in range(2):
                nc.tensor.matmul(bank(2 + half), wk2[:], ctxT[:, half * 512:(half + 1) * 512],
                                 start=True, stop=True).then_inc(l2_kv_ps, 1)

        def l2_value_pe(pe):
            pe.wait_ge(x_updated, 2 * T)
            for half in range(2):
                for q in range(4):
                    k = 4 * half + q
                    ins = nc.tensor.matmul(bank(4 + half)[:, q * P:(q + 1) * P], ctxT[:, k * P:(k + 1) * P], wv2[:],
                                           start=True, stop=True)
                ins.then_inc(l2_kv_ps, 1)

        def l2_prepare_act(act):
            act.wait_ge(early_loaded, 16 * 15)
            for half in range(2):
                act.wait_ge(l2_kv_ps, half + 1)
                nc.scalar.activation(keyT[:, half * 512:(half + 1) * 512], bank(2 + half), ACT.Identity,
                                     bias=bk2[:]).then_inc(l2_keyT, 1)

        def l2_prepare_dve(dve):
            dve.wait_ge(early_loaded, 16 * 15)
            for half in range(2):
                dve.wait_ge(l2_kv_ps, half + 3)
                nc.vector.tensor_tensor(value[:, 4 * half:4 * half + 4, :], quarters(4 + half),
                                        bv2[:].unsqueeze(1).broadcast_to([P, 4, D]), ALU.add).then_inc(l2_value, 1)

        def att_scores_pe(pe, n, qT, kT, keys):
            for t in range(T):
                b = t // 2
                nc.tensor.matmul(bank(t)[:, 0:keys], qT[:, t * P:(t + 1) * P], kT[:, b * keys:(b + 1) * keys],
                                 start=True, stop=True).then_inc(att_scores, 1)

        def att_turn_pe(pe, n, t, keys, ready, count):
            pe.wait_ge(ready, count + t + 1)
            if T * n + t >= 2:
                pe.wait_ge(att_copied[t % 2], 2 * n + t // 2)
            for k in range(keys // P):
                ins = nc.tensor.transpose(bank(4 + t % 2)[:, k * P:(k + 1) * P], att[:, t, k * P:(k + 1) * P], ident[:])
            ins.then_inc(att_turned, 1)

        def att_out_pe(pe, n, t, keys, v):
            pe.wait_ge(att_copied[t % 2], 2 * n + t // 2 + 1)
            K = keys // P
            for k in range(K):
                ins = nc.tensor.matmul(bank(6)[:, t * P:(t + 1) * P], attT[:, t, k, :], v[:, K * (t // 2) + k, :],
                                       start=(k == 0), stop=(k == K - 1))
            ins.then_inc(att_out, 1)

        def att_max_dve(dve, link, n, t, keys, scale):
            dve.wait_ge(att_scores, T * n + t + 1)
            link(nc.vector.tensor_reduce(row_max[:, t:t + 1], bank(t)[:, 0:keys], X, ALU.max))
            nc.vector.tensor_scalar(neg_max[:, t:t + 1], row_max[:, t:t + 1], -scale, None, ALU.mult).then_inc(att_negmax, 1)

        def att_copy(eng, copy, n, t, keys):
            eng.wait_ge(att_turned, T * n + t + 1)
            copy(attT[:, t, 0:keys // P, :], bank(4 + t % 2)[:, 0:keys].rearrange("p (k q) -> p k q", q=P)).then_inc(att_copied[t % 2], 1)

        def att_exp_act(act, n, keys, scale):
            for t in range(T):
                act.wait_ge(att_negmax, T * n + t + 1)
                nc.scalar.activation(att[:, t, 0:keys], bank(t)[:, 0:keys], ACT.Exp, bias=neg_max[:, t:t + 1], scale=scale,
                                     accum_out=row_sum[:, t:t + 1]).then_inc(att_exp, 1)

        def l2_pe(pe):
            pe.wait_ge(ln_xT, 3)
            nc.tensor.matmul(bank(6), wq2[:], xT[:], start=True, stop=True).then_inc(l2_query_ps, 1)
            pe.wait_ge(l2_keyT, 2)
            pe.wait_ge(l2_value, 2)
            pe.wait_ge(l2_query, 1)
            att_scores_pe(pe, 0, queryT, keyT, KB)
            for t in range(T):
                att_turn_pe(pe, 0, t, KB, att_exp, 0)
                if t >= 1:
                    att_out_pe(pe, 0, t - 1, KB, value)
            att_out_pe(pe, 0, T - 1, KB, value)

        def l2_act(act):
            act.wait_ge(l2_query_ps, 1)
            nc.scalar.activation(queryT[:], bank(6), ACT.Identity, bias=bq2[:]).then_inc(l2_query, 1)
            att_exp_act(act, 0, KB, S2)
            for t in (0, 2):
                att_copy(act, act_copy, 0, t, KB)

        def l2_dve(dve, link):
            for t in range(T):
                att_max_dve(dve, link, 0, t, KB, S2)
            for t in (1, 3):
                att_copy(dve, nc.vector.tensor_copy, 0, t, KB)
            link(nc.vector.reciprocal(row_inv[:], row_sum[:]))
            dve.wait_ge(att_out, T)
            for t in range(T):
                nc.vector.scalar_tensor_tensor(out=x[:, t, :], in0=quarters(6)[:, t, :], scalar=row_inv[:, t:t + 1],
                                               in1=x[:, t, :], op0=ALU.mult, op1=ALU.add).then_inc(x_updated, 1)

        E3 = 8
        H3 = 256
        room2 = sb("room2", [P, 8192])
        w1 = room2[:, 0:4096].rearrange("p (e c d) -> p e c d", e=E3, c=4)
        w1T = room2[:, 4096:8192].rearrange("p (e h) -> p e h", e=E3)
        wg3 = sb("wg3", [E3, D])
        wg3T = sb("wg3T", [P, E3])
        wo3 = sb("wo3", [P, H3])
        wo3T = sb("wo3T", [P, 2, D])
        bo3 = sb("bo3", [P, D])
        b1 = sb("b1", [E3, 2 * H3])
        b1_hi = sb("b1_hi", [E3, 2 * H3], BF16)
        b1_mid = sb("b1_mid", [E3, 2 * H3], BF16)
        b1_lo = sb("b1_lo", [E3, 2 * H3], BF16)
        b1_rows = sb("b1_rows", [3, E3, 2 * H3], BF16)
        ones3 = sb("ones3", [3, P], BF16)
        sig = place(4096, [P, T, H3])
        gated = place(5120, [P, T, H3])
        mixed = place(6144, [P, T, H3])
        mixedT = place(7168, [P, 2, N])
        l3_b1_parts = sem("l3_b1_parts")
        l3_b1_rows = sem("l3_b1_rows")
        l3_w_turned = sem("l3_w_turned")
        l3_w = sem("l3_w")
        l3_hidden = sem("l3_hidden")
        l3_sig = sem("l3_sig")
        l3_used = sem("l3_used")
        l3_mixed = sem("l3_mixed")
        l3_turned = sem("l3_turned")
        l3_mixedT = sem("l3_mixedT")
        l3_out = sem("l3_out")

        def l3_parts_dve(dve, link):
            dve.wait_ge(early_loaded, 16 * 15)
            link(nc.vector.tensor_copy(b1_hi[:], b1[:]))
            link(nc.vector.tensor_tensor(b1[:], b1[:], b1_hi[:], ALU.subtract))
            link(nc.vector.tensor_copy(b1_mid[:], b1[:]))
            link(nc.vector.tensor_tensor(b1[:], b1[:], b1_mid[:], ALU.subtract))
            nc.vector.memset(ones3[:], 1.0)
            nc.vector.tensor_copy(b1_lo[:], b1[:]).then_inc(l3_b1_parts, 1)

        def l3_prepare_pe(pe):
            pe.wait_ge(early_loaded, 16 * 15)
            pe.wait_ge(x_updated, 3 * T)
            nc.tensor.transpose(bank(4)[:, 0:E3], wg3[:], ident[0:E3, 0:E3])
            for k in range(2):
                ins = nc.tensor.transpose(bank(4)[:, (k + 1) * P:(k + 2) * P], wo3[:, k * P:(k + 1) * P], ident[:])
            ins.then_inc(l3_w_turned, 1)

        def l3_w1_pe(pe):
            for e in range(E3):
                if e >= 4:
                    pe.wait_ge(l3_w, 2 + e - 3)
                for c in range(4):
                    ins = nc.tensor.transpose(bank(e % 4)[:, c * P:(c + 1) * P], w1[:, e, c, :], ident[:])
                ins.then_inc(l3_w_turned, 1)

        def l3_prepare_act(act):
            act.wait_ge(l3_w_turned, 1)
            act_copy(wg3T[:], bank(4)[:, 0:E3]).then_inc(l3_w, 1)
            act_copy(wo3T[:], bank(4)[:, P:3 * P].rearrange("p (k d) -> p k d", k=2)).then_inc(l3_w, 1)

        def l3_w1_act(act):
            for e in range(E3):
                act.wait_ge(l3_w_turned, e + 2)
                act_copy(w1T[:, e, :], bank(e % 4)).then_inc(l3_w, 1)

        def l3_pe(pe):
            pe.wait_ge(ln_xT, 4)
            pe.wait_ge(l3_w, 2)
            for t in range(T):
                ins = nc.tensor.matmul(bank(6)[:, t * E3:(t + 1) * E3], xT[:, t * P:(t + 1) * P], wg3T[:], start=True, stop=True)
            ins.then_inc(router_logits, 1)
            l3_w1_pe(pe)
            pe.wait_ge(l3_w, 2 + E3)
            pe.wait_ge(l3_b1_rows, 16 * 3)
            with pe.Fori(0, E3) as e:
                for t in range(T):
                    pe.wait_ge(l3_used, T * e + (t + 1))
                    nc.tensor.matmul(bank(t), xT[:, t * P:(t + 1) * P], w1T[:, bass.ds(e, 1), :], start=True, stop=False)
                    nc.tensor.matmul(bank(t), ones3[:], b1_rows[:, bass.ds(e, 1), :], start=False, stop=True).then_inc(l3_hidden, 1)
            for k in range(2):
                for t in range(T):
                    pe.wait_ge(l3_mixed, T * E3 + t + 1)
                    ins = nc.tensor.transpose(bank(4 + k)[:, t * P:(t + 1) * P], mixed[:, t, k * P:(k + 1) * P], ident[:])
                ins.then_inc(l3_turned, 1)
            pe.wait_ge(l3_mixedT, 2)
            for t in range(T):
                for k in range(2):
                    ins = nc.tensor.matmul(bank(6)[:, t * P:(t + 1) * P], mixedT[:, k, t * P:(t + 1) * P], wo3T[:, k, :],
                                           start=(k == 0), stop=(k == 1))
            ins.then_inc(l3_out, 1)

        def l3_act(act):
            l3_w1_act(act)
            with act.Fori(0, E3) as e:
                for t in range(T):
                    act.wait_ge(l3_hidden, T * e + (t + 1))
                    nc.scalar.activation(sig[:, t, :], bank(t)[:, H3:2 * H3], ACT.Sigmoid).then_inc(l3_sig, 1)
            for k in range(2):
                act.wait_ge(l3_turned, k + 1)
                act_copy(mixedT[:, k, :], bank(4 + k)).then_inc(l3_mixedT, 1)

        def l3_dve(dve, link):
            dve.sem_inc(l3_used, T)
            for t in range(T):
                nc.vector.memset(mixed[:, t, :], 0.0).then_inc(l3_mixed, 1)
            dve.wait_ge(router_logits, 2)
            link(nc.vector.tensor_copy(logits[:, :, 0:E3], bank(6)[:, 0:T * E3].rearrange("p (t e) -> p t e", t=T)))
            shift_dve(link, logits, E3)
            dve.wait_ge(gate_exp, 2)
            top2_dve(link, gate, E3)
            weights_dve(link, E3, eps_of_all=1e-9)
            link(nc.vector.tensor_reduce(total[:], comb[:, :, 0:E3], X, ALU.add))
            for t in range(T):
                ins = nc.vector.scalar_tensor_tensor(out=x[:, t, :], in0=bo3[:], scalar=total[:, t:t + 1], in1=x[:, t, :],
                                                     op0=ALU.mult, op1=ALU.add)
            link(ins)
            with dve.Fori(0, E3) as e:
                for t in range(T + 1):
                    if t < T:
                        dve.wait_ge(l3_sig, T * e + (t + 1))
                        nc.vector.tensor_tensor(gated[:, t, :], bank(t)[:, 0:H3], sig[:, t, :], ALU.mult).then_inc(l3_used, 1)
                    if t >= 1:
                        u = t - 1
                        dve.wait_ge(l3_used, T * e + (T + u + 1))
                        dve.wait_ge(l3_mixed, T * e + (u + 1))
                        nc.vector.scalar_tensor_tensor(out=mixed[:, u, :], in0=gated[:, u, :], scalar=comb[:, u, bass.ds(e, 1)],
                                                       in1=mixed[:, u, :], op0=ALU.mult, op1=ALU.add).then_inc(l3_mixed, 1)
            l5_squares_dve(dve)
            dve.wait_ge(l3_out, 1)
            for t in range(T):
                nc.vector.tensor_tensor(x[:, t, :], x[:, t, :], quarters(6)[:, t, :], ALU.add).then_inc(x_updated, 1)

        S4 = float(D) ** -0.5
        F4 = 512
        D2V, IMG, TXT, ATT0, ATT1, FF1, FF2 = range(7)
        wd4 = sb("wd4", [P, C])
        wi4 = sb("wi4", [P, D])
        wt4 = sb("wt4", [P, D])
        wa4 = sb("wa4", [64, 2, D])
        wf14 = sb("wf14", [P, 4, 2 * D])
        wf24 = sb("wf24", [P, F4])
        bd4 = sb("bd4", [P, 1])
        bi4 = sb("bi4", [P, 1])
        bt4 = sb("bt4", [P, 1])
        ba4 = sb("ba4", [P, 2])
        ba4_rows = sb("ba4_rows", [P, 2, 64])
        bf14 = sb("bf14", [P, 4])
        bf24 = sb("bf24", [P, D])
        below = place(9728, [P, 4 * 2 * D])
        td4 = sb("td4", [P, C], BF16)
        ti4 = sb("ti4", [P, D], BF16)
        tt4 = sb("tt4", [P, D], BF16)
        ta4 = sb("ta4", [64, 2, D], BF16)
        tf14 = sb("tf14", [P, 4, 2 * D], BF16)
        tf24 = sb("tf24", [P, F4], BF16)
        tdT = sb("tdT", [C, D], BF16)
        tiT = sb("tiT", [P, D], BF16)
        ttT = sb("ttT", [P, D], BF16)
        taT = sb("taT", [P, 2, 2, 64], BF16)
        tf1T = sb("tf1T", [P, 2, F4], BF16)
        tf2T = sb("tf2T", [P, 4, D], BF16)
        abs_sum = sb("abs_sum", [P, 7])
        one_over = sb("one_over", [P, 7])
        ones = sb("ones", [P, P])
        w_scale = sb("w_scale", [P, 7])
        w_above = sb("w_above", [P, 7])
        w_below = sb("w_below", [P, 7])
        part_max = sb("part_max", [P, 8])
        chunk_max = sb("chunk_max", [P, 4])
        whole_max = sb("whole_max", [P, 8])
        i_scale = sb("i_scale", [P, 8])
        i_inv = sb("i_inv", [P, 8])
        both = sb("both", [P, 8])
        rounded = place(4096, [P, 4 * N])
        ints = sb("ints", [P, 4 * N], BF16)
        rounded_ctx = place(7168, [P, M])
        ctx_feat = place(6144, [P, M])
        key4 = room2[:, 0:2048].rearrange("p (l k) -> p l k", l=2)
        value4 = room2[:, 2048:4096].rearrange("p (l k d) -> p l k d", l=2, d=D)
        cat = sb("cat", [P, N + B])
        hid4 = place(6144, [P, 4, N])
        l4_loaded = sem("l4_loaded")
        l4_ba = sem("l4_ba")
        l4_sums = sem("l4_sums")
        l4_sums_ps = sem("l4_sums_ps")
        l4_ternary = sem("l4_ternary")
        l4_w_turned = sem("l4_w_turned")
        l4_wT = sem("l4_wT")
        l4_part_max = sem("l4_part_max")
        l4_whole_max = sem("l4_whole_max")
        l4_ints = sem("l4_ints")
        l4_both = sem("l4_both")
        l4_ps = sem("l4_ps")
        l4_feat = sem("l4_feat")
        l4_value = sem("l4_value")
        l4_fused = sem("l4_fused")
        l4_inv = sem("l4_inv")
        l4_ints_last = sem("l4_ints_last")

        def l4_const_pool():
            for j, size in ((D2V, D * C), (IMG, D * D), (TXT, D * D), (ATT0, 64 * D), (ATT1, 64 * D), (FF1, F4 * 2 * D), (FF2, D * F4)):
                nc.gpsimd.memset(one_over[:, j:j + 1], 1.0 / size)
            nc.gpsimd.memset(abs_sum[:], 0.0)
            nc.gpsimd.memset(part_max[:], 0.0)
            nc.gpsimd.memset(ones[:], 1.0).then_inc(constants, 1)

        def ternary(link, w, q, j, rows, size):
            link(nc.vector.tensor_scalar(below[0:rows, 0:size], w, w_below[0:rows, j:j + 1], None, ALU.is_lt))
            link(nc.vector.scalar_tensor_tensor(out=q, in0=w, scalar=w_above[0:rows, j:j + 1], in1=below[0:rows, 0:size],
                                                op0=ALU.is_gt, op1=ALU.subtract))

        def l4_sums_dve(weights):
            for w, j in weights:
                axis = mybir.AxisListType.XY if w is wf14 else X
                ins = nc.vector.tensor_reduce(abs_sum[:, j:j + 1], w[:], axis, ALU.add, apply_absolute_value=True)
            return ins

        def l4_early_dve(dve, link, h, window):
            step = (h, window) if isinstance(h, int) else None
            if step == (3, 1):
                dve.wait_ge(l4_loaded, 16 * 17)
                dve.wait_ge(constants, 2)
                abs_max_dve(0, ctxT[:], rows=C)
                l4_sums_dve(((wd4, D2V), (wi4, IMG), (wt4, TXT)))
            elif step == (3, 2):
                l4_sums_dve(((wf24, FF2), (wf14, FF1)))
                nc.vector.tensor_reduce(abs_sum[0:64, ATT0:ATT1 + 1], wa4[:], X, ALU.add, apply_absolute_value=True).then_inc(l4_sums, 1)
            elif step == (4, 0):
                dve.wait_ge(l4_sums_ps, 1)
                link(nc.vector.tensor_tensor(w_scale[:], bank(7)[:, 0:7], one_over[:], ALU.mult))
                dve.sem_inc(l4_ternary, 1)
                link(nc.vector.tensor_scalar(w_scale[:], w_scale[:], 1e-5, None, ALU.max))
                link(nc.vector.tensor_scalar(w_above[:], w_scale[:], 0.5, None, ALU.mult))
                link(nc.vector.tensor_scalar(w_below[:], w_scale[:], -0.5, None, ALU.mult))
            elif step == (4, 1):
                ternary(link, wd4[:], td4[:], D2V, P, C)
                ternary(link, wi4[:], ti4[:], IMG, P, D)
                ternary(link, wt4[:], tt4[:], TXT, P, D)
            elif step == (4, 2):
                for l in range(2):
                    ternary(link, wa4[:, l, :], ta4[:, l, :], ATT0 + l, 64, D)
                ternary(link, wf24[:], tf24[:], FF2, P, F4)
                dve.sem_inc(l4_ternary, 1)
            elif step == (5, 1):
                ternary(link, wf14[:].rearrange("p c i -> p (c i)"), tf14[:].rearrange("p c i -> p (c i)"), FF1, P, 4 * 2 * D)
                dve.sem_inc(l4_ternary, 1)
            elif step == (5, 2):
                scale_dve(dve, link, 0, D2V)
                ints_dve(link, 0, ctxT[:], M, rows=C, work=rounded_ctx)
            elif step == (6, 1):
                dve.wait_ge(l4_feat, 2)
                abs_max_dve(1, ctx_feat[:])
            elif step == (6, 2):
                scale_dve(dve, link, 1, IMG)
                ints_dve(link, 1, ctx_feat[:], M, work=rounded_ctx)
            elif step == (7, 1):
                dve.wait_ge(l4_feat, 4)
                abs_max_dve(2, ctx_feat[:])
                link(nc.vector.tensor_reduce(cat[:, N:N + B], ctx_feat[:].rearrange("p (b k) -> p b k", b=B), X, ALU.add))
                link(nc.vector.tensor_scalar(cat[:, N:N + B], cat[:, N:N + B], 1.0 / KB, None, ALU.mult))
            elif step == (7, 2):
                scale_dve(dve, link, 2, ATT0)
                nc.vector.tensor_tensor(both[:, 6:7], i_scale[:, 2:3], w_scale[:, ATT1:ATT1 + 1], ALU.mult).then_inc(l4_both, 1)
                ints_dve(link, 2, ctx_feat[:], M, work=rounded_ctx)

        def l4_early_pe(pe, h, point):
            step = (h, point) if isinstance(h, int) else None
            if step == (4, 0):
                pe.wait_ge(l4_sums, 1)
                nc.tensor.matmul(bank(7)[:, 0:7], ones[:], abs_sum[:], start=True, stop=True).then_inc(l4_sums_ps, 1)
            elif step == (4, 2):
                pe.wait_ge(l4_ternary, 1)
            elif step == (5, 0):
                pe.wait_ge(l4_ternary, 2)
                b7 = bank(7).bitcast(BF16)
                nc.tensor.transpose(b7[0:C, 0:P], td4[:], identb[:])
                nc.tensor.transpose(b7[:, P:2 * P], ti4[:], identb[:])
                nc.tensor.transpose(b7[:, 2 * P:3 * P], tt4[:], identb[:])
                for l in range(2):
                    nc.tensor.transpose(b7[:, 3 * P + 64 * l:3 * P + 64 * (l + 1)], ta4[:, l, :], identb[0:64, 0:64])
                for c in range(4):
                    ins = nc.tensor.transpose(b7[:, (4 + c) * P:(5 + c) * P], tf24[:, c * P:(c + 1) * P], identb[:])
                ins.then_inc(l4_w_turned, 1)
            elif step == (5, 2):
                pe.wait_ge(l4_wT, 1)
            elif step == (6, 2):
                pe.wait_ge(l4_feat, 2)
            elif step in ((6, 0), (6, 1), (7, 0), (7, 1)):
                n = 2 * (h - 6) + point
                w, rows = ((tdT, C), (tiT, P))[n // 2]
                pe.wait_ge(l4_ints, n // 2 + 1)
                if n > 0:
                    pe.wait_ge(l4_feat, n)
                half = n % 2
                nc.tensor.matmul(bank(7), w[:], ints[0:rows, half * 512:(half + 1) * 512], start=True, stop=True).then_inc(l4_ps, 1)

        def l4_early_act(act, h, point):
            step = (h, point) if isinstance(h, int) else None
            if step == (5, 0):
                act.wait_ge(l4_w_turned, 1)
                b7 = bank(7).bitcast(BF16)
                act_copy(tdT[:], b7[0:C, 0:P])
                act_copy(tiT[:], b7[:, P:2 * P])
                act_copy(ttT[:], b7[:, 2 * P:3 * P])
                for copy in range(2):
                    act_copy(taT[:, :, copy, :], b7[:, 3 * P:4 * P].rearrange("p (l o) -> p l o", l=2))
                act_copy(tf2T[:], b7[:, 4 * P:8 * P].rearrange("p (c o) -> p c o", c=4)).then_inc(l4_wT, 1)
            elif step in ((6, 0), (6, 1), (7, 0), (7, 1)):
                n = 2 * (h - 6) + point
                act.wait_ge(l4_ps, n + 1)
                act.wait_ge(l4_both, n // 2 + 1)
                half = n % 2
                nc.scalar.activation(ctx_feat[:, half * 512:(half + 1) * 512], bank(7), ACT.Identity,
                                     bias=(bd4, bi4)[n // 2][:], scale=both[:, n // 2:n // 2 + 1]).then_inc(l4_feat, 1)

        def scale_dve(dve, link, n, weight, both_now=True):
            dve.wait_ge(l4_whole_max, n + 1)
            link(nc.vector.tensor_scalar(i_scale[:, n:n + 1], whole_max[:, n:n + 1], 1e-8, 1.0 / 127.0, ALU.max, ALU.mult))
            link(nc.vector.reciprocal(i_inv[:, n:n + 1], i_scale[:, n:n + 1]))
            if both_now:
                both_dve(n, weight)

        def both_dve(n, weight):
            nc.vector.tensor_tensor(both[:, n:n + 1], i_scale[:, n:n + 1], w_scale[:, weight:weight + 1], ALU.mult).then_inc(l4_both, 1)

        def ints_dve(link, n, src, size, rows=P, work=None, at_word=0):
            work = rounded if work is None else work
            w, q = work[0:rows, at_word:at_word + size], ints[0:rows, at_word:at_word + size]
            link(nc.vector.tensor_scalar(w, src, i_inv[0:rows, n:n + 1], ROUND, ALU.mult, ALU.add))
            link(nc.vector.tensor_scalar(w, w, ROUND + 127.0, ROUND - 128.0, ALU.min, ALU.max))
            nc.vector.tensor_scalar(q, w, ROUND, None, ALU.subtract).then_inc(l4_ints, 1)

        def l4_ints_pool(pool, link):
            pool.wait_ge(l4_inv, 1)
            pool.wait_ge(l4_feat, 11)
            w = rounded[:, 3 * N:4 * N]
            link(nc.gpsimd.tensor_scalar(w, hid4[:, 3, :], i_inv[:, 5:6], ROUND, ALU.mult, ALU.add))
            link(nc.gpsimd.tensor_scalar(w, w, ROUND + 127.0, ROUND - 128.0, ALU.min, ALU.max))
            nc.gpsimd.tensor_scalar(ints[:, 3 * N:4 * N], w, ROUND, None, ALU.subtract).then_inc(l4_ints_last, 1)

        def abs_max_dve(n, src, rows=P, axis=X):
            nc.vector.tensor_reduce(part_max[0:rows, n:n + 1], src, axis, ALU.max, apply_absolute_value=True).then_inc(l4_part_max, 1)

        def whole_max_pool(pool, n):
            pool.wait_ge(l4_part_max, n + 1)
            nc.gpsimd.partition_all_reduce(whole_max[:, n:n + 1], part_max[:, n:n + 1], P, RMAX).then_inc(l4_whole_max, 1)

        def l4_ctx_dve(dve):
            for l in range(2):
                dve.wait_ge(l4_ps, 7 + l)
                for copy in range(2):
                    nc.vector.scalar_tensor_tensor(
                        out=value4[:, l, :, 64 * copy:64 * (copy + 1)], in0=bank(4 + l).rearrange("p (k o) -> p k o", k=MT),
                        scalar=both[:, (2, 6)[l]:(2, 6)[l] + 1],
                        in1=ba4_rows[:, l, :].unsqueeze(1).broadcast_to([P, MT, 64]), op0=ALU.mult, op1=ALU.add).then_inc(l4_value, 1)

        def l4_ctx_pe(pe):
            pe.wait_ge(x_updated, 4 * T)
            pe.wait_ge(l4_ints, 3)
            for l in range(2):
                for half in range(2):
                    ins = nc.tensor.matmul(bank(2 * l + half), taT[:, l, :, :], ints[:, half * 512:(half + 1) * 512], start=True, stop=True)
                ins.then_inc(l4_ps, 1)
            for l in range(2):
                for k in range(MT):
                    ins = nc.tensor.matmul(bank(4 + l)[:, k * 64:(k + 1) * 64], ints[:, k * P:(k + 1) * P], taT[:, l, 0, :], start=True, stop=True)
                ins.then_inc(l4_ps, 1)
            b6 = bank(6).bitcast(BF16)
            for half in range(2):
                for c in range(4):
                    ins = nc.tensor.transpose(b6[:, (4 * half + c) * P:(4 * half + c + 1) * P], tf14[:, c, half * P:(half + 1) * P], identb[:])
            ins.then_inc(l4_w_turned, 1)

        def l4_ctx_act(act):
            act.wait_ge(l4_both, 4)
            act.wait_ge(l4_ba, 16 * 4)
            for l in range(2):
                act.wait_ge(l4_ps, 5 + l)
                nc.scalar.activation(key4[:, l, :].rearrange("p (b k) -> p b k", b=2), PS[:, 2 * l:2 * l + 2, :], ACT.Identity,
                                     bias=ba4[:, l:l + 1], scale=both[:, (2, 6)[l]:(2, 6)[l] + 1]).then_inc(l4_feat, 1)
            act.wait_ge(l4_w_turned, 2)
            act_copy(tf1T[:], bank(6).bitcast(BF16).rearrange("p (h f) -> p h f", h=2)).then_inc(l4_wT, 1)

        def l4_dve(dve, link):
            dve.wait_ge(ln_rows, 5 * T)
            abs_max_dve(3, xn[:], axis=mybir.AxisListType.XY)
            dve.wait_ge(ln_xT, 5)
            scale_dve(dve, link, 3, TXT, both_now=False)
            dve.wait_ge(l4_ps, 8)
            ints_dve(link, 3, xT[:], N)
            both_dve(3, TXT)
            l4_ctx_dve(dve)
            l5_norm_dve(dve)
            for l in range(2):
                n = l + 1
                for t in range(T):
                    att_max_dve(dve, link, n, t, KB, S4)
                for t in range(T):
                    dve.wait_ge(att_exp, T * n + t + 1)
                    link(nc.vector.reciprocal(row_inv[:, t:t + 1], row_sum[:, t:t + 1]))
                    nc.vector.tensor_scalar(att[:, t, :], att[:, t, :], row_inv[:, t:t + 1], 0.1, ALU.mult, ALU.mult).then_inc(att_ready, 1)
                for t in (1, 3):
                    att_copy(dve, nc.vector.tensor_copy, n, t, KB)
                dve.wait_ge(att_out, T * (n + 1))
                nc.vector.tensor_tensor(cat[:, 0:N], cat[:, 0:N], bank(6), ALU.add).then_inc(l4_fused, 1)
            dve.wait_ge(l4_fused, 2)
            abs_max_dve(4, cat[:])
            l5_sim_dve(dve, link)
            scale_dve(dve, link, 4, FF1, both_now=False)
            ints_dve(link, 4, cat[:], N + B)
            both_dve(4, FF1)
            for c in range(4):
                dve.wait_ge(l4_feat, 8 + c)
                ins = nc.vector.tensor_reduce(chunk_max[:, c:c + 1], hid4[:, c, :], X, ALU.max, apply_absolute_value=True)
            link(ins)
            abs_max_dve(5, chunk_max[:])
            link(nc.vector.tensor_tensor(x[:], x[:], bf24[:].unsqueeze(1).broadcast_to([P, T, D]), ALU.add))
            scale_dve(dve, link, 5, FF2, both_now=False)
            dve.sem_inc(l4_inv, 1)
            for c in range(3):
                ints_dve(link, 5, hid4[:, c, :], N, at_word=c * N)
            both_dve(5, FF2)
            dve.wait_ge(l4_both, 7)
            dve.wait_ge(l4_ps, 14)
            for t in range(T):
                nc.vector.scalar_tensor_tensor(out=x[:, t, :], in0=bank(t)[:, 0:P], scalar=both[:, 5:6], in1=x[:, t, :],
                                               op0=ALU.mult, op1=ALU.add).then_inc(x_updated, 1)

        def l4_pe(pe):
            pe.wait_ge(l4_ints, 4)
            pe.wait_ge(l4_wT, 2)
            l5_norm_pe(pe)
            nc.tensor.matmul(bank(7), ttT[:], ints[:, 0:N], start=True, stop=True).then_inc(l4_ps, 1)
            for l in range(2):
                n = l + 1
                if l == 0:
                    pe.wait_ge(l4_feat, 7)
                else:
                    pe.wait_ge(l4_fused, 1)
                att_scores_pe(pe, n, cat, key4[:, l, :], KB)
                if l == 0:
                    pe.wait_ge(l4_value, 4)
                for t in range(T):
                    att_turn_pe(pe, n, t, KB, att_ready, T * l)
                    if t >= 1:
                        l4_attended_pe(pe, n, l, t - 1)
                l4_attended_pe(pe, n, l, T - 1)
            pe.wait_ge(l4_ints, 5)
            for c in range(4):
                nc.tensor.matmul(bank(c), tf1T[:, 0, c * P:(c + 1) * P], ints[:, 0:N], start=True, stop=False)
                nc.tensor.matmul(bank(c), tf1T[:, 1, c * P:(c + 1) * P], wide(ints[:, N:N + B], N // B),
                                 start=False, stop=True).then_inc(l4_ps, 1)
            for c in range(4):
                if c < 3:
                    pe.wait_ge(l4_ints, 6 + c)
                else:
                    pe.wait_ge(l4_ints_last, 1)
                for t in range(T):
                    ins = nc.tensor.matmul(bank(t)[:, 0:P], ints[:, c * N + t * P:c * N + (t + 1) * P], tf2T[:, c, :],
                                           start=(c == 0), stop=(c == 3))
            ins.then_inc(l4_ps, 1)

        def l4_attended_pe(pe, n, l, t):
            pe.wait_ge(att_copied[t % 2], 2 * n + t // 2 + 1)
            K = KB // P
            for k in range(K):
                ins = nc.tensor.matmul(bank(6)[:, t * P:(t + 1) * P], value4[:, l, K * (t // 2) + k, :], attT[:, t, k, :],
                                       start=(k == 0), stop=(k == K - 1))
            ins.then_inc(att_out, 1)

        def l4_act(act):
            act.wait_ge(l4_ps, 9)
            act.wait_ge(l4_both, 5)
            nc.scalar.activation(cat[:, 0:N], bank(7), ACT.Identity, bias=bt4[:], scale=both[:, 3:4]).then_inc(l4_feat, 1)
            l5_sim_act(act)
            for l in range(2):
                att_exp_act(act, l + 1, KB, S4)
                for t in (0, 2):
                    att_copy(act, act_copy, l + 1, t, KB)
            act.wait_ge(l4_both, 6)
            for c in range(4):
                act.wait_ge(l4_ps, 10 + c)
                nc.scalar.activation(hid4[:, c, :], bank(c), ACT.Relu, bias=bf14[:, c:c + 1], scale=both[:, 4:5]).then_inc(l4_feat, 1)

        E5 = 16
        K5 = N // B
        S5 = float(D) ** -0.5
        proj5 = place_weights(0, [P, E5, 3 * D])
        oproj5 = place_weights(6144, [P, E5, D])
        sim5 = sb("sim5", [P, E5])
        squares5 = sb("squares5", [P, E5])
        norm5 = sb("norm5", [P, E5])
        gates5 = sb("gates5", [P, E5])
        xnorm5 = sb("xnorm5", [P, T])
        idle5 = sb("idle5", [P, T])
        parts5 = sb("parts5", [P, T, 3 * E5], BF16)
        comb5T = sb("comb5T", [P, N], BF16)
        pick5 = sb("pick5", [P, E5, P], BF16)
        scaled = place(4096, [P, 2, N])
        qkv5 = place(5120, [P, T, 3 * D])
        key5T = place(6656, [P, N])
        o5 = place(7168, [P, T, D])
        o5T = place(7680, [P, N])
        junk5 = place(8192, [P, T, D])
        l5_squares = sem("l5_squares")
        l5_norm_ps = sem("l5_norm_ps")
        l5_norm2 = sem("l5_norm2")
        l5_norm = sem("l5_norm")
        l5_gate = sem("l5_gate")
        l5_xsum = sem("l5_xsum")
        l5_xnorm = sem("l5_xnorm")
        l5_sim = sem("l5_sim")
        l5_weight = [sem("l5_weight"), sem("l5_weight_o")]
        l5_scaled = [sem("l5_scaled"), sem("l5_scaled_o")]
        l5_used = [sem("l5_used"), sem("l5_used_o")]
        l5_qkv = sem("l5_qkv")
        l5_qk_turned = sem("l5_qk_turned")
        l5_qk = sem("l5_qk")
        l5_o = sem("l5_o")
        l5_o_turned = sem("l5_o_turned")
        l5_oT = sem("l5_oT")

        def l5_const_pool(pool, link):
            link(nc.gpsimd.memset(pick5[:], 0.0))
            for k in range(3):
                link(nc.gpsimd.affine_select(out=pick5[:], in_=pick5[:], compare_op=ALU.not_equal, fill=1.0, base=-E5 * k,
                                             pattern=[[-1, E5], [0, P]], channel_multiplier=1))
            nc.gpsimd.memset(comb5T[:], 0.0).then_inc(constants, 1)

        def l5_squares_dve(dve):
            dve.wait_ge(late_loaded, 16 * 14)
            nc.vector.tensor_tensor(squares5[:], sim5[:], sim5[:], ALU.mult).then_inc(l5_squares, 1)

        def l5_norm_pe(pe):
            pe.wait_ge(l5_squares, 1)
            nc.tensor.matmul(bank(6)[:, 0:E5], ones[:], squares5[:], start=True, stop=True).then_inc(l5_norm_ps, 1)

        def l5_norm_dve(dve):
            dve.wait_ge(l5_norm_ps, 1)
            nc.vector.tensor_scalar(norm5[:], bank(6)[:, 0:E5], 1e-24, None, ALU.max).then_inc(l5_norm2, 1)

        def l5_sim_dve(dve, link):
            dve.wait_ge(l5_gate, 1)
            link(nc.vector.tensor_scalar(gates5[:], gates5[:], 1.0, None, ALU.add))
            link(nc.vector.reciprocal(gates5[:], gates5[:]))
            dve.wait_ge(l5_norm, 1)
            nc.vector.tensor_tensor(sim5[:], sim5[:], norm5[:], ALU.mult).then_inc(l5_sim, 1)

        def l5_sim_act(act):
            act.wait_ge(late_loaded, 16 * 14)
            nc.scalar.activation(gates5[:], gates5[:], ACT.Exp, scale=-1.0).then_inc(l5_gate, 1)

        def l5_norm_pool(pool):
            pool.wait_ge(l5_norm2, 1)
            nc.gpsimd.tensor_tensor(norm5[:], norm5[:], minus_half[:], ALU.pow).then_inc(l5_norm, 1)

        def l5_xnorm_pool(pool):
            pool.wait_ge(l5_xsum, 1)
            nc.gpsimd.tensor_tensor(xnorm5[:], xnorm5[:], minus_half[:, 0:T], ALU.pow).then_inc(l5_xnorm, 1)

        def l5_router_dve(dve, link):
            dve.wait_ge(ln_rows, 6 * T)
            link(nc.vector.tensor_tensor(junk5[:], xn[:], xn[:], ALU.mult))
            link(nc.vector.tensor_reduce(xnorm5[:], junk5[:], X, ALU.add))
            nc.vector.tensor_scalar(xnorm5[:], xnorm5[:], 1e-24, None, ALU.max).then_inc(l5_xsum, 1)
            dve.wait_ge(router_logits, 3)
            dve.wait_ge(l5_xnorm, 1)
            link(nc.vector.tensor_tensor(logits[:], bank(6)[:, 0:T * E5].rearrange("p (t e) -> p t e", t=T), wide(xnorm5[:], E5), ALU.mult))
            link(nc.vector.tensor_tensor(logits[:], logits[:], gates5[:].unsqueeze(1).broadcast_to([P, T, E5]), ALU.subtract))
            top2_dve(link, logits, E5)
            link(nc.vector.tensor_scalar(logits[:], logits[:], 0.0, None, ALU.max))
            shift_dve(link, logits, E5)
            link(nc.vector.tensor_scalar(equal[:], logits[:], 0.0, None, ALU.is_gt))
            link(nc.vector.tensor_reduce(total2[:], equal[:], X, ALU.add))
            link(nc.vector.tensor_scalar(idle5[:], total2[:], 0.0, None, ALU.is_equal))
            link(nc.vector.tensor_tensor(chosen[:], chosen[:], wide(idle5[:], E5), ALU.mult))
            link(nc.vector.tensor_tensor(chosen[:], chosen[:], equal[:], ALU.add))
            dve.wait_ge(gate_exp, 3)
            weights_dve(link, E5)
            for k in range(3):
                part = parts5[:, :, k * E5:(k + 1) * E5]
                link(nc.vector.tensor_copy(part, comb[:]))
                if k < 2:
                    link(nc.vector.tensor_tensor(comb[:], comb[:], part, ALU.subtract))
            dve.sem_inc(comb_parts, 1)
            dve.wait_ge(comb_parts_ps, 1)
            dve.wait_ge(constants, 3)
            nc.vector.tensor_copy(comb5T[0:3 * E5, :], bank(5).bitcast(BF16)[0:3 * E5, 0:N]).then_inc(comb_rows, 1)

        def l5_router_pe(pe):
            pe.wait_ge(ln_xT, 6)
            pe.wait_ge(l5_sim, 1)
            for t in range(T):
                ins = nc.tensor.matmul(bank(6)[:, t * E5:(t + 1) * E5], xT[:, t * P:(t + 1) * P], sim5[:], start=True, stop=True)
            ins.then_inc(router_logits, 1)
            l6_prepare_pe(pe)
            pe.wait_ge(comb_parts, 1)
            for t in range(T):
                ins = nc.tensor.transpose(bank(5).bitcast(BF16)[0:3 * E5, t * P:(t + 1) * P], parts5[:, t, :], identb[:])
            ins.then_inc(comb_parts_ps, 1)

        def l5_weight_pe(pe, phase, e, static, slot):
            pe.wait_ge(l5_scaled[phase], e + 1)
            nc.tensor.matmul(bank(4 + slot), pick5[:, e, :] if static else pick5[:, bass.ds(e, 1), :], comb5T[:],
                             start=True, stop=True).then_inc(l5_weight[phase], 1)

        def l5_expert_pe(pe, phase, e, static, slot, first, last):
            if not last:
                l5_weight_pe(pe, phase, e + 1, static, 1 - slot)
            pe.wait_ge(l5_scaled[phase], e + 3)
            width, w = ((3 * D, proj5), (D, oproj5))[phase]
            for t in range(T):
                ins = nc.tensor.matmul(bank(t)[:, 0:width], scaled[:, slot, t * P:(t + 1) * P],
                                       w[:, e, :] if static else w[:, bass.ds(e, 1), :], start=first, stop=last)
            ins.then_inc(l5_used[phase], 1)

        def l5_sum_pe(pe, phase):
            l5_weight_pe(pe, phase, 0, True, 0)
            for e in range(2):
                l5_expert_pe(pe, phase, e, True, e, e == 0, False)
            with pe.Fori(1, E5 // 2 - 1) as pair:
                for k in range(2):
                    l5_expert_pe(pe, phase, 2 * pair + k, False, k, False, False)
            for e in range(E5 - 2, E5):
                l5_expert_pe(pe, phase, e, True, e % 2, False, e == E5 - 1)

        def l5_sum_dve(dve, phase, source):
            dve.sem_inc(l5_scaled[phase], 2)
            with dve.Fori(0, E5 // 2) as pair:
                for k in range(2):
                    dve.wait_ge(l5_weight[phase], 2 * pair + (k + 1))
                    dve.wait_ge(l5_used[phase], 2 * pair + (k + 1))
                    nc.vector.tensor_tensor(scaled[:, k, :], source[:], bank(4 + k), ALU.mult).then_inc(l5_scaled[phase], 1)

        def l5_pe(pe):
            pe.wait_ge(comb_rows, 1)
            pe.wait_ge(l6_v_raw, 2)
            pe.sem_inc(l5_used[0], 2)
            l5_sum_pe(pe, 0)
            pe.wait_ge(l5_qkv, 4)
            for k in range(2):
                for t in range(T):
                    ins = nc.tensor.transpose(bank(4 + k)[:, t * P:(t + 1) * P], qkv5[:, t, k * D:(k + 1) * D], ident[:])
                ins.then_inc(l5_qk_turned, 1)
            pe.wait_ge(l5_qk, 2)
            att_scores_pe(pe, 3, queryT, key5T, K5)
            for t in range(T):
                att_turn_pe(pe, 3, t, K5, att_exp, 3 * T)
                if t >= 1:
                    att_out_pe(pe, 3, t - 1, K5, qkv5[:, :, 2 * D:3 * D])
            att_out_pe(pe, 3, T - 1, K5, qkv5[:, :, 2 * D:3 * D])
            pe.wait_ge(l5_o, T)
            for t in range(T):
                ins = nc.tensor.transpose(bank(7)[:, t * P:(t + 1) * P], o5[:, t, :], ident[:])
            ins.then_inc(l5_o_turned, 1)
            pe.wait_ge(l5_oT, 1)
            pe.sem_inc(l5_used[1], 2)
            l5_sum_pe(pe, 1)

        def l5_act(act):
            act.wait_ge(l5_used[0], E5 + 2)
            for t in (1, 3):
                act_copy(qkv5[:, t, :], bank(t)[:, 0:3 * D]).then_inc(l5_qkv, 1)
            act.wait_ge(l5_qk_turned, 2)
            act_copy(key5T[:], bank(5)).then_inc(l5_qk, 1)
            att_exp_act(act, 3, K5, S5)
            for t in (0, 2):
                att_copy(act, act_copy, 3, t, K5)
            act.wait_ge(l5_o_turned, 1)
            act_copy(o5T[:], bank(7)).then_inc(l5_oT, 1)

        def l5_dve(dve, link):
            l5_sum_dve(dve, 0, xT)
            dve.wait_ge(l5_used[0], E5 + 2)
            for t in (0, 2):
                nc.vector.tensor_copy(qkv5[:, t, :], bank(t)[:, 0:3 * D]).then_inc(l5_qkv, 1)
            dve.wait_ge(l5_qk_turned, 1)
            nc.vector.tensor_copy(queryT[:], bank(4)).then_inc(l5_qk, 1)
            for t in range(T):
                att_max_dve(dve, link, 3, t, K5, S5)
            for t in (1, 3):
                att_copy(dve, nc.vector.tensor_copy, 3, t, K5)
            dve.wait_ge(att_exp, 4 * T)
            link(nc.vector.reciprocal(row_inv[:], row_sum[:]))
            for t in range(T):
                dve.wait_ge(att_out, 4 * T)
                nc.vector.tensor_scalar(o5[:, t, :], quarters(6)[:, t, :], row_inv[:, t:t + 1], None, ALU.mult).then_inc(l5_o, 1)
            dve.wait_ge(l5_oT, 1)
            l5_sum_dve(dve, 1, o5T)
            dve.wait_ge(l5_used[1], E5 + 2)
            for t in range(T):
                nc.vector.tensor_tensor(x[:, t, :], x[:, t, :], bank(t)[:, 0:D], ALU.add).then_inc(x_updated, 1)

        H6 = 16
        J6 = D // H6
        KT6 = MT // B
        R6 = 9 * J6
        TOP6 = 96
        S6 = float(J6) ** -0.5
        wq6 = sb("wq6", [P, D])
        wkv6 = sb("wkv6", [P, 2, C])
        wo6 = sb("wo6", [P, D])
        bq6 = sb("bq6", [P, 1])
        bk6 = sb("bk6", [P, 1])
        bkv6 = sb("bkv6", [P, 2 * D])
        bo6 = sb("bo6", [P, D])
        wq6T = sb("wq6T", [P, D])
        wk6T = sb("wk6T", [C, D])
        wv6T = sb("wv6T", [C, D])
        wo6T = sb("wo6T", [P, D])
        value6 = sb("value6", [P, MT, H6, J6])
        value_head = sb("value_head", [P, MT, 2 * J6])
        max6 = sb("max6", [P, T])
        rest6 = sb("rest6", [P, T])
        max_parts = weight_room[:, 6400:6656].bitcast(BF16).rearrange("p (t c) -> p t c", t=T)
        key6 = place(9216, [P, M])
        k6_parts = room[:, 10240:11776].bitcast(BF16).rearrange("p (a n) -> p a n", a=3)
        key6_stack = room2[0:TOP6 + 3, :].bitcast(BF16).rearrange("p (h n) -> p h n", h=H6)
        query6_stack = room[0:TOP6 + 3, 8192:12288].bitcast(BF16).rearrange("p (h n) -> p h n", h=H6)
        o6_rows = room[0:2 * J6, 0:8192].rearrange("p (h n) -> p h n", h=H6)
        probs6 = place_weights(3072, [P, 2, M])
        query6 = place_weights(5120, [P, N])
        q6_parts = weight_room[:, 5632:6400].bitcast(BF16).rearrange("p (a n) -> p a n", a=3)
        o6_stack = room2[:, 0:512]
        sum6_stack = room2[:, 512:1024]
        inv6 = room2[:, 1024:1536]
        o6T = room2[:, 1536:2048]
        l6_wo_order = sem("l6_wo_order")
        l6_w_turned = sem("l6_w_turned")
        l6_w = sem("l6_w")
        l6_k_ps = sem("l6_k_ps")
        l6_key = sem("l6_key")
        l6_k_parts = sem("l6_k_parts")
        l6_k_stack = sem("l6_k_stack")
        l6_v_ps = sem("l6_v_ps")
        l6_v_raw = sem("l6_v_raw")
        l6_value = sem("l6_value")
        l6_q_ps = sem("l6_q_ps")
        l6_q_parts = sem("l6_q_parts")
        l6_q_stack = sem("l6_q_stack")
        l6_row_scores = sem("l6_row_scores")
        l6_max = sem("l6_max")
        l6_max_parts = sem("l6_max_parts")
        l6_max_turned = sem("l6_max_turned")
        l6_max_rows = sem("l6_max_rows")
        l6_zero = sem("l6_zero")
        l6_scores = sem("l6_scores")
        l6_probs = sem("l6_probs")
        l6_value_head = sem("l6_value_head")
        l6_o_ps = sem("l6_o_ps")
        l6_o_rows = sem("l6_o_rows")
        l6_o_stack = sem("l6_o_stack")
        l6_oT = sem("l6_oT")
        l6_y = sem("l6_y")

        def l6_prepare_pe(pe):
            pe.wait_ge(late_loaded, 16 * 14)
            nc.tensor.transpose(bank(0)[:, 0:P], wq6[:], ident[:])
            pe.wait_ge(l6_wo_order, 1)
            nc.tensor.transpose(bank(0)[:, P:2 * P], wo6T[:], ident[:])
            for k in range(2):
                ins = nc.tensor.transpose(bank(0)[0:C, (2 + k) * P:(3 + k) * P], wkv6[:, k, :], ident[:])
            ins.then_inc(l6_w_turned, 1)
            pe.wait_ge(l6_w, 4)
            for half in range(2):
                ins = nc.tensor.matmul(bank(1 + half), wk6T[:], ctxT[:, half * 512:(half + 1) * 512], start=True, stop=True)
            ins.then_inc(l6_k_ps, 1)
            for half in range(2):
                for q in range(4):
                    k = 4 * half + q
                    ins = nc.tensor.matmul(bank(3 + half)[:, q * P:(q + 1) * P], ctxT[:, k * P:(k + 1) * P], wv6T[:], start=True, stop=True)
            ins.then_inc(l6_v_ps, 1)

        def l6_prepare_act(act):
            act.wait_ge(l6_w_turned, 1)
            b0 = bank(0)
            act_copy(wq6T[:].rearrange("p (j h) -> p j h", j=J6), b0[:, 0:P].rearrange("p (h j) -> p j h", j=J6)).then_inc(l6_w, 1)
            act_copy(wo6T[:], b0[:, P:2 * P]).then_inc(l6_w, 1)
            kv = b0[0:C, 2 * P:4 * P].rearrange("p (h s j) -> p s j h", s=2, j=J6)
            act_copy(wk6T[:].rearrange("p (j h) -> p j h", j=J6), kv[:, 0]).then_inc(l6_w, 1)
            act_copy(wv6T[:].rearrange("p (h j) -> p j h", j=J6), kv[:, 1]).then_inc(l6_w, 1)
            act.wait_ge(l6_k_ps, 1)
            act.wait_ge(late_loaded, 16 * 14)
            nc.scalar.activation(key6.rearrange("p (b n) -> p b n", b=2), PS[:, 1:3, :], ACT.Identity, bias=bk6[:]).then_inc(l6_key, 1)
            act.wait_ge(l6_v_ps, 1)
            for half in range(2):
                act_copy(value6[:, 4 * half:4 * half + 4, :, :],
                         bank(3 + half).rearrange("p (k h j) -> p k h j", k=4, j=J6)).then_inc(l6_v_raw, 1)

        def split_parts(engine_inc, engine, link, parts, whole, done):
            for a in range(3):
                ins = engine.tensor_copy(parts[:, a, :], whole)
                if a < 2:
                    link(ins)
                    engine_inc.sem_inc(done, 1)
                    link(engine.tensor_tensor(whole, whole, parts[:, a, :], ALU.subtract))
            ins.then_inc(done, 1)

        def l6_prepare_pool(pool, link):
            pool.wait_ge(late_loaded, 16 * 14)
            nc.gpsimd.tensor_copy(wo6T[:].rearrange("p (j h) -> p j h", j=J6),
                                  wo6[:].rearrange("p (h j) -> p j h", j=J6)).then_inc(l6_wo_order, 1)
            pool.wait_ge(l6_key, 1)
            split_parts(pool, nc.gpsimd, link, k6_parts, key6, l6_k_parts)
            pool.wait_ge(l6_v_raw, 2)
            bv = bkv6[:].rearrange("p (h s j) -> p s h j", s=2, j=J6)[:, 1]
            for k in range(MT):
                nc.gpsimd.tensor_tensor(value6[:, k, :, :], value6[:, k, :, :], bv, ALU.add).then_inc(l6_value, 1)
            nc.gpsimd.memset(value_head[:, :, J6:2 * J6], 1.0).then_inc(l6_value, 1)

        def l6_k_stack_sp(sp):
            sp.wait_ge(x_updated, 5 * T)
            sp.wait_ge(constants, 4)
            sp.dma_start(key6_stack[TOP6:TOP6 + 3, :, :], onesb[0:3, :].unsqueeze(1).broadcast_to([3, P, P])).then_inc(l6_k_stack, 16)
            zeros = comb5T[3 * E5:3 * E5 + TOP6 - R6, :].unsqueeze(1)
            sp.dma_start(key6_stack[R6:TOP6, :, :], zeros.broadcast_to([TOP6 - R6, H6 * M // N, N])).then_inc(l6_k_stack, 16)
            sp.wait_ge(l6_k_parts, 3)
            for a in range(3):
                for b in range(3):
                    r = (3 * a + b) * J6
                    sp.dma_start(key6_stack[r:r + J6, :, :], k6_parts[:, b, :]).then_inc(l6_k_stack, 16)

        def l6_q_stack_dma(eng, a):
            for b in range(3):
                r = (3 * a + b) * J6
                eng.dma_start(query6_stack[r:r + J6, :, :], q6_parts[:, a, :]).then_inc(l6_q_stack, 16)

        def l6_sp(sp):
            sp.wait_ge(l6_k_stack, 16 * 11)
            zeros = comb5T[3 * E5:3 * E5 + TOP6 - R6, :].unsqueeze(1)
            sp.dma_start(query6_stack[R6:TOP6, :, :], zeros.broadcast_to([TOP6 - R6, H6, N])).then_inc(l6_q_stack, 16)
            for a in range(3):
                sp.wait_ge(l6_q_parts, a + 1)
                l6_q_stack_dma(sp, a)

        def l6_o_sp(sp):
            sp.wait_ge(l6_o_rows, H6 + 1)
            sp.dma_start(o6_stack, o6_rows[0:J6, :, :]).then_inc(l6_o_stack, 16)
            sp.dma_start(sum6_stack, o6_rows[J6:2 * J6, :, :]).then_inc(l6_o_stack, 16)

        def l6_row_scores_pe(pe, g, b, free=True, low=0):
            if free:
                pe.wait_ge(l6_max, 2 * g + b)
            for t in range(2):
                q = (2 * b + t) * P
                ins = nc.tensor.matmul(bank(low + t), query6_stack[0:R6, at(g), q:q + P], key6_stack[0:R6, at(g), b * KB:(b + 1) * KB],
                                       start=True, stop=True)
            ins.then_inc(l6_row_scores, 1)

        def l6_turn_pe(pe, g):
            pe.wait_ge(l6_max_parts, g + 1)
            for t in range(T):
                ins = nc.tensor.transpose(bank(2).bitcast(BF16)[:, t * P:(t + 1) * P], max_parts[:, t, :], identb[:])
            ins.then_inc(l6_max_turned, 1)

        def l6_st_pe(pe, g, b):
            if b == 0:
                pe.wait_ge(l6_max_rows, g + 1)
            for k in range(4):
                ins = nc.tensor.matmul(bank(3 + 2 * b + k // 2)[:, (k % 2) * K5:(k % 2 + 1) * K5],
                                       key6_stack[:, at(g), b * KB + k * P:b * KB + (k + 1) * P],
                                       query6_stack[:, at(g), b * K5:(b + 1) * K5], start=True, stop=True)
            ins.then_inc(l6_scores, 1)

        def l6_pv_pe(pe, g, b):
            if b == 0:
                pe.wait_ge(l6_o_rows, g + 1)
            pe.wait_ge(l6_value_head, 2 * g + (b + 1))
            pe.wait_ge(l6_probs, 2 * g + (b + 1))
            for k in range(4):
                ins = nc.tensor.matmul(bank(7)[0:2 * J6, b * K5:(b + 1) * K5], value_head[:, 4 * b + k, :],
                                       probs6[:, b, k * K5:(k + 1) * K5], start=(k == 0), stop=(k == 3))
            ins.then_inc(l6_o_ps, 1)

        def l6_head_pe(pe, g, first=False, turn=True, rows=True):
            l6_st_pe(pe, g, 0)
            if not first:
                l6_pv_pe(pe, g - 1, 1)
            if turn:
                l6_turn_pe(pe, g + 1)
            l6_st_pe(pe, g, 1)
            if rows:
                l6_row_scores_pe(pe, g + 2, 0)
            l6_pv_pe(pe, g, 0)
            if rows:
                l6_row_scores_pe(pe, g + 2, 1)

        def l6_pe(pe):
            pe.wait_ge(ln_xT, 7)
            nc.tensor.matmul(bank(5), wq6T[:], xT[:], start=True, stop=True).then_inc(l6_q_ps, 1)
            pe.wait_ge(l6_value, MT + 1)
            pe.wait_ge(l6_k_stack, 16 * 11)
            pe.wait_ge(l6_q_stack, 16 * 10)
            l6_row_scores_pe(pe, 0, 0, free=False)
            l6_row_scores_pe(pe, 0, 1, free=False, low=3)
            l6_row_scores_pe(pe, 1, 0)
            l6_turn_pe(pe, 0)
            l6_row_scores_pe(pe, 1, 1)
            l6_head_pe(pe, 0, first=True)
            with pe.Fori(1, H6 - 2) as g:
                l6_head_pe(pe, g)
            l6_head_pe(pe, H6 - 2, rows=False)
            l6_head_pe(pe, H6 - 1, turn=False, rows=False)
            l6_pv_pe(pe, H6 - 1, 1)
            for t in range(T):
                pe.wait_ge(l6_oT, t + 1)
                ins = nc.tensor.matmul(bank(5)[:, t * P:(t + 1) * P], o6T[:, t * P:(t + 1) * P], wo6T[:], start=True, stop=True)
            ins.then_inc(l6_y, 1)

        def l6_max_dve(dve, link, g, banks=(0, 0)):
            for b in range(2):
                dve.wait_ge(l6_row_scores, 2 * g + (b + 1))
                nc.vector.tensor_reduce(max6[:, 2 * b:2 * b + 2], PS[:, banks[b]:banks[b] + 2, :], X, ALU.max).then_inc(l6_max, 1)
            dve.wait_ge(l6_max, 2 * g + 2)
            link(nc.vector.tensor_scalar(max_parts[:, :, TOP6], max6[:], -1.0, None, ALU.mult))
            link(nc.vector.scalar_tensor_tensor(out=rest6[:], in0=max6[:], scalar=-1.0, in1=max_parts[:, :, TOP6],
                                                op0=ALU.mult, op1=ALU.subtract))
            link(nc.vector.tensor_copy(max_parts[:, :, TOP6 + 1], rest6[:]))
            link(nc.vector.tensor_tensor(rest6[:], rest6[:], max_parts[:, :, TOP6 + 1], ALU.subtract))
            nc.vector.tensor_copy(max_parts[:, :, TOP6 + 2], rest6[:]).then_inc(l6_max_parts, 1)

        def l6_rows_dve(dve, g):
            dve.wait_ge(l6_max_turned, g + 1)
            nc.vector.tensor_copy(query6_stack[TOP6:TOP6 + 3, at(g), :].rearrange("p a n -> p (a n)"),
                                  bank(2).bitcast(BF16)[TOP6:TOP6 + 3, 0:N]).then_inc(l6_max_rows, 1)

        def l6_dve(dve, link):
            dve.wait_ge(l6_q_ps, 1)
            dve.wait_ge(late_loaded, 16 * 14)
            link(nc.vector.tensor_scalar(q6_parts[:, 0, :], bank(5), bq6[:], None, ALU.add))
            dve.sem_inc(l6_q_parts, 1)
            link(nc.vector.scalar_tensor_tensor(out=query6, in0=bank(5), scalar=bq6[:], in1=q6_parts[:, 0, :],
                                                op0=ALU.add, op1=ALU.subtract))
            link(nc.vector.tensor_copy(q6_parts[:, 1, :], query6))
            dve.sem_inc(l6_q_parts, 1)
            nc.vector.tensor_tensor(q6_parts[:, 2, :], query6, q6_parts[:, 1, :], ALU.subtract).then_inc(l6_q_parts, 1)
            link(nc.vector.tensor_tensor(x[:], x[:], bo6[:].unsqueeze(1).broadcast_to([P, T, D]), ALU.add))
            dve.wait_ge(l6_zero, 1)
            l6_max_dve(dve, link, 0, banks=(0, 3))
            l6_rows_dve(dve, 0)
            l6_max_dve(dve, link, 1)
            l6_rows_dve(dve, 1)
            l6_max_dve(dve, link, 2)
            with dve.Fori(0, H6 - 3) as g:
                link.enter(g, 4)
                l6_rows_dve(dve, g + 2)
                l6_max_dve(dve, link, g + 3)
            link.leave(H6 - 3)
            l6_rows_dve(dve, H6 - 1)
            dve.wait_ge(l6_o_stack, 32)
            for t in range(T):
                cols = slice(t * P, (t + 1) * P)
                link(nc.vector.reciprocal(inv6[:, cols], sum6_stack[:, cols]))
                nc.vector.tensor_tensor(o6T[:, cols], o6_stack[:, cols], inv6[:, cols], ALU.mult).then_inc(l6_oT, 1)
            dve.wait_ge(l6_y, 1)
            for t in range(T):
                nc.vector.tensor_tensor(x[:, t, :], x[:, t, :], quarters(5)[:, t, :], ALU.add).then_inc(x_updated, 1)

        def l6_exp_act(act, g, b):
            act.wait_ge(l6_scores, 2 * g + (b + 1))
            nc.scalar.activation(probs6[:, b, :].rearrange("p (c n) -> p c n", c=2), PS[:, 3 + 2 * b:5 + 2 * b, :], ACT.Exp,
                                 scale=S6).then_inc(l6_probs, 1)

        def l6_o_act(act, g):
            act.wait_ge(l6_o_ps, 2 * g + 2)
            act_copy(o6_rows[:, at(g), :], bank(7)[0:2 * J6, :]).then_inc(l6_o_rows, 1)

        def l6_act(act):
            act.sem_inc(l6_o_rows, 1)
            for b in range(2):
                l6_exp_act(act, 0, b)
            with act.Fori(1, H6) as g:
                l6_exp_act(act, g, 0)
                l6_o_act(act, g - 1)
                l6_exp_act(act, g, 1)
            l6_o_act(act, H6 - 1)

        def l6_pool(pool):
            pool.wait_ge(x_updated, 6 * T)
            nc.gpsimd.memset(max_parts, 0.0).then_inc(l6_zero, 1)
            pool.wait_ge(l6_value, MT + 1)
            for b in range(2):
                half = slice(b * KT6, (b + 1) * KT6)
                nc.gpsimd.tensor_copy(value_head[:, half, 0:J6], value6[:, half, 0, :]).then_inc(l6_value_head, 1)
            with pool.Fori(1, H6) as g:
                for b in range(2):
                    half = slice(b * KT6, (b + 1) * KT6)
                    pool.wait_ge(l6_o_ps, 2 * g - (1 - b))
                    nc.gpsimd.tensor_copy(value_head[:, half, 0:J6], value6[:, half, bass.ds(g, 1), :].rearrange("p k a j -> p k (a j)")).then_inc(l6_value_head, 1)

        E7 = 8
        F7 = 512
        CAP7 = 160
        NS7 = CAP7 - P
        wr7 = sb("wr7", [P, E7])
        w17 = [place_weights(1536 * s, [P, F7]) for s in range(2)]
        w37 = [place_weights(1536 * s + 512, [P, F7]) for s in range(2)]
        w27 = [place_weights(1536 * s + 1024, [P, 4, D]) for s in range(2)]
        chosen7 = sb("chosen7", [P, T, E7], BF16)
        earlier7 = sb("earlier7", [P, P], BF16)
        onesb = sb("onesb", [P, P], BF16)
        place7 = sb("place7", [P, T, E7])
        places7b = sb("places7b", [P, T, E7], BF16)
        slot7 = sb("slot7", [P, 2])
        gather7 = place(0, [P, T, CAP7])
        x7T = place(640, [P, CAP7])
        silu7 = place(800, [P, 2, 2 * CAP7])
        hidden7T = place(1440, [P, 4, CAP7])
        spread7 = place(2080, [P, 2, N])
        rest7 = place(6144, [2 * NS7, E7 // 2, N])
        y7 = place(4128, [P, D])
        y7_rest = place(4256, [2 * NS7, D])
        out7T = place(4384, [P, N])
        place7T = place(4896, [P, N // 2]).bitcast(BF16)
        places7 = place(5152, [P, CAP7])
        token_place7 = place(5376, [P, N])
        l7_loaded = [sem("l7_loaded_even"), sem("l7_loaded_odd")]
        l7_zero = sem("l7_zero")
        l7_chosen = sem("l7_chosen")
        l7_before = sem("l7_before")
        l7_gather = sem("l7_gather")
        l7_x_ps = sem("l7_x_ps")
        l7_x = sem("l7_x")
        l7_broad = sem("l7_broad")
        l7_token_place = sem("l7_token_place")
        l7_spread = sem("l7_spread")
        l7_h = sem("l7_h")
        l7_silu = sem("l7_silu")
        l7_hidden = sem("l7_hidden")
        l7_y_ps = sem("l7_y_ps")
        l7_y = sem("l7_y")
        l7_out = sem("l7_out")
        l7_outT = sem("l7_outT")
        l7_turned = sem("l7_turned")

        def l7_const_pool(pool, link):
            link(nc.gpsimd.memset(earlier7[:], 1.0))
            link(nc.gpsimd.affine_select(out=earlier7[:], in_=earlier7[:], compare_op=ALU.is_gt, fill=0.0, base=0,
                                         pattern=[[1, P]], channel_multiplier=-1))
            nc.gpsimd.memset(onesb[:], 1.0).then_inc(constants, 1)

        def l7_load(sp, w1, w3, w2, slot):
            sp.dma_start(w17[slot], w1).then_inc(l7_loaded[slot], 16)
            sp.dma_start(w37[slot], w3).then_inc(l7_loaded[slot], 16)
            sp.dma_start(w27[slot], w2).then_inc(l7_loaded[slot], 16)

        def l7_first_loads_sp(sp):
            sp.wait_ge(x_updated, 6 * T)
            for e in range(2):
                l7_load(sp, i["L3_ffn_W1"][e], i["L3_ffn_W3"][e], i["L3_ffn_W2"][e].rearrange("(c p) d -> p c d", p=P), e)

        def l7_loads_sp(sp):
            W1, W3 = i["L3_ffn_W1"], i["L3_ffn_W3"]
            W2 = i["L3_ffn_W2"].rearrange("e (c p) d -> e p c d", p=P)
            with sp.Fori(0, E7 // 2 - 1) as pair:
                for k in range(2):
                    sp.wait_ge(l7_y_ps, 2 * pair + (k + 1))
                    e = 2 * pair + (k + 2)
                    l7_load(sp, W1[bass.ds(e, 1)].rearrange("a d f -> d (a f)"), W3[bass.ds(e, 1)].rearrange("a d f -> d (a f)"),
                            W2[bass.ds(e, 1)].rearrange("a p c d -> p (a c) d"), k)

        def l7_numbers_pe(pe):
            pe.wait_ge(constants, 4)
            nc.tensor.matmul(bank(4)[:, 0:P], onesb[:], earlier7[:], start=True, stop=True)
            nc.tensor.matmul(bank(4)[:, P:P + 1], earlier7[:], onesb[:, 0:1], start=True, stop=True).then_inc(constants, 1)

        def l7_numbers_dve(dve, link):
            dve.wait_ge(constants, 5)
            nc.vector.tensor_scalar(places7[:, 0:P], bank(4)[:, 0:P], 1.0, None, ALU.add)
            nc.vector.tensor_scalar(places7[:, P:CAP7], bank(4)[:, 0:NS7], float(P + 1), None, ALU.add)
            nc.vector.tensor_scalar(slot7[:, 0:1], bank(4)[:, P:P + 1], 1.0, None, ALU.add)
            for k in range(2):
                rows = slice(k * NS7, (k + 1) * NS7)
                ins = nc.vector.tensor_scalar(slot7[rows, 1:2], bank(4)[rows, P:P + 1], float(P + 1 - k * NS7), None, ALU.add)
            link(ins)

        def l7_router_pe(pe):
            pe.wait_ge(ln_xT, 8)
            pe.wait_ge(late_loaded, 16 * 14)
            for t in range(T):
                ins = nc.tensor.matmul(bank(6)[:, t * E7:(t + 1) * E7], xT[:, t * P:(t + 1) * P], wr7[:], start=True, stop=True)
            ins.then_inc(router_logits, 1)
            pe.wait_ge(l7_chosen, 1)
            for t in range(T):
                cols = bank(7)[:, t * E7:(t + 1) * E7]
                for u in range(t):
                    nc.tensor.matmul(cols, onesb[:], chosen7[:, u, :], start=(u == 0), stop=False)
                ins = nc.tensor.matmul(cols, earlier7[:], chosen7[:, t, :], start=(t == 0), stop=True)
            ins.then_inc(l7_before, 1)

        def l7_rows_pe(pe):
            pe.wait_ge(comb_parts, 2)
            b5 = bank(5).bitcast(BF16)
            for t in range(T):
                nc.tensor.transpose(b5[0:3 * E5, t * P:(t + 1) * P], parts5[:, t, :], identb[:])
                ins = nc.tensor.transpose(b5[0:E7, N + t * P:N + (t + 1) * P], places7b[:, t, :], identb[:])
            ins.then_inc(comb_parts_ps, 1)

        def l7_router_dve(dve, link):
            dve.wait_ge(router_logits, 4)
            link(nc.vector.tensor_scalar(logits[:, :, 0:E7], bank(6)[:, 0:T * E7].rearrange("p (t e) -> p t e", t=T),
                                         1e4, -1e4, ALU.min, ALU.max))
            shift_dve(link, logits, E7)
            top2_dve(link, logits, E7)
            nc.vector.tensor_copy(chosen7[:], chosen[:, :, 0:E7]).then_inc(l7_chosen, 1)
            dve.wait_ge(l7_before, 1)
            before = bank(7)[:, 0:T * E7].rearrange("p (t e) -> p t e", t=T)
            link(nc.vector.scalar_tensor_tensor(out=place7[:], in0=before, scalar=1.0, in1=chosen[:, :, 0:E7],
                                                op0=ALU.add, op1=ALU.mult))
            l7_gather_dve(dve, 0, first=True)
            dve.wait_ge(gate_exp, 4)
            weights_dve(link, E7, eps=1e-12)
            for k in range(3):
                part = parts5[:, :, k * E5:k * E5 + E7]
                link(nc.vector.tensor_copy(part, comb[:, :, 0:E7]))
                if k < 2:
                    link(nc.vector.tensor_tensor(comb[:, :, 0:E7], comb[:, :, 0:E7], part, ALU.subtract))
            nc.vector.tensor_copy(places7b[:], place7[:]).then_inc(comb_parts, 1)
            dve.wait_ge(comb_parts_ps, 2)
            dve.wait_ge(l7_zero, 1)
            b5 = bank(5).bitcast(BF16)
            nc.vector.tensor_copy(comb5T[0:3 * E5, :], b5[0:3 * E5, 0:N]).then_inc(comb_rows, 1)
            nc.vector.tensor_copy(place7T[0:E7, :], b5[0:E7, N:2 * N]).then_inc(comb_rows, 1)

        def l7_broad_pe(pe, e):
            nc.tensor.matmul(bank(5), pick5[:, at(e), :], place7T, start=True, stop=True)
            nc.tensor.matmul(bank(6), pick5[:, at(e), :], comb5T[:], start=True, stop=True).then_inc(l7_broad, 1)

        def l7_x_pe(pe, e):
            pe.wait_ge(l7_gather, e + 1)
            for t in range(T):
                ins = nc.tensor.matmul(bank(0)[:, 2 * CAP7:3 * CAP7], xn[:, t, :], gather7[:, t, :], start=(t == 0), stop=(t == T - 1))
            ins.then_inc(l7_x_ps, 1)

        def l7_spread_pe(pe, e, slot, pair, first=False, last=False):
            pe.wait_ge(l7_y, 2 * e + 2)
            pe.wait_ge(l7_spread, e + 1)
            ins = nc.tensor.matmul(bank(7), y7, spread7[:, slot, :], start=first, stop=False)
            if slot == 1:
                ins = nc.tensor.matmul(bank(7), y7_rest, rest7[:, at(pair), :], start=False, stop=last)
            if last:
                ins.then_inc(l7_out, 1)

        def l7_chunks_pe(pe, e, slot, loads):
            pe.wait_ge(l7_x, e + 1)
            pe.wait_ge(l7_loaded[slot], 48 * loads)
            for p in range(2):
                for half, w in enumerate((w17, w37)):
                    for c in range(2):
                        chunk = (2 * p + c) * P
                        ins = nc.tensor.matmul(bank(2 * p + half)[:, c * CAP7:(c + 1) * CAP7], w[slot][:, chunk:chunk + P], x7T,
                                               start=True, stop=True)
                ins.then_inc(l7_h, 1)

        def l7_next_pe(pe, e):
            pe.wait_ge(l7_silu, 2 * e - 1)
            l7_x_pe(pe, e)

        def l7_y_pe(pe, e, slot):
            pe.wait_ge(l7_hidden, 2 * e + 2)
            for s, n in enumerate((P, NS7)):
                for c in range(4):
                    ins = nc.tensor.matmul(bank(4)[0:n, s * D:(s + 1) * D], hidden7T[:, c, s * P:s * P + n], w27[slot][:, c, :],
                                           start=(c == 0), stop=(c == 3))
            ins.then_inc(l7_y_ps, 1)

        def l7_expert_pe(pe, e, slot, pair, last=False):
            l7_chunks_pe(pe, e, slot, pair + 1)
            l7_spread_pe(pe, e - 1, 1 - slot, pair - 1 + slot)
            if not last:
                pe.wait_ge(l7_spread, e + 1)
                l7_broad_pe(pe, e + 1)
                l7_next_pe(pe, e + 1)
            l7_y_pe(pe, e, slot)

        def l7_pe(pe):
            l7_x_pe(pe, 0)
            l7_rows_pe(pe)
            l7_chunks_pe(pe, 0, 0, 1)
            pe.wait_ge(comb_rows, 3)
            l7_broad_pe(pe, 0)
            l7_next_pe(pe, 1)
            l7_y_pe(pe, 0, 0)
            l7_chunks_pe(pe, 1, 1, 1)
            l7_spread_pe(pe, 0, 0, 0, first=True)
            l7_broad_pe(pe, 1)
            l7_next_pe(pe, 2)
            l7_y_pe(pe, 1, 1)
            pe.wait_ge(l7_spread, 2)
            l7_broad_pe(pe, 2)
            with pe.Fori(1, E7 // 2 - 1) as pair:
                for k in range(2):
                    l7_expert_pe(pe, 2 * pair + k, k, pair)
            l7_expert_pe(pe, E7 - 2, 0, E7 // 2 - 1)
            l7_expert_pe(pe, E7 - 1, 1, E7 // 2 - 1, last=True)
            l7_spread_pe(pe, E7 - 1, 1, E7 // 2 - 1, last=True)
            pe.wait_ge(l7_outT, 1)
            for t in range(T):
                ins = nc.tensor.transpose(bank(4)[:, t * P:(t + 1) * P], out7T[:, t * P:(t + 1) * P], ident[:])
            ins.then_inc(l7_turned, 1)

        def l7_pool(pool):
            pool.wait_ge(x_updated, 7 * T)
            nc.gpsimd.memset(place7T, 0.0).then_inc(l7_zero, 1)

        def l7_x_act(act, e):
            act.wait_ge(l7_x_ps, e + 1)
            act_copy(x7T, bank(0)[:, 2 * CAP7:3 * CAP7]).then_inc(l7_x, 1)

        def l7_place_act(act, e):
            act.wait_ge(l7_broad, e + 1)
            act_copy(token_place7, bank(5)).then_inc(l7_token_place, 1)

        def l7_expert_act(act, e, slot, places=(1,), last=False):
            for p in range(2):
                act.wait_ge(l7_h, 2 * e + (p + 1))
                nc.scalar.activation(silu7[:, p, :], bank(2 * p)[:, 0:2 * CAP7], ACT.Silu).then_inc(l7_silu, 1)
            if not last:
                l7_place_act(act, e + places[0])
                l7_x_act(act, e + 1)
            act.wait_ge(l7_y_ps, e + 1)
            act_copy(y7, bank(4)[:, 0:D]).then_inc(l7_y, 1)
            act_copy(y7_rest[slot * NS7:(slot + 1) * NS7, :], bank(4)[0:NS7, D:2 * D]).then_inc(l7_y, 1)
            for later in places[1:]:
                l7_place_act(act, e + later)

        def l7_act(act):
            l7_x_act(act, 0)
            l7_expert_act(act, 0, 0, places=(0,))
            l7_expert_act(act, 1, 1, places=(0, 1))
            with act.Fori(1, E7 // 2 - 1) as pair:
                for k in range(2):
                    l7_expert_act(act, 2 * pair + k, k)
            l7_expert_act(act, E7 - 2, 0)
            l7_expert_act(act, E7 - 1, 1, last=True)

        def l7_gather_dve(dve, e, first=False):
            if not first:
                dve.wait_ge(l7_x_ps, e)
            nc.vector.tensor_tensor(gather7, places7.unsqueeze(1).broadcast_to([P, T, CAP7]), place7[:, :, at(e)].broadcast_to([P, T, CAP7]),
                                    ALU.is_equal).then_inc(l7_gather, 1)

        def l7_spread_dve(dve, e, slot, pair):
            dve.wait_ge(l7_token_place, e + 1)
            rows = slice(slot * NS7, (slot + 1) * NS7)
            for out, part, c in ((spread7[:, slot, :], slice(0, P), 0), (rest7[rows, at(pair), :].rearrange("p a n -> p (a n)"), rows, 1)):
                ins = nc.vector.scalar_tensor_tensor(out=out, in0=token_place7[part, :], scalar=slot7[part, c:c + 1],
                                                     in1=bank(6)[part, :], op0=ALU.is_equal, op1=ALU.mult)
            ins.then_inc(l7_spread, 1)

        def l7_hidden_dve(dve, e):
            for p in range(2):
                dve.wait_ge(l7_silu, 2 * e + (p + 1))
                nc.vector.tensor_tensor(hidden7T[:, 2 * p:2 * p + 2, :], silu7[:, p, :].rearrange("p (c n) -> p c n", c=2),
                                        bank(2 * p + 1)[:, 0:2 * CAP7].rearrange("p (c n) -> p c n", c=2), ALU.mult).then_inc(l7_hidden, 1)

        def l7_dve(dve):
            for e in range(2):
                l7_gather_dve(dve, e + 1)
                l7_hidden_dve(dve, e)
                l7_spread_dve(dve, e, e, 0)
            l7_spread_dve(dve, 2, 0, 1)
            with dve.Fori(1, E7 // 2 - 1) as pair:
                for k in range(2):
                    l7_gather_dve(dve, 2 * pair + (k + 1))
                    l7_hidden_dve(dve, 2 * pair + k)
                    l7_spread_dve(dve, 2 * pair + (k + 1), 1 - k, pair + k)
            l7_gather_dve(dve, E7 - 1)
            l7_hidden_dve(dve, E7 - 2)
            l7_spread_dve(dve, E7 - 1, 1, E7 // 2 - 1)
            l7_hidden_dve(dve, E7 - 1)
            dve.wait_ge(l7_out, 1)
            nc.vector.tensor_copy(out7T, bank(7)).then_inc(l7_outT, 1)
            dve.wait_ge(l7_turned, 1)
            for t in range(T):
                nc.vector.tensor_tensor(x[:, t, :], x[:, t, :], quarters(4)[:, t, :], ALU.add).then_inc(x_updated, 1)

        x_dram = i["x"].rearrange("b (t p) d -> p (b t) d", p=P)
        out_dram = out.rearrange("b (t p) d -> p (b t) d", p=P)
        ctx_dram = i["ctx_768"].rearrange("b (t p) c -> p (b t) c", p=P)

        def row(v, n):
            return v.unsqueeze(0).broadcast_to([n, v.shape[0]])

        block = ctx.enter_context(nc.Block())

        @block.sync
        def _(sp):
            sp.dma_start(x[:], x_dram).then_inc(x_loaded, 16)
            sp.dma_start(ctx_rows[:], ctx_dram).then_inc(ctx_loaded, 16)
            sp.dma_start(wq[:], i["L0_xattn_Wq"]).then_inc(l0_qk_loaded, 16)
            sp.dma_start(wk[:], i["L0_xattn_Wk"]).then_inc(l0_qk_loaded, 16)
            sp.dma_start(wv[:], i["L0_xattn_Wv"]).then_inc(l0_loaded, 16)
            sp.dma_start(wout[:], i["L0_xattn_Wout"].rearrange("(h p) d -> p h d", p=P)).then_inc(l0_loaded, 16)
            sp.dma_start(bout[:], row(i["L0_xattn_bout"], P)).then_inc(l0_loaded, 16)
            sp.dma_start(we[:], i["L0_ffn_We"].rearrange("e o i -> o e i")).then_inc(early_loaded, 16)
            sp.dma_start(wg1[:], i["L0_ffn_Wg"]).then_inc(early_loaded, 16)
            sp.dma_start(bg1[:], row(i["L0_ffn_bg"], P)).then_inc(early_loaded, 16)
            sp.dma_start(be1[:], i["L0_ffn_be"]).then_inc(early_loaded, 16)
            sp.dma_start(wq2[:], i["L1_xattn_Wq"]).then_inc(early_loaded, 16)
            sp.dma_start(wk2[:], i["L1_xattn_Wk"]).then_inc(early_loaded, 16)
            sp.dma_start(wv2[:], i["L1_xattn_Wv"]).then_inc(early_loaded, 16)
            sp.dma_start(bq2[:], i["L1_xattn_bq"].unsqueeze(1)).then_inc(early_loaded, 16)
            sp.dma_start(bk2[:], i["L1_xattn_bk"].unsqueeze(1)).then_inc(early_loaded, 16)
            sp.dma_start(bv2[:], row(i["L1_xattn_bv"], P)).then_inc(early_loaded, 16)
            sp.dma_start(b1[:], i["L1_ffn_b1"]).then_inc(early_loaded, 16)
            sp.dma_start(wg3[:], i["L1_ffn_Wg"]).then_inc(early_loaded, 16)
            sp.dma_start(wo3[:], i["L1_ffn_Wo"]).then_inc(early_loaded, 16)
            sp.dma_start(bo3[:], row(i["L1_ffn_bo"], P)).then_inc(early_loaded, 16)
            sp.dma_start(w1[:], i["L1_ffn_W1"].rearrange("e (c p) d -> p e c d", p=P)).then_inc(early_loaded, 16)
            sp.dma_start(wd4[:], i["L2_xattn_W_d2v"]).then_inc(l4_loaded, 16)
            sp.dma_start(wi4[:], i["L2_xattn_W_img"]).then_inc(l4_loaded, 16)
            sp.dma_start(wt4[:], i["L2_xattn_W_txt"]).then_inc(l4_loaded, 16)
            sp.dma_start(wf14[:], i["L2_xattn_W_f1"].rearrange("(c p) i -> p c i", p=P)).then_inc(l4_loaded, 16)
            sp.dma_start(wf24[:], i["L2_xattn_W_f2"]).then_inc(l4_loaded, 16)
            for l in range(2):
                wa, ba = i[f"L2_xattn_W_att{l}"], i[f"L2_xattn_b_att{l}"]
                sp.dma_start(wa4[:, l, :], wa).then_inc(l4_loaded, 16)
                sp.dma_start(ba4_rows[:, l, :], row(ba, P)).then_inc(l4_loaded, 16)
                for copy in range(2):
                    sp.dma_start(ba4[64 * copy:64 * (copy + 1), l:l + 1], ba.unsqueeze(1)).then_inc(l4_ba, 16)
            sp.dma_start(bd4[:], i["L2_xattn_b_d2v"].unsqueeze(1)).then_inc(l4_loaded, 16)
            sp.dma_start(bi4[:], i["L2_xattn_b_img"].unsqueeze(1)).then_inc(l4_loaded, 16)
            sp.dma_start(bt4[:], i["L2_xattn_b_txt"].unsqueeze(1)).then_inc(l4_loaded, 16)
            for c in range(4):
                sp.dma_start(bf14[:, c:c + 1], i["L2_xattn_b_f1"][c * P:(c + 1) * P].unsqueeze(1)).then_inc(l4_loaded, 16)
            sp.dma_start(bf24[:], row(i["L2_xattn_b_f2"], P)).then_inc(l4_loaded, 16)
            sp.wait_ge(l3_b1_parts, 1)
            for k, part in enumerate((b1_hi, b1_mid, b1_lo)):
                sp.dma_start(b1_rows[k:k + 1, :, :], part[:]).then_inc(l3_b1_rows, 16)
            sp.wait_ge(x_updated, 2 * T)
            for k, name in enumerate(("q", "k", "v")):
                sp.dma_start(proj5[:, :, k * D:(k + 1) * D], i[f"L2_ffn_{name}_proj"].rearrange("e c h -> c e h")).then_inc(late_loaded, 16)
            sp.dma_start(oproj5[:], i["L2_ffn_o_proj"].rearrange("e h c -> h e c")).then_inc(late_loaded, 16)
            sp.dma_start(sim5[:], i["L2_ffn_sim_matrix"]).then_inc(late_loaded, 16)
            sp.dma_start(gates5[:], row(i["L2_ffn_gates"], P)).then_inc(late_loaded, 16)
            sp.dma_start(wq6[:], i["L3_xattn_Wq"]).then_inc(late_loaded, 16)
            sp.dma_start(wkv6[:], i["L3_xattn_Wkv"].rearrange("(k p) c -> p k c", p=P)).then_inc(late_loaded, 16)
            sp.dma_start(wo6[:], i["L3_xattn_Wo"]).then_inc(late_loaded, 16)
            with nc.allow_non_contiguous_dma(reason="128 elements, in the features' new order"):
                sp.dma_start(bq6[:], i["L3_xattn_bq"].rearrange("(h j) -> j h", j=J6)).then_inc(late_loaded, 16)
                sp.dma_start(bk6[:], i["L3_xattn_bkv"].rearrange("(h s j) -> s j h", s=2, j=J6)[0]).then_inc(late_loaded, 16)
            sp.dma_start(bkv6[:], row(i["L3_xattn_bkv"], P)).then_inc(late_loaded, 16)
            sp.dma_start(bo6[:], row(i["L3_xattn_bo"], P)).then_inc(late_loaded, 16)
            sp.dma_start(wr7[:], i["L3_ffn_Wr"]).then_inc(late_loaded, 16)
            l6_k_stack_sp(sp)
            l6_sp(sp)
            l7_first_loads_sp(sp)
            l6_o_sp(sp)
            l7_loads_sp(sp)
            sp.wait_ge(x_updated, T * 8)
            sp.dma_start(out_dram, x[:]).then_inc(stored, 16)
            sp.wait_ge(stored, 16)

        @block.gpsimd
        def _(pool):
            link = Chain(pool, pool_chain)
            const_pool(pool)
            ln_pool(pool, link, 0)
            rev_pool()
            l4_const_pool()
            l5_const_pool(pool, link)
            l7_const_pool(pool, link)
            l0_pool(pool)
            for k in range(3):
                whole_max_pool(pool, k)
            for n in range(1, 8):
                ln_pool(pool, link, n)
                if n == 1:
                    l1_pool(pool)
                if n == 5:
                    l5_xnorm_pool(pool)
                    l6_prepare_pool(pool, link)
                if n == 6:
                    l6_pool(pool)
                if n == 7:
                    l7_pool(pool)
                if n == 4:
                    for k in range(3, 6):
                        whole_max_pool(pool, k)
                        if k == 3:
                            l5_norm_pool(pool)
                    l4_ints_pool(pool, link)

        @block.tensor
        def _(pe):
            fold_pe(pe)
            ln_pe(pe, 0)
            l0_pe(pe)
            l1_prepare_pe(pe)
            ln_pe(pe, 1)
            l1_pe(pe)
            l2_value_pe(pe)
            ln_pe(pe, 2)
            l2_pe(pe)
            l3_prepare_pe(pe)
            ln_pe(pe, 3)
            l3_pe(pe)
            l4_ctx_pe(pe)
            ln_pe(pe, 4)
            l4_pe(pe)
            ln_pe(pe, 5)
            l5_router_pe(pe)
            l5_pe(pe)
            ln_pe(pe, 6)
            l6_pe(pe)
            l7_numbers_pe(pe)
            ln_pe(pe, 7)
            l7_router_pe(pe)
            l7_pe(pe)

        @block.scalar
        def _(act):
            fold_copy(act, act_copy, 1, fold_act)
            ln_act(act, 0)
            l0_act(act)
            l1_prepare_act(act)
            ln_act(act, 1)
            gate_act(act, 1, E1)
            l1_act(act)
            l2_prepare_act(act)
            ln_act(act, 2)
            l2_act(act)
            l3_prepare_act(act)
            ln_act(act, 3)
            gate_act(act, 2, E3)
            l3_act(act)
            l4_ctx_act(act)
            ln_act(act, 4)
            l4_act(act)
            ln_act(act, 5)
            l6_prepare_act(act)
            gate_act(act, 3, E5)
            l5_act(act)
            ln_act(act, 6)
            l6_act(act)
            ln_act(act, 7)
            gate_act(act, 4, E7)
            l7_act(act)

        @block.vector
        def _(dve):
            link = Chain(dve, dve_chain)
            ln_dve(dve, link, 0)
            fold_copy(dve, nc.vector.tensor_copy, 0, fold_dve)
            l0_dve(dve, link)
            ln_dve(dve, link, 1)
            l3_parts_dve(dve, link)
            l1_dve(dve, link)
            ln_dve(dve, link, 2)
            l2_prepare_dve(dve)
            l2_dve(dve, link)
            ln_dve(dve, link, 3)
            l3_dve(dve, link)
            ln_dve(dve, link, 4)
            l4_dve(dve, link)
            ln_dve(dve, link, 5)
            l5_router_dve(dve, link)
            l5_dve(dve, link)
            ln_dve(dve, link, 6)
            l6_dve(dve, link)
            ln_dve(dve, link, 7)
            l7_numbers_dve(dve, link)
            l7_router_dve(dve, link)
            l7_dve(dve)


def kernel(**inputs):
    import numpy as np
    import concourse.bacc as bacc
    from concourse.bass_utils import run_bass_kernel_spmd

    nc = bacc.Bacc("TRN2", target_bir_lowering=False, num_devices=1)
    arrays, given = {}, {}
    for name, value in inputs.items():
        a = np.ascontiguousarray(value)
        arrays[f"in_{name}"] = a
        given[name] = nc.dram_tensor(f"in_{name}", a.shape, mybir.dt.from_np(a.dtype), kind="ExternalInput").ap()
    out = nc.dram_tensor("out_x", given["x"].shape, F32, kind="ExternalOutput").ap()
    build(nc, given, out)
    return run_bass_kernel_spmd(nc, [arrays], core_ids=[0]).results[0]["out_x"]
```
